# Optimizing a Trainium2 kernel written in Bass

```python
import numpy as np
import jax
import jax.numpy as jnp

def _softmax(x, axis=-1):
    return jax.nn.softmax(x, axis=axis)

def _gelu(x):
    return jax.nn.gelu(x, approximate=True)

def _silu(x):
    return jax.nn.silu(x)

def _sigmoid(x):
    return jax.nn.sigmoid(x)

def _layernorm(x, axis=-1, eps=1e-05):
    m = jnp.mean(x, axis=axis, keepdims=True)
    v = jnp.var(x, axis=axis, keepdims=True)
    return (x - m) / jnp.sqrt(v + eps)

def _scatter_add(tgt, idx, src, axis=0):
    return tgt.at[idx].add(src)

def _segment_sum(src, seg, n):
    return jax.ops.segment_sum(src, seg, n)
kernel_name = 'mk_hybrid_d1_jaxref_r8_f259c6'

def setup_inputs(seed: int=0):
    np.random.seed(seed)
    _w = jnp.asarray

    def _L0_attn_a_setup():
        import jax, jax.numpy as jnp
        import numpy as np
        HEAD_DIM = 128
        HIDDEN_DIM = 128
        B, S = (4, 512)
        key = jax.random.key(seed)
        k_x, k_q, k_k, k_v, k_o = jax.random.split(key, 5)
        scale = 1.0 / np.sqrt(HIDDEN_DIM)
        return {'x': jax.random.normal(k_x, (B, S, HIDDEN_DIM), dtype=jnp.float32), 'head_dim_mask': jnp.ones((HEAD_DIM,), dtype=jnp.int32), 'w_q': jax.random.normal(k_q, (HIDDEN_DIM, HEAD_DIM), dtype=jnp.float32) * scale, 'w_k': jax.random.normal(k_k, (HIDDEN_DIM, HEAD_DIM), dtype=jnp.float32) * scale, 'w_v': jax.random.normal(k_v, (HIDDEN_DIM, HEAD_DIM), dtype=jnp.float32) * scale, 'w_o': jax.random.normal(k_o, (HEAD_DIM, HIDDEN_DIM), dtype=jnp.float32) * (1.0 / np.sqrt(HEAD_DIM))}
    _L0_attn_a_in = _L0_attn_a_setup()

    def _L0_attn_b_setup():
        import jax, jax.numpy as jnp
        import numpy as np
        import math
        B, N, D, H = (1, 512, 128, 16)
        HS = D // H
        NEG_INF = -10000.0
        key = jax.random.key(seed)
        k1, k2, k3, k4, k5 = jax.random.split(key, 5)
        return {'encodings': jax.random.normal(k1, (B, N, D), dtype=jnp.float32), 'attn_W': jax.random.normal(k2, (D, 3 * D), dtype=jnp.float32) * 0.02, 'attn_b': jax.random.normal(k3, (3 * D,), dtype=jnp.float32) * 0.02, 'out_W': jax.random.normal(k4, (D, D), dtype=jnp.float32) * 0.02, 'out_b': jax.random.normal(k5, (D,), dtype=jnp.float32) * 0.02}
    _L0_attn_b_in = _L0_attn_b_setup()

    def _L0_ffn_setup():
        import math
        import jax, jax.numpy as jnp
        import numpy as np
        H = 128
        F = 512
        E = 8
        TOP_K = 2
        CAP_FACTOR = 1.25
        MIN_CAP = 4
        SHARED_SCALE = 0.1

        def _top2_gating(logits, capacity):
            N, nE = logits.shape
            gates = jax.nn.softmax(logits, axis=-1)
            idx1 = jnp.argmax(gates, axis=-1)
            mask1 = jax.nn.one_hot(idx1, nE, dtype=gates.dtype)
            idx2 = jnp.argmax(gates * (1.0 - mask1), axis=-1)
            mask2 = jax.nn.one_hot(idx2, nE, dtype=gates.dtype)
            pos1 = jnp.cumsum(mask1, axis=0) - mask1
            mask1 = mask1 * (pos1 < capacity)
            pos2 = jnp.cumsum(mask2, axis=0) - mask2 + jnp.sum(mask1, axis=0, keepdims=True)
            mask2 = mask2 * (pos2 < capacity)
            g1 = jnp.sum(gates * mask1, axis=-1)
            g2 = jnp.sum(gates * mask2, axis=-1)
            denom = jnp.maximum(g1 + g2, jnp.finfo(gates.dtype).eps)
            g1, g2 = (g1 / denom, g2 / denom)
            loc1 = jnp.sum(pos1 * mask1, axis=-1).astype(jnp.int32)
            loc2 = jnp.sum(pos2 * mask2, axis=-1).astype(jnp.int32)
            oh1 = jax.nn.one_hot(loc1, capacity, dtype=gates.dtype)
            oh2 = jax.nn.one_hot(loc2, capacity, dtype=gates.dtype)
            combine = (g1[:, None] * mask1)[:, :, None] * oh1[:, None, :] + (g2[:, None] * mask2)[:, :, None] * oh2[:, None, :]
            dispatch = (combine > 0).astype(gates.dtype)
            return (combine, dispatch)
        key = jax.random.key(seed)
        ks = jax.random.split(key, 10)
        s_h = 1.0 / math.sqrt(H)
        s_f = 1.0 / math.sqrt(F)
        return {'hidden_states': jax.random.normal(ks[0], (2, 256, H), jnp.float32), 'router_w': jax.random.uniform(ks[1], (H, E), jnp.float32, -s_h, s_h), 'w1': jax.random.uniform(ks[2], (E, H, F), jnp.float32, -s_h, s_h), 'b1': jax.random.uniform(ks[3], (E, F), jnp.float32, -s_h, s_h), 'w2': jax.random.uniform(ks[4], (E, F, H), jnp.float32, -s_f, s_f), 'b2': jax.random.uniform(ks[5], (E, H), jnp.float32, -s_f, s_f), 'sw1': jax.random.uniform(ks[6], (H, F), jnp.float32, -s_h, s_h), 'sb1': jax.random.uniform(ks[7], (F,), jnp.float32, -s_h, s_h), 'sw2': jax.random.uniform(ks[8], (F, H), jnp.float32, -s_f, s_f), 'sb2': jax.random.uniform(ks[9], (H,), jnp.float32, -s_f, s_f)}
    _L0_ffn_in = _L0_ffn_setup()
    _d = {'L0_attn_a_x': _L0_attn_a_in['x'], 'L0_attn_a_head_dim_mask': _L0_attn_a_in['head_dim_mask'], 'L0_attn_a_w_q': _L0_attn_a_in['w_q'], 'L0_attn_a_w_k': _L0_attn_a_in['w_k'], 'L0_attn_a_w_v': _L0_attn_a_in['w_v'], 'L0_attn_a_w_o': _L0_attn_a_in['w_o'], 'L0_attn_b_attn_W': _L0_attn_b_in['attn_W'], 'L0_attn_b_attn_b': _L0_attn_b_in['attn_b'], 'L0_attn_b_out_W': _L0_attn_b_in['out_W'], 'L0_attn_b_out_b': _L0_attn_b_in['out_b'], 'L0_ffn_router_w': _L0_ffn_in['router_w'], 'L0_ffn_w1': _L0_ffn_in['w1'], 'L0_ffn_b1': _L0_ffn_in['b1'], 'L0_ffn_w2': _L0_ffn_in['w2'], 'L0_ffn_b2': _L0_ffn_in['b2'], 'L0_ffn_sw1': _L0_ffn_in['sw1'], 'L0_ffn_sb1': _L0_ffn_in['sb1'], 'L0_ffn_sw2': _L0_ffn_in['sw2'], 'L0_ffn_sb2': _L0_ffn_in['sb2']}
    _x0 = _d['L0_attn_a_x']
    _d['L0_attn_a_x'] = jax.random.normal(jax.random.fold_in(jax.random.key(seed), 1), (16, 256, 128), dtype=_x0.dtype)
    del _x0
    return _d

def reference(L0_attn_a_x, L0_attn_a_head_dim_mask, L0_attn_a_w_q, L0_attn_a_w_k, L0_attn_a_w_v, L0_attn_a_w_o, L0_attn_b_attn_W, L0_attn_b_attn_b, L0_attn_b_out_W, L0_attn_b_out_b, L0_ffn_router_w, L0_ffn_w1, L0_ffn_b1, L0_ffn_w2, L0_ffn_b2, L0_ffn_sw1, L0_ffn_sb1, L0_ffn_sw2, L0_ffn_sb2):

    def _L0_attn_a_ref(x, head_dim_mask, w_q, w_k, w_v, w_o):
        import jax, jax.numpy as jnp
        import numpy as np
        HEAD_DIM = 128
        HIDDEN_DIM = 128
        B, S = (4, 512)
        q = jnp.einsum('bsh,hd->bsd', x, w_q)
        k = jnp.einsum('bsh,hd->bsd', x, w_k)
        v = jnp.einsum('bsh,hd->bsd', x, w_v)
        scale = 1.0 / jnp.sqrt(jnp.asarray(HEAD_DIM, dtype=x.dtype))
        scores = jnp.einsum('bqd,bkd->bqk', q, k) * scale
        A = jax.nn.softmax(scores, axis=-1)
        h = jnp.einsum('bqk,bkd->bqd', A, v)
        h = h * head_dim_mask.astype(h.dtype)
        y = jnp.einsum('bsd,dh->bsh', h, w_o)
        return y

    def _L0_attn_b_ref(encodings, attn_W, attn_b, out_W, out_b):
        import jax, jax.numpy as jnp
        import numpy as np
        import math
        B, N, D, H = (1, 512, 128, 16)
        HS = D // H
        NEG_INF = -10000.0
        b, n, d = encodings.shape
        qkv = encodings @ attn_W + attn_b
        qkv = qkv.reshape(b, n, H, 3 * HS).transpose(0, 2, 1, 3)
        q, k, v = jnp.split(qkv, 3, axis=-1)
        scores = jnp.einsum('bhki,bhqi->bhkq', k, q) / math.sqrt(HS)
        mask = jnp.arange(n)[:, None] <= jnp.arange(n)[None, :]
        scores = jnp.where(mask, scores, jnp.float32(NEG_INF))
        prob = jax.nn.softmax(scores, axis=2)
        combined = jnp.einsum('bhkq,bhkl->bhql', prob, v)
        out = combined.transpose(0, 2, 1, 3).reshape(b, n, d)
        return out @ out_W + out_b

    def _L0_ffn_ref(hidden_states, router_w, w1, b1, w2, b2, sw1, sb1, sw2, sb2):
        import math
        import jax, jax.numpy as jnp
        import numpy as np
        H = 128
        F = 512
        E = 8
        TOP_K = 2
        CAP_FACTOR = 1.25
        MIN_CAP = 4
        SHARED_SCALE = 0.1

        def _top2_gating(logits, capacity):
            N, nE = logits.shape
            gates = jax.nn.softmax(logits, axis=-1)
            idx1 = jnp.argmax(gates, axis=-1)
            mask1 = jax.nn.one_hot(idx1, nE, dtype=gates.dtype)
            idx2 = jnp.argmax(gates * (1.0 - mask1), axis=-1)
            mask2 = jax.nn.one_hot(idx2, nE, dtype=gates.dtype)
            pos1 = jnp.cumsum(mask1, axis=0) - mask1
            mask1 = mask1 * (pos1 < capacity)
            pos2 = jnp.cumsum(mask2, axis=0) - mask2 + jnp.sum(mask1, axis=0, keepdims=True)
            mask2 = mask2 * (pos2 < capacity)
            g1 = jnp.sum(gates * mask1, axis=-1)
            g2 = jnp.sum(gates * mask2, axis=-1)
            denom = jnp.maximum(g1 + g2, jnp.finfo(gates.dtype).eps)
            g1, g2 = (g1 / denom, g2 / denom)
            loc1 = jnp.sum(pos1 * mask1, axis=-1).astype(jnp.int32)
            loc2 = jnp.sum(pos2 * mask2, axis=-1).astype(jnp.int32)
            oh1 = jax.nn.one_hot(loc1, capacity, dtype=gates.dtype)
            oh2 = jax.nn.one_hot(loc2, capacity, dtype=gates.dtype)
            combine = (g1[:, None] * mask1)[:, :, None] * oh1[:, None, :] + (g2[:, None] * mask2)[:, :, None] * oh2[:, None, :]
            dispatch = (combine > 0).astype(gates.dtype)
            return (combine, dispatch)
        B, S, h = hidden_states.shape
        x = hidden_states.reshape(-1, h)
        N = x.shape[0]
        capacity = min(max(MIN_CAP, math.ceil(TOP_K * CAP_FACTOR * N / E)), N)
        logits = x @ router_w
        combine, dispatch = _top2_gating(logits, capacity)
        expert_in = jnp.einsum('nec,nh->ech', dispatch, x)
        hmid = jax.nn.silu(jnp.einsum('ech,ehf->ecf', expert_in, w1) + b1[:, None, :])
        expert_out = jnp.einsum('ecf,efh->ech', hmid, w2) + b2[:, None, :]
        y = jnp.einsum('nec,ech->nh', combine, expert_out)
        shared = jax.nn.silu(x @ sw1 + sb1) @ sw2 + sb2
        out = y + SHARED_SCALE * shared
        return out.reshape(B, S, h)
    x = L0_attn_a_x
    x = x + _L0_attn_a_ref(_layernorm(x, axis=-1), L0_attn_a_head_dim_mask, L0_attn_a_w_q, L0_attn_a_w_k, L0_attn_a_w_v, L0_attn_a_w_o)
    x = x + _L0_ffn_ref(_layernorm(x, axis=-1), L0_ffn_router_w, L0_ffn_w1, L0_ffn_b1, L0_ffn_w2, L0_ffn_b2, L0_ffn_sw1, L0_ffn_sb1, L0_ffn_sw2, L0_ffn_sb2)
    x = x + _L0_attn_b_ref(_layernorm(x, axis=-1), L0_attn_b_attn_W, L0_attn_b_attn_b, L0_attn_b_out_W, L0_attn_b_out_b)
    x = x + _L0_ffn_ref(_layernorm(x, axis=-1), L0_ffn_router_w, L0_ffn_w1, L0_ffn_b1, L0_ffn_w2, L0_ffn_b2, L0_ffn_sw1, L0_ffn_sb1, L0_ffn_sw2, L0_ffn_sb2)
    return x

_drawn_inputs = setup_inputs


def setup_inputs(seed=0):
    import zlib

    import numpy as np

    out = dict(_drawn_inputs(seed))
    spreads = {}
    factors = {'L0_attn_b_attn_W': 4.796,
     'L0_attn_b_attn_b': 8.0,
     'L0_attn_b_out_W': 4.335,
     'L0_ffn_sb1': 8.0,
     'L0_ffn_sb2': 7.345}
    for name, (base, spread) in spreads.items():
        noise = np.random.default_rng([zlib.crc32(name.encode()), seed]).standard_normal(out[name].shape)
        drawn = base * np.exp(spread * noise) if base else spread * noise
        out[name] = jnp.asarray(drawn.astype(out[name].dtype))
    for name, factor in factors.items():
        out[name] = (out[name] * factor).astype(out[name].dtype)
    return out
```

```python
import math
from contextlib import ExitStack

import concourse.bass as bass
from concourse import mybir

ALU = mybir.AluOpType
ACT = mybir.ActivationFunctionType
AX = mybir.AxisListType
F32 = mybir.dt.float32
BF16 = mybir.dt.bfloat16
F32R = mybir.dt.float32r
I32 = mybir.dt.int32
U32 = mybir.dt.uint32

P = 128
SEQS, SEQ, D = 16, 256, 128
T = SEQS * SEQ
NT = T // P
PAIRS = SEQS // 2
E, F = 8, 512
FT = F // P
CAP = min(max(4, math.ceil(2 * 1.25 * T / E)), T)
ST = CAP // P
CH = 2
CHUNKS = ST // CH
SLOT_TILES = E * ST
RING = 5
EPS = 1e-5
TINY = 1.1920928955078125e-07
MASKED = -1e30
SHARED_SCALE = 0.1
HEADS, HD = 16, 8
GRP = HEADS // 4
LAYERS = 2


def need(eng, sem, value):
    if not isinstance(value, int) or value > 0:
        eng.wait_ge(sem, value)


def alone(eng, sem, value, set_already):
    if not isinstance(value, int):
        value = eng.to_reg(value)
        eng.wait_ge(set_already, 1)
    need(eng, sem, value)


def valid(pair):
    return not isinstance(pair, int) or 0 <= pair < PAIRS


def shifted_group(i, h, g, by):
    q = GRP * h + g + by
    return i + q // (2 * GRP), q // GRP % 2, q % GRP


class Signals:
    pass


def build(nc, x_in, hd_mask, w_q, w_k, w_v, w_o, attn_W, attn_b, out_W, out_b, router_w,
          w1, b1, w2, b2, sw1, sb1, sw2, sb2, out):
    with ExitStack() as ctx:
        def sb(name, shape, dt=F32):
            return ctx.enter_context(nc.sbuf_tensor(name, shape, dt))

        def sem(name):
            return ctx.enter_context(nc.semaphore(name))

        xn_rows = nc.dram_tensor("xn_rows", [T, D], F32).ap()
        y_rows = nc.dram_tensor("y_rows", [2 * T, D], F32).ap()

        qk_rows = nc.dram_tensor("qk_rows", [2, P, 2, 2, SEQ], F32).ap()

        bank = [ctx.enter_context(nc.psum_tensor(f"bank{k}", [P, 512], F32)) for k in range(8)]

        ident = sb("ident", [P, P])
        ident_bf = sb("ident_bf", [P, P], BF16)
        before = sb("before", [P, P], BF16)
        ones_bf = sb("ones_bf", [P, P], BF16)
        iota_lo = sb("iota_lo", [P, P], BF16)
        iota_hi = sb("iota_hi", [P, SLOT_TILES], BF16)
        part1 = sb("part1", [P, 1])
        rev = sb("rev", [P, E])
        slot_base = sb("slot_base", [P, E, NT])
        tile_code = sb("tile_code", [P, 2 * NT], BF16)
        carry = sb("carry", [P, 2 * E * NT])
        neg_half = sb("neg_half", [P, 4])

        wq = sb("wq", [P, D]); wk = sb("wk", [P, D]); wv = sb("wv", [P, D]); wo = sb("wo", [P, D])
        mask_i = sb("mask_i", [P, 1], I32); mask_f = sb("mask_f", [P, 1])
        wT = sb("wT", [P, 3, D])
        wo_m = sb("wo_m", [P, D])
        m_qk = sb("m_qk", [P, D])
        m_vo = sb("m_vo", [P, D])
        router = sb("router", [P, E])
        sw1_s = sb("sw1_s", [P, F]); sw2_s = sb("sw2_s", [P, FT, D])
        bias_rows = sb("bias_rows", [38, P]); bias_T = sb("bias_T", [P, 38])
        b2_b = sb("b2_b", [P, E, D]); sb2_b = sb("sb2_b", [P, D])

        x = sb("x", [P, NT, D])
        xnT_all = sb("xnT_all", [P, T])
        logits = sb("logits", [P, NT, E])
        gate = sb("gate", [P, 2, NT])

        st = sb("st", [P, 4, 6]); mv = sb("mv", [P, 4, 2]); ve = sb("ve", [P, 4]); rstd = sb("rstd", [P, 4])
        st2 = sb("st2", [P, 4, 6]); mv2 = sb("mv2", [P, 4, 2]); ve2 = sb("ve2", [P, 4]); rstd2 = sb("rstd2", [P, 4])
        xn = sb("xn", [P, 4, D])
        xn2 = sb("xn2", [P, 4, D])
        logT = sb("logT", [E, 512])

        xnT = sb("xnT", [P, 2, SEQ]); v_s = sb("v_s", [P, 2, 2, D])
        negmax = sb("negmax", [P, 2, 2]); psums = sb("psums", [P, 2, 2]); rsum = sb("rsum", [P, 2, 2])

        r1 = sb("r1", [P, NT]); r2 = sb("r2", [P, NT])
        G = sb("G", [P, NT, E])
        MK = sb("MK", [P, 2, E, NT], BF16)
        keep1 = sb("keep1", [P, E])
        fill = sb("fill", [P, 2, NT]); slot = sb("slot", [P, 2, NT]); slot_i = sb("slot_i", [P, 2, NT], I32)
        hi_i = sb("hi_i", [P, 2, NT], I32); lo_i = sb("lo_i", [P, 2, NT], I32)
        hi_f = sb("hi_f", [P, 2, NT]); hi_b = sb("hi_b", [P, 2 * NT], BF16); lo_b = sb("lo_b", [P, 2 * NT], BF16)
        den = sb("den", [P, NT])
        with ExitStack() as shared_place:
            def sb_r(name, shape, dt=F32):
                return shared_place.enter_context(nc.sbuf_tensor(name, shape, dt))

            shared = sb_r("shared", [P, NT, D])
            G1 = sb_r("G1", [P, NT, E]); t1 = sb_r("t1", [P, NT, E]); m1 = sb_r("m1", [P, NT, E])
            INC = sb_r("INC", [P, 2, E, NT]); POS = sb_r("POS", [P, 2, E, NT]); KM = sb_r("KM", [P, 2, E, NT])
            GK = sb_r("GK", [P, 2, E, NT])
            hsh = sb_r("hsh", [P, 2, FT, 512])
            OH = sb_r("OH", [P, 2 * NT, SLOT_TILES], BF16)
            OL = sb_r("OL", [P, 2 * NT, P], BF16)
            RH = sb_r("RH", [P, 2 * NT, 2, SLOT_TILES], BF16)

        zero_rows = shared

        bdk = sb("bdk", [P, 2, GRP, 4, SEQ], F32R)
        pt = sb("pt", [P, 2, 3, 512])
        qc = sb("qc", [P, 2, GRP, SEQ], F32R)
        qk32 = sb("qk32", [P, 2, SEQ])
        qks = sb("qks", [P, 2, 2, 2, SEQ], F32R)
        oT = sb("oT", [P, GRP, SEQ])
        on = sb("on", [P, 2, HEADS, HD]); onT = sb("onT", [P, SEQ]); osum = sb("osum", [P, 2, HEADS])
        probs = sb("probs", [P, 2, 2, SEQ]); pT = sb("pT", [P, 2, SEQ]); gT = sb("gT", [P, SEQ])
        xg = sb("xg", [P, RING, CH, D])
        yo = sb("yo", [P, RING, CH, D])
        hT = sb("hT", [P, 2, FT, CH * P])
        row_f = sb("row_f", [P, SLOT_TILES]); row_e = sb("row_e", [P, SLOT_TILES])
        tok_idx = sb("tok_idx", [P, SLOT_TILES], U32); row_idx = sb("row_idx", [P, SLOT_TILES], U32)

        w1_s = [sb(f"w1_s{k}", [P, F]) for k in range(2)]
        w2_s = [sb(f"w2_s{k}", [P, FT, D]) for k in range(2)]
        tok_cur = sb("tok_cur", [P, 2, ST], U32); row_cur = sb("row_cur", [P, 2, ST], U32)
        b1_cur = sb("b1_cur", [P, 2, FT])
        xgT = sb("xgT", [P, 2, CH * P])
        yab = sb("yab", [P, 2, 4, D])

        kc = sb("kc", [P, 2, GRP, SEQ], F32R)
        v_ext = sb("v_ext", [P, 2, 2, HEADS, 32])
        negp = sb("negp", [P, 2, 2, P])
        cmask = sb("cmask", [P, P], BF16)
        head_p = sb("head_p", [P, 4, 4]); head_m = sb("head_m", [P, 4])
        qkv_w = sb("qkv_w", [P, HEADS, 3, HD]); w3 = sb("w3", [P, 3, HEADS, HD]); ow = sb("ow", [P, D])
        bv_b = sb("bv_b", [P, HEADS, HD]); ob_b = sb("ob_b", [P, D]); bq_s = sb("bq_s", [P, 1])


        S = Signals()
        S.const_pool = sem("const_pool")
        S.const_dve = sem("const_dve")
        S.x_head = sem("x_head")
        S.x_tail = sem("x_tail")
        S.w_in = sem("w_in")
        S.w_moe_in = sem("w_moe_in")
        S.zero_set = sem("zero_set")
        S.y_zeroed = sem("y_zeroed")
        S.const_chain = sem("const_chain")
        S.bias_tr = sem("bias_tr")
        S.bias_set = sem("bias_set")
        S.w_tr = sem("w_tr")
        S.w_trs = sem("w_trs")
        S.wfold_mm = sem("wfold_mm")
        S.wfold = sem("wfold")
        S.ln_stats = sem("ln_stats")
        S.ln_mv = sem("ln_mv")
        S.ln_ve = sem("ln_ve")
        S.ln_rstd = sem("ln_rstd")
        S.xn_ready = sem("xn_ready")
        S.xn_tr = sem("xn_tr")
        S.xnT_ready = sem("xnT_ready")
        S.g_done = sem("g_done")
        S.gT_ready = sem("gT_ready")
        S.v_done = sem("v_done")
        S.v_ready = sem("v_ready")
        S.scores_done = sem("scores_done")
        S.max_ready = sem("max_ready")
        S.probs_ready = sem("probs_ready")
        S.probs_tr = sem("probs_tr")
        S.pT_ready = sem("pT_ready")
        S.y_done = sem("y_done")
        S.rsum_ready = sem("rsum_ready")
        S.attn_added = sem("attn_added")
        S.ln2_stats = sem("ln2_stats")
        S.ln2_mv = sem("ln2_mv")
        S.ln2_ve = sem("ln2_ve")
        S.ln2_rstd = sem("ln2_rstd")
        S.xn2_ready = sem("xn2_ready")
        S.xn2_tr = sem("xn2_tr")
        S.xn2T_ready = sem("xn2T_ready")
        S.xn2_stored = sem("xn2_stored")
        S.logT_done = sem("logT_done")
        S.logT_ready = sem("logT_ready")
        S.log_done = sem("log_done")
        S.log_ready = sem("log_ready")
        S.route = sem("route")
        S.shifted = sem("shifted")
        S.exped = sem("exped")
        S.masks_ready = sem("masks_ready")
        S.count_done = sem("count_done")
        S.onehot_ready = sem("onehot_ready")
        S.index_done = sem("index_done")
        S.index_ready = sem("index_ready")
        S.sh1_done = sem("sh1_done")
        S.sh1_ready = sem("sh1_ready")
        S.sh2_done = sem("sh2_done")
        S.sh2_ready = sem("sh2_ready")
        S.shared_added = sem("shared_added")
        S.xg_tr = sem("xg_tr")
        S.xgT_ready = sem("xgT_ready")
        S.h_done = sem("h_done")
        S.h_ready = sem("h_ready")
        S.yo_done = sem("yo_done")
        S.yo_ready = sem("yo_ready")
        S.w1_in0 = sem("w1_in0")
        S.w1_in1 = sem("w1_in1")
        S.idx_cur = sem("idx_cur")
        S.b1_set = sem("b1_set")
        S.comb = sem("comb")
        S.y_in = sem("y_in")
        S.y_used = sem("y_used")
        S.stored = sem("stored")
        S.final_ready = sem("final_ready")
        S.wb_in = sem("wb_in")
        S.init_b = sem("init_b")
        S.tb_done = sem("tb_done")
        S.tb_ready = sem("tb_ready")
        S.qk_done = sem("qk_done")
        S.qk32_ready = sem("qk32_ready")
        S.vb_done = sem("vb_done")
        S.vb_ready = sem("vb_ready")
        S.hilo_hi = sem("hilo_hi")
        S.hilo_done = sem("hilo_done")
        S.qks_stored0 = sem("qks_stored0")
        S.qks_stored1 = sem("qks_stored1")
        S.kc_in0 = sem("kc_in0")
        S.kc_in1 = sem("kc_in1")
        S.qc_in0 = sem("qc_in0")
        S.qc_in1 = sem("qc_in1")
        S.bd_done = sem("bd_done")
        S.a_done = sem("a_done")
        S.amax_done = sem("amax_done")
        S.negT_done = sem("negT_done")
        S.neg_set = sem("neg_set")
        S.c_done = sem("c_done")
        S.exp_done = sem("exp_done")
        S.aff_done = sem("aff_done")
        S.pv_done = sem("pv_done")
        S.ot_ready = sem("ot_ready")
        S.otr_done = sem("otr_done")
        S.osum_ready = sem("osum_ready")
        S.on_ready = sem("on_ready")
        S.onT_done = sem("onT_done")
        S.onT_ready = sem("onT_ready")
        S.pr_done = sem("pr_done")
        S.xb_added = sem("xb_added")
        S.ob_added = sem("ob_added")
        S.v_set = sem("v_set")
        gat = [sem(f"gathered{k}") for k in range(RING)]
        sca = [sem(f"scattered{k}") for k in range(RING)]
        N_CONST_POOL = 17

        x_rows = x_in.rearrange("b (h p) d -> p (b h) d", p=P)
        out_rows = out.rearrange("b (h p) d -> p (b h) d", p=P)

        block = ctx.enter_context(nc.Block())

        @block.sync
        def _(sp):
            sp.dma_start(x[:, 0:4, :], x_rows[:, 0:4, :]).then_inc(S.x_head, 16)
            sp.dma_start(x[:, 4:NT, :], x_rows[:, 4:NT, :]).then_inc(S.x_tail, 16)
            sp.dma_start(sw1_s[:, :], sw1).then_inc(S.w_moe_in, 16)
            sp.dma_start(sw2_s[:, :, :], sw2.rearrange("(f p) d -> p f d", p=P)).then_inc(S.w_moe_in, 16)
            sp.dma_start(b2_b[:, :, :], b2.unsqueeze(0).broadcast_to([P, E, D])).then_inc(S.w_moe_in, 16)
            sp.dma_start(sb2_b[:, :], sb2.unsqueeze(0).broadcast_to([P, D])).then_inc(S.w_moe_in, 16)
            sp.dma_start(qkv_w[:, :, :, :].rearrange("p h c d -> p (h c d)"), attn_W).then_inc(S.wb_in, 16)
            sp.dma_start(ow[:, :], out_W).then_inc(S.wb_in, 16)
            sp.dma_start(ob_b[:, :], out_b.unsqueeze(0).broadcast_to([P, D])).then_inc(S.wb_in, 16)
            sp.dma_start(bv_b[:, :, :], attn_b.rearrange("(h c d) -> c h d", c=3, d=HD)[2:3].broadcast_to([P, HEADS, HD])
                         ).then_inc(S.wb_in, 16)

            def store_xn(l, i):
                alone(sp, S.xn2_ready, PAIRS * l + i + 1, S.x_head)
                sp.dma_start(xn_rows.rearrange("(t p) d -> p t d", p=P)[:, bass.ds(4 * i, 4), :],
                             xn2[:, :, :]).then_inc(S.xn2_stored, 16)

            def weights(l, i):
                for h, sm in enumerate((S.w1_in0, S.w1_in1)):
                    n = l * E * CHUNKS + (2 * i + h - 1) * CHUNKS
                    alone(sp, S.yo_done, n, S.x_head)
                    sp.dma_start(w1_s[h][:, :], w1[bass.ds(2 * i + h, 1), :, :].rearrange("a p f -> p (a f)")).then_inc(sm, 16)
                    sp.dma_start(w2_s[h][:, :, :], w2[bass.ds(2 * i + h, 1), :, :].rearrange("a (f p) d -> p (a f) d", p=P)).then_inc(sm, 16)

            def y_in(l, pair):
                alone(sp, S.y_used, PAIRS * l + pair, S.x_head)
                for c in range(2):
                    src = y_rows[c * T:(c + 1) * T, :].rearrange("(t p) d -> p t d", p=P)
                    sp.dma_start(yab[:, c, :, :], src[:, bass.ds(4 * pair, 4), :]).then_inc(S.y_in, 16)

            def restack(t, par):
                n = 2 * t + par
                rows_stored, k_in, q_in = ((S.qks_stored0, S.kc_in0, S.qc_in0), (S.qks_stored1, S.kc_in1, S.qc_in1))[par]
                alone(sp, S.hilo_done, n + 1, S.x_head)
                need(sp, k_in, 48 * t)
                need(sp, q_in, 48 * t)
                sp.dma_start(qk_rows[par], qks[:, par, :, :, :].bitcast(F32)).then_inc(rows_stored, 16)
                alone(sp, rows_stored, 16 * t + 16, S.x_head)
                need(sp, S.bd_done, GRP * (n - 1))
                rows = qk_rows[par].rearrange("(g r) a b t -> r g a b t", g=GRP)
                for part, half in enumerate((0, 1, 0)):
                    sp.dma_start(kc[32 * part:32 * part + 32, par, :, :].bitcast(F32), rows[:, :, half, 1, :]).then_inc(k_in, 16)
                need(sp, S.c_done, 3 * GRP * (n - 1))
                for part, half in enumerate((0, 0, 1)):
                    sp.dma_start(qc[32 * part:32 * part + 32, par, :, :].bitcast(F32), rows[:, :, half, 0, :]).then_inc(q_in, 16)

            def attn_b_pair(i):
                if valid(i + 1):
                    restack(i + 1, 0)
                if valid(i - 2):
                    store_xn(1, i - 2)
                if valid(i + 3):
                    y_in(0, i + 3)
                if valid(i + 1):
                    restack(i + 1, 1)

            with sp.Fori(0, PAIRS) as i:
                store_xn(0, i)
            weights(0, 0)
            for l in range(LAYERS):
                with sp.Fori(1, E // 2) as i:
                    weights(l, i)
                for k in range(RING):
                    sp.wait_ge(sca[k], 32 * (l + 1) * E * CHUNKS // RING)
                y_in(l, 0)
                if l == 0:
                    y_in(0, 1)
                    weights(1, 0)
                    for i in range(-1, 2):
                        attn_b_pair(i)
                    with sp.Fori(2, PAIRS - 3) as i:
                        attn_b_pair(i)
                    for i in range(PAIRS - 3, PAIRS + 1):
                        attn_b_pair(i)
                    store_xn(1, PAIRS - 1)
            with sp.Fori(1, PAIRS) as i:
                y_in(1, i)
            with sp.Fori(0, PAIRS) as i:
                alone(sp, S.y_used, PAIRS + i + 1, S.x_head)
                sp.dma_start(out_rows[:, bass.ds(4 * i, 4), :], x[:, bass.ds(4 * i, 4), :]).then_inc(S.stored, 16)
            sp.wait_ge(S.stored, 16 * PAIRS)

        @block.gpsimd
        def _(pool):
            n_const = 0

            def const(ins):
                nonlocal n_const
                n_const += 1
                return ins.then_inc(S.const_pool, 1)

            const(pool.memset(zero_rows[:, :, :], 0.0))
            const(pool.memset(ident[:, :], 0.0))
            const(pool.memset(before[:, :], 1.0))
            pool.wait_ge(S.const_pool, 3)
            for half in range(2):
                pool.dma_start(y_rows[half * T:(half + 1) * T, :].rearrange("(t p) d -> p t d", p=P),
                               zero_rows[:, :, :]).then_inc(S.y_zeroed, 16)
            const(pool.affine_select(out=ident[:, :], in_=ident[:, :], compare_op=ALU.not_equal, fill=1.0,
                                     base=0, pattern=[[-1, P]], channel_multiplier=1))
            const(pool.affine_select(out=before[:, :], in_=before[:, :], compare_op=ALU.is_gt, fill=0.0,
                                     base=0, pattern=[[1, P]], channel_multiplier=-1))
            const(pool.memset(neg_half[:, :], -0.5))
            const(pool.memset(ones_bf[:, :], 1.0))
            const(pool.iota(iota_lo[:, :], [[1, P]], base=0, channel_multiplier=0, allow_small_or_imprecise_dtypes=True))
            const(pool.iota(iota_hi[:, :], [[1, SLOT_TILES]], base=0, channel_multiplier=0, allow_small_or_imprecise_dtypes=True))
            const(pool.iota(part1[:, :], [[1, 1]], base=1, channel_multiplier=1, allow_small_or_imprecise_dtypes=True))
            const(pool.iota(rev[:, :], [[-1, E]], base=E, channel_multiplier=0, allow_small_or_imprecise_dtypes=True))
            const(pool.iota(slot_base[:, :, :], [[CAP, E], [0, NT]], base=0, channel_multiplier=0, allow_small_or_imprecise_dtypes=True))
            const(pool.iota(tile_code[:, :], [[1, 2 * NT]], base=0, channel_multiplier=0, allow_small_or_imprecise_dtypes=True))
            const(pool.memset(carry[:, :], 1.0))
            const(pool.memset(cmask[:, :], 0.0))
            pool.wait_ge(S.const_pool, n_const)
            const(pool.memset(carry[:, :].rearrange("p (r t) -> p r t", t=NT)[:, :, 0:1], 0.0))
            const(pool.affine_select(out=cmask[:, :], in_=cmask[:, :], compare_op=ALU.is_ge, fill=MASKED,
                                     base=0, pattern=[[-1, P]], channel_multiplier=1))
            assert n_const == N_CONST_POOL, n_const

            def rstd_of(mv_, ve_, out_, s_in, s_mid, s_out, n):
                alone(pool, s_in, n, S.const_pool)
                pool.tensor_scalar(ve_[:, :], mv_[:, :, 1], EPS, 1.0, ALU.add, ALU.mult).then_inc(s_mid, 1)
                alone(pool, s_mid, n, S.const_pool)
                pool.tensor_tensor(out_[:, :], ve_[:, :], neg_half[:, :], ALU.pow).then_inc(s_out, 1)

            rstd_of(mv, ve, rstd, S.ln_mv, S.ln_ve, S.ln_rstd, 1)
            with pool.Fori(0, PAIRS - 1) as i:
                rstd_of(mv, ve, rstd, S.ln_mv, S.ln_ve, S.ln_rstd, i + 2)
                rstd_of(mv2, ve2, rstd2, S.ln2_mv, S.ln2_ve, S.ln2_rstd, i + 1)
            rstd_of(mv2, ve2, rstd2, S.ln2_mv, S.ln2_ve, S.ln2_rstd, PAIRS)

            alone(pool, S.wb_in, 16 * 4, S.const_pool)
            for c in range(3):
                pool.tensor_copy(w3[:, c, :, :], qkv_w[:, :, c, :])
            pool.tensor_copy(ident_bf[:, :], ident[:, :]).then_inc(S.init_b, 1)
            pool.wait_ge(S.init_b, 1)
            pool.memset(kc[96:P, :, :, :].bitcast(F32), 1.0).then_inc(S.init_b, 1)
            pool.wait_ge(S.init_b, 2)
            pool.memset(negp[:, :, :, :], 0.0)
            pool.memset(v_ext[:, :, :, :, 0:HD], 0.0)
            pool.memset(v_ext[:, :, :, :, HD + 1:32], 0.0)
            pool.memset(v_ext[:, :, :, :, HD:HD + 1], 1.0)
            pool.memset(head_p[:, :, :], 1.0).then_inc(S.init_b, 1)
            pool.wait_ge(S.init_b, 3)
            pool.affine_select(out=head_p[:, :, :], in_=head_p[:, :, :], compare_op=ALU.is_ge, fill=0.0,
                               base=0, pattern=[[-32, 4], [-8, 4]], channel_multiplier=1).then_inc(S.init_b, 1)
            pool.wait_ge(S.init_b, 4)
            pool.affine_select(out=head_p[:, :, :], in_=head_p[:, :, :], compare_op=ALU.is_ge, fill=0.0,
                               base=HD - 1, pattern=[[32, 4], [8, 4]], channel_multiplier=-1).then_inc(S.init_b, 1)
            pool.wait_ge(S.init_b, 5)
            pool.tensor_tensor(head_p[:, 0:2, :], head_p[:, 0:2, :], head_p[:, 2:4, :], ALU.add).then_inc(S.init_b, 1)
            pool.wait_ge(S.init_b, 6)
            pool.tensor_tensor(head_m[:, :], head_p[:, 0, :], head_p[:, 1, :], ALU.add).then_inc(S.init_b, 1)

            def take_idx(n, h, ex):
                pool.tensor_copy(tok_cur[:, h, :], tok_idx[:, bass.ds(ST * ex, ST)]).then_inc(S.idx_cur, 1)
                pool.tensor_copy(row_cur[:, h, :], row_idx[:, bass.ds(ST * ex, ST)]).then_inc(S.idx_cur, 1)
                alone(pool, S.idx_cur, n, S.const_pool)

            def gather(l, i, k):
                i, k = i + k // (2 * CHUNKS), k % (2 * CHUNKS)
                h, c, r = k // CHUNKS, k % CHUNKS, k % RING
                alone(pool, S.xg_tr, l * E * CHUNKS + 2 * CHUNKS * i + k - RING + 1, S.const_pool)
                for j in range(CH):
                    pool.indirect_dma_start(xg[:, r, j, :], None, xn_rows,
                                            bass.IndirectOffsetOnAxis(ap=tok_cur[:, h, c * CH + j:c * CH + j + 1], axis=0)
                                            ).then_inc(gat[r], 16)

            def scatter(l, i, k):
                h, c, r = k // CHUNKS, k % CHUNKS, k % RING
                alone(pool, S.yo_ready, l * E * CHUNKS + 2 * CHUNKS * i + k + 1, S.const_pool)
                for j in range(CH):
                    pool.indirect_dma_start(y_rows, bass.IndirectOffsetOnAxis(ap=row_cur[:, h, c * CH + j:c * CH + j + 1], axis=0),
                                            yo[:, r, j, :], None, bounds_check=2 * T - 1, oob_is_err=False
                                            ).then_inc(sca[r], 16)

            AHEAD = 3

            def expert_pair(l, i, last):
                for k in range(2 * CHUNKS):
                    if not last or k + AHEAD < 2 * CHUNKS:
                        gather(l, i, k + AHEAD)
                    scatter(l, i, k)
                    if not last and k == CHUNKS:
                        for r in range(RING):
                            alone(pool, sca[r], 32 * (l * E * CHUNKS // RING + 2 * i + 1), S.const_pool)
                        take_idx(2 * E * l + 4 * i + 6, 0, 2 * i + 2)
                if not last:
                    for r in range(RING):
                        alone(pool, sca[r], 32 * (l * E * CHUNKS // RING + 2 * i + 2), S.const_pool)
                    take_idx(2 * E * l + 4 * i + 8, 1, 2 * i + 3)

            def block_diag(t, par, g):
                U = 2 * GRP * t + GRP * par + g
                if g == 0:
                    alone(pool, (S.kc_in0, S.kc_in1)[par], 48 * t + 48, S.const_pool)
                alone(pool, S.c_done, 3 * (U - 2 * GRP) + 3, S.const_pool)
                for j in range(4):
                    a = pool.tensor_scalar(bdk[:, par, g, j, :], kc[:, par, g, :].bitcast(F32), head_m[:, j:j + 1], 1.0,
                                           ALU.mult, ALU.mult)
                a.then_inc(S.bd_done, 1)

            def causal(t, par, g):
                U = 2 * GRP * t + GRP * par + g
                alone(pool, S.exp_done, 3 * U + 3, S.const_pool)
                first = pt[:, g % 2, 0:2, :].rearrange("p u (j q) -> p (u j) q", j=2)[:, :, 0:P]
                second = pt[:, g % 2, 2, :].rearrange("p (j q) -> p j q", j=4)
                for blk in (first, second):
                    a = pool.affine_select(out=blk, in_=blk, compare_op=ALU.is_ge, fill=0.0, base=0,
                                           pattern=[[0, 4], [1, P]], channel_multiplier=-1)
                a.then_inc(S.aff_done, 1)

            def place_v(t, par):
                n = 2 * t + par
                alone(pool, S.vb_ready, n + 1, S.const_pool)
                alone(pool, S.pv_done, GRP * (n - 1), S.const_pool)
                pool.tensor_copy(v_ext[:, par, :, :, 0:HD], v_s[:, par, :, :].rearrange("p k (h d) -> p k h d", d=HD)
                                 ).then_inc(S.v_set, 1)

            def add_ob(i):
                alone(pool, S.xn_ready, PAIRS + i + 1, S.const_pool)
                xs = x[:, bass.ds(4 * i, 4), :]
                pool.tensor_tensor(xs, xs, ob_b[:, :].unsqueeze(1).broadcast_to([P, 4, D]), ALU.add).then_inc(S.ob_added, 1)

            def attn_b_pair(i):
                for h in range(2):
                    for g in range(GRP):
                        if h == 0 and g == 0 and valid(i - 2):
                            rstd_of(mv2, ve2, rstd2, S.ln2_mv, S.ln2_ve, S.ln2_rstd, PAIRS + i - 1)
                        if h == 1 and g == 3 and valid(i + 2):
                            rstd_of(mv, ve, rstd, S.ln_mv, S.ln_ve, S.ln_rstd, PAIRS + i + 3)
                        t, par, gg = shifted_group(i, h, g, 2)
                        if valid(t):
                            block_diag(t, par, gg)
                        t, par, gg = shifted_group(i, h, g, -2)
                        if valid(t):
                            causal(t, par, gg)
                        if h == 0 and g == 1 and valid(i + 1):
                            add_ob(i + 1)
                        t, par, gg = shifted_group(i, h, g, GRP)
                        if g == 3 and valid(t):
                            place_v(t, par)

            for l in range(LAYERS):
                alone(pool, S.index_ready, l + 1, S.const_pool)
                if l == 0:
                    alone(pool, S.y_zeroed, 32, S.const_pool)
                alone(pool, S.xn2_stored, 16 * PAIRS * (l + 1), S.const_pool)
                take_idx(2 * E * l + 2, 0, 0)
                take_idx(2 * E * l + 4, 1, 1)
                for k in range(AHEAD):
                    gather(l, 0, k)
                expert_pair(l, 0, False)
                with pool.Fori(1, E // 2 - 1) as i:
                    expert_pair(l, i, False)
                expert_pair(l, E // 2 - 1, True)
                if l == 0:
                    rstd_of(mv, ve, rstd, S.ln_mv, S.ln_ve, S.ln_rstd, PAIRS + 1)
                    pool.wait_ge(S.init_b, 7)
                    for i in range(-1, 2):
                        attn_b_pair(i)
                    with pool.Fori(2, PAIRS - 2) as i:
                        attn_b_pair(i)
                    for i in range(PAIRS - 2, PAIRS + 1):
                        attn_b_pair(i)
                    rstd_of(mv2, ve2, rstd2, S.ln2_mv, S.ln2_ve, S.ln2_rstd, 2 * PAIRS)

        @block.tensor
        def _(pe):
            pe.wait_ge(S.const_pool, N_CONST_POOL)
            pe.wait_ge(S.w_in, 16 * 10)
            pe.transpose(bank[0][:, 0:38], bias_rows[:, :], ident[0:38, 0:38]).then_inc(S.bias_tr, 1)
            for k, w in enumerate((wq, wk, wv)):
                m = pe.transpose(bank[1][:, k * P:(k + 1) * P], w[:, :], ident[:, :])
            m.then_inc(S.w_tr, 1)
            pe.wait_ge(S.w_trs, 2)
            pe.matmul(bank[2][:, 0:P], wT[:, 0, :], wT[:, 1, :], start=True, stop=True)
            pe.matmul(bank[2][:, P:2 * P], wT[:, 2, :], wo_m[:, :], start=True, stop=True).then_inc(S.wfold_mm, 1)
            pe.wait_ge(S.wfold, 1)
            pe.wait_ge(S.bias_set, 1)

            T_, GT_, V_, S_, PT_, Y_, R_, L_ = bank

            def a1(n, nb):
                need(pe, S.xnT_ready, n)
                for j in range(2):
                    m = pe.transpose(T_[:, j * P:(j + 1) * P], xn[:, 2 * nb + j, :], ident[:, :])
                m.then_inc(S.xn_tr, 1)

            def a2(n, nb):
                pe.wait_ge(S.xnT_ready, n + 1)
                need(pe, S.gT_ready, n)
                pe.matmul(GT_[:, 0:SEQ], m_qk[:, :], xnT[:, nb, :], start=True, stop=True).then_inc(S.g_done, 1)
                need(pe, S.v_ready, n)
                for j in range(2):
                    m = pe.matmul(V_[:, j * P:(j + 1) * P], xnT[:, nb, j * P:(j + 1) * P], m_vo[:, :], start=True, stop=True)
                m.then_inc(S.v_done, 1)

            def a3(n, nb):
                pe.wait_ge(S.gT_ready, n + 1)
                need(pe, S.probs_ready, n)
                for q in range(2):
                    m = pe.matmul(S_[:, q * SEQ:(q + 1) * SEQ], gT[:, q * P:(q + 1) * P], xnT[:, nb, :], start=True, stop=True)
                m.then_inc(S.scores_done, 1)

            def a4(q_, b):
                pe.wait_ge(S.probs_ready, q_ + 1)
                need(pe, S.pT_ready, q_)
                for kt in range(2):
                    for q in range(2):
                        m = pe.transpose(PT_[:, kt * SEQ + q * P:kt * SEQ + (q + 1) * P], probs[:, b, q, kt * P:(kt + 1) * P], ident[:, :])
                m.then_inc(S.probs_tr, 1)

            def a5(q_, b):
                pe.wait_ge(S.pT_ready, q_ + 1)
                pe.wait_ge(S.v_ready, q_ + 1)
                need(pe, S.attn_added, q_)
                for q in range(2):
                    for kt in range(2):
                        m = pe.matmul(Y_[:, q * P:(q + 1) * P], pT[:, kt, q * P:(q + 1) * P], v_s[:, b, kt, :],
                                      start=(kt == 0), stop=(kt == 1))
                m.then_inc(S.y_done, 1)

            def r_transpose(n, bk=R_):
                pe.wait_ge(S.xn2_ready, n + 1)
                need(pe, S.log_ready, n)
                for j in range(4):
                    m = pe.transpose(bk[:, j * P:(j + 1) * P], xn2[:, j, :], ident[:, :])
                m.then_inc(S.xn2_tr, 1)

            def r_logits(n, i, bk=L_):
                pe.wait_ge(S.xn2T_ready, n + 1)
                pe.matmul(bk[0:E, 0:512], router[:, :], xnT_all[:, bass.ds(512 * i, 512)], start=True, stop=True).then_inc(S.logT_done, 1)

            def r_back(n, bk=R_):
                alone(pe, S.logT_ready, n + 1, S.const_pool)
                for j in range(4):
                    m = pe.transpose(bk[:, j * E:(j + 1) * E], logT[:, j * P:(j + 1) * P], ident[0:E, 0:E])
                m.then_inc(S.log_done, 1)

            def attn_pair(i, first, last):
                for h in range(2):
                    cur, nxt, more = 2 * i + h, 2 * i + h + 1, not (last and h == 1)
                    if more:
                        if h == 1:
                            pe.wait_ge(S.xn_ready, i + 2)
                        a1(nxt, 1 - h)
                    if not first:
                        if h == 0:
                            r_transpose(i - 1)
                        else:
                            r_back(i - 1)
                    a4(cur, h)
                    if more:
                        a2(nxt, 1 - h)
                    if not first and h == 0:
                        r_logits(i - 1, i - 1)
                    a5(cur, h)
                    if more:
                        a3(nxt, 1 - h)

            pe.wait_ge(S.xn_ready, 1)
            a1(0, 0)
            a2(0, 0)
            a3(0, 0)
            attn_pair(0, True, False)
            with pe.Fori(1, PAIRS - 1) as i:
                attn_pair(i, False, False)
            attn_pair(PAIRS - 1, False, True)
            r_transpose(PAIRS - 1)
            r_logits(PAIRS - 1, PAIRS - 1)
            r_back(PAIRS - 1)

            HB = bank[0:4]
            XT = bank[4:6]
            YB = bank[6:8]

            def sh_first(l, c, cb):
                for f in range(FT):
                    need(pe, S.sh1_ready, l * PAIRS * FT + 4 * c - FT + f + 1)
                    pe.matmul(HB[f][:, :], sw1_s[:, f * P:(f + 1) * P], xnT_all[:, bass.ds(512 * c, 512)],
                              start=True, stop=True).then_inc(S.sh1_done, 1)

            def sh_second(l, c, cb):
                pe.wait_ge(S.sh1_ready, l * PAIRS * FT + FT * c + FT)
                need(pe, S.sh2_ready, l * PAIRS + c - 1)
                for t in range(4):
                    for f in range(FT):
                        m = pe.matmul(YB[cb][:, t * P:(t + 1) * P], hsh[:, cb, f, t * P:(t + 1) * P], sw2_s[:, f, :],
                                      start=(f == 0), stop=(f == FT - 1))
                m.then_inc(S.sh2_done, 1)

            def shared_pair(l, i, first):
                for h in range(2):
                    c = 2 * i + h
                    sh_first(l, c, h)
                    if not (first and h == 0):
                        sh_second(l, c - 1, 1 - h)

            def counts(l):
                pe.wait_ge(S.masks_ready, l + 1)
                flat = MK[:, :, :, :].rearrange("p c e t -> p (c e t)")
                pe.matmul(XT[0][:, :], before[:, :], flat, start=True, stop=True)
                pe.matmul(XT[1][:, :], ones_bf[:, :], flat, start=True, stop=True).then_inc(S.count_done, 1)

            def index(l):
                pe.wait_ge(S.onehot_ready, l + 1)
                for n in range(2 * NT):
                    m = pe.matmul(XT[0][:, 0:2 * SLOT_TILES], OL[:, n, :], RH[:, n, :, :].rearrange("p a s -> p (a s)"),
                                  start=(n == 0), stop=(n == 2 * NT - 1))
                m.then_inc(S.index_done, 1)

            def x_tr(l, i, k):
                i, k = i + k // (2 * CHUNKS), k % (2 * CHUNKS)
                r = k % RING
                pe.wait_ge(gat[r], 32 * (l * E * CHUNKS // RING + 2 * i + k // RING + 1))
                n = l * E * CHUNKS + 2 * CHUNKS * i + k
                need(pe, S.xgT_ready, n - 1)
                for j in range(CH):
                    m = pe.transpose(XT[k % 2][:, j * P:(j + 1) * P], xg[:, r, j, :], ident[:, :])
                m.then_inc(S.xg_tr, 1)

            def first_mm(l, i, k):
                n = l * E * CHUNKS + 2 * CHUNKS * i + k
                h = k // CHUNKS
                if k % CHUNKS == 0:
                    pe.wait_ge((S.w1_in0, S.w1_in1)[h], 32 * (l * E // 2 + i + 1))
                pe.wait_ge(S.xgT_ready, n + 1)
                need(pe, S.h_ready, n - 1)
                for f in range(FT):
                    bk = HB[2 * (k % 2) + f // 2]
                    m = pe.matmul(bk[:, (f % 2) * 256:(f % 2) * 256 + 256], w1_s[h][:, f * P:(f + 1) * P], xgT[:, k % 2, :],
                                  start=True, stop=True)
                m.then_inc(S.h_done, 1)

            def second_mm(l, i, k):
                if k < 0:
                    i, k = i - 1, k + 2 * CHUNKS
                n = l * E * CHUNKS + 2 * CHUNKS * i + k
                h = k // CHUNKS
                pe.wait_ge(S.h_ready, n + 1)
                need(pe, S.yo_ready, n - 1)
                for j in range(CH):
                    for f in range(FT):
                        m = pe.matmul(YB[k % 2][:, j * P:(j + 1) * P], hT[:, k % 2, f, j * P:(j + 1) * P], w2_s[h][:, f, :],
                                      start=(f == 0), stop=(f == FT - 1))
                m.then_inc(S.yo_done, 1)

            def expert_pair(l, i, first, last):
                for k in range(2 * CHUNKS):
                    first_mm(l, i, k)
                    if not (last and k == 2 * CHUNKS - 1):
                        x_tr(l, i, k + 1)
                    if not (first and k == 0):
                        second_mm(l, i, k - 1)

            AB, CB, OB, MB, XB, ZB = bank[0:2], bank[2:4], bank[4], bank[5], bank[6], bank[7]

            def pass1(t, par, g):
                U = 2 * GRP * t + GRP * par + g
                if g == 0:
                    pe.wait_ge((S.qc_in0, S.qc_in1)[par], 48 * t + 48)
                pe.wait_ge(S.bd_done, U + 1)
                for k in range(3):
                    bk, qt = AB[(g + k) % 2], min(k, 1)
                    need(pe, S.amax_done, 3 * U + k - 1)
                    q = qc[0:96, par, g, qt * P:qt * P + P]
                    if k == 0:
                        pe.matmul(bk[:, :], q, bdk[0:96, par, g, :, 0:P], start=True, stop=False)
                        m = pe.matmul(bk[:, :], ident_bf[:, :], cmask[:, :].unsqueeze(1).broadcast_to([P, 4, P]),
                                      start=False, stop=True)
                    else:
                        pe.matmul(bk[:, :], q, bdk[0:96, par, g, 2 * k - 2:2 * k, :], start=True, stop=False)
                        m = pe.matmul(bk[:, :].rearrange("p (j k) -> p j k", j=2)[:, :, P:SEQ], ident_bf[:, :],
                                      cmask[:, :].unsqueeze(1).broadcast_to([P, 2, P]), start=False, stop=True)
                    m.then_inc(S.a_done, 1)

            def neg_transpose(t, par, g):
                U = 2 * GRP * t + GRP * par + g
                pe.wait_ge(S.amax_done, 3 * U + 3)
                need(pe, S.neg_set, U)
                for qt in range(2):
                    m = pe.transpose(MB[:, qt * P:qt * P + P], negp[:, g % 2, qt, :], ident[:, :])
                m.then_inc(S.negT_done, 1)

            def pass2(t, par, g):
                U = 2 * GRP * t + GRP * par + g
                pe.wait_ge(S.neg_set, U + 1)
                for k in range(3):
                    bk = CB[(g + k) % 2]
                    need(pe, S.exp_done, 3 * U + k - 1)
                    if k < 2:
                        for j in range(2):
                            m = pe.matmul(bk[:, j * SEQ:j * SEQ + SEQ], bdk[:, par, g, 2 * k + j, 0:P], qc[:, par, g, :],
                                          start=True, stop=True)
                    else:
                        for j in range(4):
                            m = pe.matmul(bk[:, j * P:j * P + P], bdk[:, par, g, j, P:SEQ], qc[:, par, g, P:SEQ],
                                          start=True, stop=True)
                    m.then_inc(S.c_done, 1)

            def values(t, par, g):
                n = 2 * t + par
                U = GRP * n + g
                pe.wait_ge(S.aff_done, U + 1)
                if g == 0:
                    pe.wait_ge(S.v_set, n + 1)
                if g % 2 == 0:
                    need(pe, S.ot_ready, 2 * n + g // 2)
                c0 = (g % 2) * SEQ
                for kt in range(2):
                    for j in range(4):
                        if kt == 0:
                            rhs = pt[:, g % 2, j // 2, (j % 2) * SEQ:(j % 2) * SEQ + SEQ]
                        else:
                            rhs = pt[:, g % 2, 2, j * P:j * P + P]
                        m = pe.matmul(OB[32 * j:32 * j + 32, c0 + kt * P:c0 + SEQ], v_ext[:, par, kt, 4 * g + j, :], rhs,
                                      start=(kt == 0), stop=(kt == 1))
                m.then_inc(S.pv_done, 1)

            def b_transpose(t, par):
                n = 2 * t + par
                pe.wait_ge(S.xn_ready, PAIRS + t + 1)
                need(pe, S.vb_ready, n)
                for j in range(2):
                    m = pe.transpose(ZB[:, j * P:(j + 1) * P], xn[:, 2 * par + j, :], ident[:, :])
                m.then_inc(S.tb_done, 1)

            def b_project(t, par):
                n = 2 * t + par
                pe.wait_ge(S.tb_ready, n + 1)
                need(pe, S.onT_ready, n - 3)
                need(pe, S.qk32_ready, n)
                for c in range(2):
                    m = pe.matmul(XB[:, c * SEQ:(c + 1) * SEQ], w3[:, c, :, :].rearrange("p h d -> p (h d)"), xnT[:, par, :],
                                  start=True, stop=True)
                m.then_inc(S.qk_done, 1)
                for j in range(2):
                    m = pe.matmul(ZB[:, j * P:(j + 1) * P], xnT[:, par, j * P:(j + 1) * P],
                                  w3[:, 2, :, :].rearrange("p h d -> p (h d)"), start=True, stop=True)
                m.then_inc(S.vb_done, 1)

            def o_back(t, par):
                n = 2 * t + par
                pe.wait_ge(S.ot_ready, 2 * n + 2)
                need(pe, S.xb_added, n)
                for qt in range(2):
                    for g in range(GRP):
                        m = pe.transpose((XB, ZB)[qt][:, g * P:(g + 1) * P], oT[:, g, qt * P:(qt + 1) * P], ident[:, :])
                m.then_inc(S.otr_done, 1)

            def on_transpose(t, par):
                n = 2 * t + par
                pe.wait_ge(S.on_ready, n + 1)
                for qt in range(2):
                    m = pe.transpose(XB[:, qt * P:(qt + 1) * P], on[:, qt, :, :].rearrange("p h d -> p (h d)"), ident[:, :])
                m.then_inc(S.onT_done, 1)

            def out_project(t, par):
                n = 2 * t + par
                pe.wait_ge(S.onT_ready, n + 1)
                need(pe, S.qk32_ready, min(n + 5, SEQS) if isinstance(n, int) else n + 5)
                for qt in range(2):
                    m = pe.matmul(XB[:, qt * P:(qt + 1) * P], onT[:, qt * P:(qt + 1) * P], ow[:, :], start=True, stop=True)
                m.then_inc(S.pr_done, 1)

            def attn_b_pair(i):
                for h in range(2):
                    for g in range(GRP):
                        if valid(i):
                            pass1(i, h, g)
                        if g == 0:
                            if valid(i - 1):
                                on_transpose(i - 1, h)
                            if valid(i + 1):
                                b_transpose(i + 1, h)
                        if g == 1 and valid(i + 1):
                            b_project(i + 1, h)
                        if g == 2:
                            if valid(i - 1):
                                out_project(i - 1, h)
                            if valid(i + 1):
                                pe.wait_ge(S.vb_ready, 2 * i + h + 3)
                            if valid(i - 2) and h == 0:
                                r_transpose(PAIRS + i - 2, ZB)
                            if valid(i - 2) and h == 1:
                                r_logits(PAIRS + i - 2, i - 2, ZB)
                        t, par, gg = shifted_group(i, h, g, -1)
                        if valid(t):
                            neg_transpose(t, par, gg)
                        t, par, gg = shifted_group(i, h, g, -2)
                        if valid(t):
                            pass2(t, par, gg)
                        t, par, gg = shifted_group(i, h, g, -3)
                        if valid(t):
                            values(t, par, gg)
                        if g == 2 and h == 1 and valid(i - 2):
                            r_back(PAIRS + i - 2, ZB)
                        t, par, gg = shifted_group(i, h, g, -GRP)
                        if g == 3 and valid(t):
                            if valid(i - 2):
                                if h == 0:
                                    pe.wait_ge(S.xn2T_ready, PAIRS + i - 1)
                                else:
                                    pe.wait_ge(S.log_ready, PAIRS + i - 1)
                            o_back(t, par)

            for l in range(LAYERS):
                if l == 0:
                    pe.wait_ge(S.w_moe_in, 16 * 4)
                shared_pair(l, 0, True)
                counts(l)
                with pe.Fori(1, PAIRS // 2 - 1) as i:
                    shared_pair(l, i, False)
                index(l)
                shared_pair(l, PAIRS // 2 - 1, False)
                sh_second(l, PAIRS - 1, 1)
                pe.wait_ge(S.index_ready, l + 1)
                pe.wait_ge(S.sh2_ready, PAIRS * (l + 1))
                x_tr(l, 0, 0)
                expert_pair(l, 0, True, False)
                with pe.Fori(1, E // 2 - 1) as i:
                    expert_pair(l, i, False, False)
                expert_pair(l, E // 2 - 1, False, True)
                second_mm(l, E // 2 - 1, 2 * CHUNKS - 1)
                if l == 0:
                    pe.wait_ge(S.init_b, 7)
                    for i in range(-1, 2):
                        attn_b_pair(i)
                    with pe.Fori(2, PAIRS - 2) as i:
                        attn_b_pair(i)
                    for i in range(PAIRS - 2, PAIRS + 1):
                        attn_b_pair(i)
                    r_transpose(2 * PAIRS - 1, ZB)
                    r_logits(2 * PAIRS - 1, PAIRS - 1, ZB)
                    r_back(2 * PAIRS - 1, ZB)
                    pe.wait_ge(S.log_ready, 2 * PAIRS)

        @block.scalar
        def _(act):
            for dst, src in ((wq, w_q), (wk, w_k), (wv, w_v), (wo, w_o), (router, router_w)):
                act.dma_start(dst[:, :], src).then_inc(S.w_in, 16)
            act.dma_start(mask_i[:, :], hd_mask.rearrange("(p a) -> p a", a=1)).then_inc(S.w_in, 16)
            act.dma_start(bias_rows[0:E * FT, :], b1.rearrange("e (f p) -> (e f) p", p=P)).then_inc(S.w_in, 16)
            act.dma_start(bias_rows[E * FT:E * FT + FT, :], sb1.rearrange("(f p) -> f p", p=P)).then_inc(S.w_in, 16)
            qkv_b = attn_b.rearrange("(h c d) -> c h d", c=3, d=8)
            act.dma_start(bias_rows[36:37, :], qkv_b[0:1].rearrange("c h d -> c h d")).then_inc(S.w_in, 16)
            act.dma_start(bias_rows[37:38, :], qkv_b[1:2].rearrange("c h d -> c h d")).then_inc(S.w_in, 16)
            act.wait_ge(S.w_tr, 1)
            act.activation(wT[:, :, :].rearrange("p a d -> p (a d)"), bank[1][:, 0:3 * P], ACT.Copy).then_inc(S.w_trs, 1)
            act.wait_ge(S.bias_tr, 1)
            act.activation(bias_T[:, :], bank[0][:, 0:38], ACT.Copy).then_inc(S.bias_set, 1)

            T_, GT_, V_, S_, PT_, Y_, R_, L_ = bank

            def t_copy(n, nb):
                act.wait_ge(S.xn_tr, n + 1)
                need(act, S.scores_done, n - 1)
                act.activation(xnT[:, nb, :], T_[:, 0:SEQ], ACT.Copy).then_inc(S.xnT_ready, 1)

            def v_copy(n, nb):
                act.wait_ge(S.v_done, n + 1)
                need(act, S.y_done, n - 1)
                act.activation(v_s[:, nb, :, :].rearrange("p a d -> p (a d)"), V_[:, 0:SEQ], ACT.Copy).then_inc(S.v_ready, 1)

            def exps(n, nb):
                act.wait_ge(S.max_ready, n + 1)
                need(act, S.probs_tr, n - 1)
                for q in range(2):
                    a = act.activation(probs[:, nb, q, :], S_[:, q * SEQ:(q + 1) * SEQ], ACT.Exp,
                                       bias=negmax[:, nb, q:q + 1], accum_out=psums[:, nb, q:q + 1])
                a.then_inc(S.probs_ready, 1)

            def r_copy(n, i, bk=R_):
                act.wait_ge(S.xn2_tr, n + 1)
                act.activation(xnT_all[:, bass.ds(512 * i, 512)], bk[:, :], ACT.Copy).then_inc(S.xn2T_ready, 1)

            def logT_copy(n, bk=L_):
                act.wait_ge(S.logT_done, n + 1)
                need(act, S.log_done, n)
                act.activation(logT[:, :], bk[0:E, 0:512], ACT.Copy).then_inc(S.logT_ready, 1)

            def log_copy(n, i, bk=R_):
                act.wait_ge(S.log_done, n + 1)
                act.activation(logits[:, bass.ds(4 * i, 4), :].rearrange("p t e -> p (t e)"), bk[:, 0:4 * E], ACT.Copy).then_inc(S.log_ready, 1)

            def attn_pair(i, first, last):
                for h in range(2):
                    nxt, more = 2 * i + h + 1, not (last and h == 1)
                    if more:
                        t_copy(nxt, 1 - h)
                    if not first:
                        if h == 0:
                            r_copy(i - 1, i - 1)
                        else:
                            log_copy(i - 1, i - 1)
                    if more:
                        v_copy(nxt, 1 - h)
                    if not first and h == 0:
                        logT_copy(i - 1)
                    if more:
                        exps(nxt, 1 - h)

            t_copy(0, 0)
            v_copy(0, 0)
            exps(0, 0)
            attn_pair(0, True, False)
            with act.Fori(1, PAIRS - 1) as i:
                attn_pair(i, False, False)
            attn_pair(PAIRS - 1, False, True)
            r_copy(PAIRS - 1, PAIRS - 1)
            logT_copy(PAIRS - 1)
            log_copy(PAIRS - 1, PAIRS - 1)

            HB, YB = bank[0:4], bank[6:8]

            def sh_silu(l, c, cb):
                need(act, S.sh2_done, l * PAIRS + c - 1)
                for f in range(FT):
                    act.wait_ge(S.sh1_done, l * PAIRS * FT + FT * c + f + 1)
                    act.activation(hsh[:, cb, f, :], HB[f][:, :], ACT.Silu,
                                   bias=bias_T[:, E * FT + f:E * FT + f + 1]).then_inc(S.sh1_ready, 1)

            def sh_out(l, c, cb):
                act.wait_ge(S.sh2_done, l * PAIRS + c + 1)
                act.activation(shared[:, bass.ds(4 * c, 4), :].rearrange("p t d -> p (t d)"), YB[cb][:, :], ACT.Copy,
                               scale=SHARED_SCALE).then_inc(S.sh2_ready, 1)

            def shared_pair(l, i, first):
                for h in range(2):
                    c = 2 * i + h
                    sh_silu(l, c, h)
                    if not (first and h == 0):
                        sh_out(l, c - 1, 1 - h)

            def silus(l, i, k):
                n = l * E * CHUNKS + 2 * CHUNKS * i + k
                h = k // CHUNKS
                if k % CHUNKS == 0:
                    e = 2 * i + h
                    act.activation(b1_cur[:, h, :], bias_T[:, bass.ds(FT * e, FT)], ACT.Copy).then_inc(S.b1_set, 1)
                    act.wait_ge(S.b1_set, l * E + e + 1)
                act.wait_ge(S.h_done, n + 1)
                need(act, S.yo_done, n - 1)
                for f in range(FT):
                    a = act.activation(hT[:, k % 2, f, :], HB[2 * (k % 2) + f // 2][:, (f % 2) * 256:(f % 2) * 256 + 256],
                                       ACT.Silu, bias=b1_cur[:, h, f:f + 1])
                a.then_inc(S.h_ready, 1)

            act.activation(bq_s[:, :], bias_T[:, 36:37], ACT.Copy, scale=HD ** -0.5)

            AB, CB, OB, MB, XB, ZB = bank[0:2], bank[2:4], bank[4], bank[5], bank[6], bank[7]

            def o_copy(t, par, half):
                n = 2 * t + par
                act.wait_ge(S.pv_done, GRP * n + 2 * half + 2)
                need(act, S.otr_done, n)
                act.activation(oT[:, 2 * half:2 * half + 2, :].rearrange("p g t -> p (g t)"), OB[:, :], ACT.Copy).then_inc(S.ot_ready, 1)

            def on_copy(t, par):
                n = 2 * t + par
                act.wait_ge(S.onT_done, n + 1)
                need(act, S.pr_done, n)
                act.activation(onT[:, :], XB[:, 0:SEQ], ACT.Copy).then_inc(S.onT_ready, 1)

            def bt_copy(t, par):
                n = 2 * t + par
                act.wait_ge(S.tb_done, n + 1)
                need(act, S.vb_done, n - 1)
                act.activation(xnT[:, par, :], ZB[:, 0:SEQ], ACT.Copy).then_inc(S.tb_ready, 1)

            def qk_bias(t, par):
                n = 2 * t + par
                act.wait_ge(S.qk_done, n + 1)
                need(act, S.hilo_done, n)
                act.activation(qk32[:, 0, :], XB[:, 0:SEQ], ACT.Identity, bias=bq_s[:, 0:1], scale=HD ** -0.5)
                act.activation(qk32[:, 1, :], XB[:, SEQ:2 * SEQ], ACT.Identity, bias=bias_T[:, 37:38]).then_inc(S.qk32_ready, 1)

            def neg_copy(t, par, g):
                U = 2 * GRP * t + GRP * par + g
                act.wait_ge(S.negT_done, U + 1)
                act.activation(qc[96:P, par, g, :], MB[96:P, 0:SEQ], ACT.Copy).then_inc(S.neg_set, 1)

            def exps_b(t, par, g):
                U = 2 * GRP * t + GRP * par + g
                need(act, S.pv_done, U - 1)
                for k in range(3):
                    act.wait_ge(S.c_done, 3 * U + k + 1)
                    act.activation(pt[:, g % 2, k, :], CB[(g + k) % 2][:, :], ACT.Exp).then_inc(S.exp_done, 1)

            def attn_b_pair(i):
                for h in range(2):
                    for g in range(GRP):
                        t, par, gg = shifted_group(i, h, g, -GRP)
                        if g % 2 == 1 and valid(t):
                            o_copy(t, par, g // 2)
                        if g == 0:
                            if valid(i - 1):
                                on_copy(i - 1, h)
                            if valid(i + 1):
                                bt_copy(i + 1, h)
                        if g == 1 and valid(i + 1):
                            qk_bias(i + 1, h)
                        if g == 2 and valid(i - 2):
                            if h == 0:
                                r_copy(PAIRS + i - 2, i - 2, ZB)
                            else:
                                logT_copy(PAIRS + i - 2, ZB)
                        t, par, gg = shifted_group(i, h, g, -1)
                        if valid(t):
                            neg_copy(t, par, gg)
                        t, par, gg = shifted_group(i, h, g, -2)
                        if valid(t):
                            exps_b(t, par, gg)
                        if g == 2 and h == 1 and valid(i - 2):
                            log_copy(PAIRS + i - 2, i - 2, ZB)

            for l in range(LAYERS):
                act.wait_ge(S.y_zeroed, 32)
                act.wait_ge(S.shifted, l + 1)
                act.activation(G[:, :, :], G[:, :, :], ACT.Exp).then_inc(S.exped, 1)
                shared_pair(l, 0, True)
                with act.Fori(1, PAIRS // 2) as i:
                    shared_pair(l, i, False)
                sh_out(l, PAIRS - 1, 1)
                for k in range(2 * CHUNKS):
                    silus(l, 0, k)
                with act.Fori(1, E // 2) as i:
                    for k in range(2 * CHUNKS):
                        silus(l, i, k)
                if l == 0:
                    for i in range(-1, 2):
                        attn_b_pair(i)
                    with act.Fori(2, PAIRS - 2) as i:
                        attn_b_pair(i)
                    for i in range(PAIRS - 2, PAIRS + 1):
                        attn_b_pair(i)
                    r_copy(2 * PAIRS - 1, PAIRS - 1, ZB)
                    logT_copy(2 * PAIRS - 1, ZB)
                    log_copy(2 * PAIRS - 1, PAIRS - 1, ZB)

        @block.vector
        def _(dve):
            dve.wait_ge(S.w_in, 16 * 10)
            dve.tensor_copy(mask_f[:, :], mask_i[:, :]).then_inc(S.const_dve, 1)
            dve.wait_ge(S.const_dve, 1)
            dve.tensor_scalar(wo_m[:, :], wo[:, :], mask_f[:, 0:1], None, ALU.mult).then_inc(S.w_trs, 1)
            dve.wait_ge(S.wfold_mm, 1)
            dve.tensor_scalar(m_qk[:, :], bank[2][:, 0:P], float(D) ** -0.5, None, ALU.mult)
            dve.tensor_copy(m_vo[:, :], bank[2][:, P:2 * P]).then_inc(S.wfold, 1)

            T_, GT_, V_, S_, PT_, Y_, R_, L_ = bank

            def stats(i, n, st_, mv_, s_st, s_mv):
                for j in range(4):
                    a = dve.bn_stats(st_[:, j, :], x[:, bass.ds(4 * i + j, 1), :].rearrange("p a d -> p (a d)"))
                a.then_inc(s_st, 1)
                alone(dve, s_st, n, S.const_dve)
                for j in range(4):
                    a = dve.bn_aggr(mv_[:, j, :], st_[:, j, :])
                a.then_inc(s_mv, 1)

            def norm(i, n, dst, mv_, rstd_, s_rstd, s_out):
                dve.wait_ge(s_rstd, n)
                for j in range(4):
                    a = dve.tensor_scalar(dst[:, j, :], x[:, bass.ds(4 * i + j, 1), :].rearrange("p a d -> p (a d)"),
                                          mv_[:, j, 0:1], rstd_[:, j:j + 1], ALU.subtract, ALU.mult)
                a.then_inc(s_out, 1)

            def norm_a(i):
                need(dve, S.xn_tr, 2 * i)
                norm(i, i + 1, xn, mv, rstd, S.ln_rstd, S.xn_ready)

            def norm_r(n, i):
                need(dve, S.xn2_tr, n)
                need(dve, S.xn2_stored, 16 * n)
                norm(i, n + 1, xn2, mv2, rstd2, S.ln2_rstd, S.xn2_ready)

            def g_copy(n):
                dve.wait_ge(S.g_done, n + 1)
                need(dve, S.scores_done, n)
                dve.tensor_copy(gT[:, :], GT_[:, 0:SEQ]).then_inc(S.gT_ready, 1)

            def maxes(n, nb):
                dve.wait_ge(S.scores_done, n + 1)
                dve.tensor_reduce(negmax[:, nb, :], S_[:, :].rearrange("p (q k) -> p q k", q=2), AX.X, ALU.max,
                                  negate=True).then_inc(S.max_ready, 1)

            def p_copy(q_, b):
                dve.wait_ge(S.probs_tr, q_ + 1)
                need(dve, S.y_done, q_)
                dve.tensor_copy(pT[:, :, :].rearrange("p a k -> p (a k)"), PT_[:, :]).then_inc(S.pT_ready, 1)
                dve.reciprocal(rsum[:, b, :], psums[:, b, :]).then_inc(S.rsum_ready, 1)

            def add_attn(q_, b, i, h):
                dve.wait_ge(S.y_done, q_ + 1)
                dve.wait_ge(S.rsum_ready, q_ + 1)
                for q in range(2):
                    xs = x[:, bass.ds(4 * i + 2 * h + q, 1), :].rearrange("p a d -> p (a d)")
                    a = dve.scalar_tensor_tensor(out=xs, in0=Y_[:, q * P:(q + 1) * P], scalar=rsum[:, b, q:q + 1], in1=xs,
                                                 op0=ALU.mult, op1=ALU.add)
                a.then_inc(S.attn_added, 1)

            def attn_pair(i, first, last):
                for h in range(2):
                    cur, nxt, more = 2 * i + h, 2 * i + h + 1, not (last and h == 1)
                    if h == 0:
                        if not first:
                            norm_r(i - 1, i - 1)
                        if not last:
                            stats(i + 1, i + 2, st, mv, S.ln_stats, S.ln_mv)
                    p_copy(cur, h)
                    if more:
                        g_copy(nxt)
                    if h == 0 and not last:
                        norm_a(i + 1)
                    add_attn(cur, h, i, h)
                    if more:
                        maxes(nxt, 1 - h)
                    if h == 1:
                        alone(dve, S.attn_added, 2 * i + 2, S.const_dve)
                        stats(i, i + 1, st2, mv2, S.ln2_stats, S.ln2_mv)

            dve.wait_ge(S.x_head, 16)
            stats(0, 1, st, mv, S.ln_stats, S.ln_mv)
            norm_a(0)
            g_copy(0)
            maxes(0, 0)
            dve.wait_ge(S.x_tail, 16)
            attn_pair(0, True, False)
            with dve.Fori(1, PAIRS - 1) as i:
                attn_pair(i, False, False)
            attn_pair(PAIRS - 1, False, True)
            norm_r(PAIRS - 1, PAIRS - 1)

            steps = [0]

            def step(ins, wait=True):
                steps[0] += 1
                ins.then_inc(S.route, 1)
                if wait:
                    dve.wait_ge(S.route, steps[0])

            def over_e(a):
                return a.unsqueeze(2).broadcast_to([P, NT, E])

            def routing(l):
                XT = bank[4:6]
                dve.wait_ge(S.log_ready, PAIRS * (l + 1))
                if l == 0:
                    dve.wait_ge(S.const_pool, N_CONST_POOL)
                    dve.wait_ge(S.w_moe_in, 16 * 4)
                step(dve.tensor_reduce(r1[:, :], logits[:, :, :], AX.X, ALU.max))
                dve.tensor_tensor(G[:, :, :], logits[:, :, :], over_e(r1[:, :]), ALU.subtract).then_inc(S.shifted, 1)
                dve.wait_ge(S.exped, l + 1)
                step(dve.tensor_reduce(r1[:, :], G[:, :, :], AX.X, ALU.add))
                step(dve.reciprocal(r2[:, :], r1[:, :]))
                step(dve.tensor_tensor(G[:, :, :], G[:, :, :], over_e(r2[:, :]), ALU.mult))
                rev_b = rev[:, :].unsqueeze(1).broadcast_to([P, NT, E])
                for c, g in enumerate((G, G1)):
                    step(dve.tensor_reduce(r1[:, :], g[:, :, :], AX.X, ALU.max))
                    step(dve.tensor_tensor(t1[:, :, :], g[:, :, :], over_e(r1[:, :]), ALU.is_equal))
                    step(dve.tensor_tensor(t1[:, :, :], t1[:, :, :], rev_b, ALU.mult))
                    step(dve.tensor_reduce(r2[:, :], t1[:, :, :], AX.X, ALU.max))
                    step(dve.tensor_tensor(m1[:, :, :], t1[:, :, :], over_e(r2[:, :]), ALU.is_equal))
                    a = dve.tensor_copy(MK[:, c, :, :].rearrange("p e t -> p t e"), m1[:, :, :])
                    if c == 0:
                        step(dve.tensor_tensor(t1[:, :, :], G[:, :, :], m1[:, :, :], ALU.mult))
                        step(dve.tensor_tensor(G1[:, :, :], G[:, :, :], t1[:, :, :], ALU.subtract))
                a.then_inc(S.masks_ready, 1)
                dve.wait_ge(S.masks_ready, l + 1)
                flat = lambda a: a[:, :, :, :].rearrange("p c e t -> p (c e t)")
                dve.wait_ge(S.count_done, l + 1)
                step(dve.tensor_tensor_scan(flat(INC), carry[:, :], XT[1][:, :], 0.0, ALU.mult, ALU.add))
                step(dve.tensor_tensor(flat(POS), flat(INC), XT[0][:, :], ALU.add), False)
                step(dve.tensor_scalar(keep1[:, :], INC[:, 0, :, NT - 1], float(CAP), None, ALU.min))
                step(dve.tensor_tensor(flat(POS), flat(POS), XT[1][:, :], ALU.subtract))
                step(dve.tensor_tensor(POS[:, 1, :, :], POS[:, 1, :, :], keep1[:, :].unsqueeze(2).broadcast_to([P, E, NT]), ALU.add))
                step(dve.scalar_tensor_tensor(out=flat(KM), in0=flat(POS), scalar=float(CAP), in1=flat(MK), op0=ALU.is_lt, op1=ALU.mult))
                for c in range(2):
                    step(dve.tensor_tensor(POS[:, c, :, :], POS[:, c, :, :], slot_base[:, :, :], ALU.add), c == 1)
                step(dve.tensor_tensor(flat(POS), flat(POS), flat(KM), ALU.mult), False)
                for c in range(2):
                    step(dve.tensor_tensor(GK[:, c, :, :], KM[:, c, :, :], G[:, :, :].rearrange("p t e -> p e t"), ALU.mult), c == 1)
                for c in range(2):
                    step(dve.tensor_reduce(slot[:, c, :], POS[:, c, :, :].rearrange("p e t -> p t e"), AX.X, ALU.add), False)
                    step(dve.tensor_reduce(fill[:, c, :], KM[:, c, :, :].rearrange("p e t -> p t e"), AX.X, ALU.add), c == 1)
                step(dve.tensor_copy(slot_i[:, :, :], slot[:, :, :]))
                step(dve.tensor_scalar(hi_i[:, :, :], slot_i[:, :, :], 7, None, ALU.logical_shift_right), False)
                step(dve.tensor_scalar(lo_i[:, :, :], slot_i[:, :, :], 127, None, ALU.bitwise_and), False)
                step(dve.tensor_scalar(fill[:, :, :], fill[:, :, :], -float(P), float(P), ALU.mult, ALU.add))
                step(dve.tensor_copy(hi_f[:, :, :], hi_i[:, :, :]), False)
                step(dve.tensor_copy(lo_b[:, :], lo_i[:, :, :].rearrange("p c t -> p (c t)")))
                step(dve.tensor_tensor(hi_b[:, :], hi_f[:, :, :].rearrange("p c t -> p (c t)"),
                                       fill[:, :, :].rearrange("p c t -> p (c t)"), ALU.add))
                n2 = 2 * NT
                step(dve.tensor_tensor(OL[:, :, :], iota_lo[:, :].unsqueeze(1).broadcast_to([P, n2, P]),
                                       lo_b[:, :].unsqueeze(2).broadcast_to([P, n2, P]), ALU.is_equal), False)
                step(dve.tensor_tensor(OH[:, :, :], iota_hi[:, :].unsqueeze(1).broadcast_to([P, n2, SLOT_TILES]),
                                       hi_b[:, :].unsqueeze(2).broadcast_to([P, n2, SLOT_TILES]), ALU.is_equal))
                dve.tensor_scalar(RH[:, :, 0, :], OH[:, :, :], part1[:, 0:1], None, ALU.mult)
                dve.tensor_tensor(RH[:, :, 1, :], OH[:, :, :], tile_code[:, :].unsqueeze(2).broadcast_to([P, n2, SLOT_TILES]),
                                  ALU.mult).then_inc(S.onehot_ready, 1)
                for c in range(2):
                    step(dve.tensor_reduce(gate[:, c, :], GK[:, c, :, :].rearrange("p e t -> p t e"), AX.X, ALU.add), c == 1)
                step(dve.tensor_tensor(den[:, :], gate[:, 0, :], gate[:, 1, :], ALU.add))
                step(dve.tensor_scalar(den[:, :], den[:, :], TINY, None, ALU.max))
                step(dve.reciprocal(r1[:, :], den[:, :]))
                step(dve.tensor_tensor(gate[:, :, :], gate[:, :, :], r1[:, :].unsqueeze(1).broadcast_to([P, 2, NT]), ALU.mult))
                dve.wait_ge(S.index_done, l + 1)
                a_, b_ = XT[0][:, 0:SLOT_TILES], XT[0][:, SLOT_TILES:2 * SLOT_TILES]
                step(dve.tensor_scalar(row_f[:, :], b_, float(P), -1.0, ALU.mult, ALU.add))
                step(dve.tensor_tensor(row_f[:, :], a_, row_f[:, :], ALU.add))
                step(dve.tensor_scalar(row_e[:, :], b_, float(NT), -float(T), ALU.is_ge, ALU.mult))
                step(dve.tensor_tensor(row_e[:, :], row_e[:, :], row_f[:, :], ALU.add))
                step(dve.tensor_scalar(tok_idx[:, :], row_e[:, :], 0.0, None, ALU.max))
                step(dve.tensor_scalar(row_e[:, :], a_, 0.0, 4.0 * T, ALU.is_equal, ALU.mult))
                dve.tensor_tensor(row_idx[:, :], row_e[:, :], row_f[:, :], ALU.add).then_inc(S.index_ready, 1)

            def add_shared(l):
                for c in range(PAIRS):
                    dve.wait_ge(S.sh2_ready, l * PAIRS + c + 1)
                    dve.tensor_tensor(x[:, 4 * c:4 * c + 4, :], x[:, 4 * c:4 * c + 4, :], shared[:, 4 * c:4 * c + 4, :], ALU.add).then_inc(S.shared_added, 1)
                dve.wait_ge(S.shared_added, PAIRS * 2 * l + PAIRS)
                for c in range(PAIRS):
                    dve.scalar_tensor_tensor(out=x[:, 4 * c:4 * c + 4, :], in0=sb2_b[:, :].unsqueeze(1).broadcast_to([P, 4, D]),
                                             scalar=SHARED_SCALE, in1=x[:, 4 * c:4 * c + 4, :], op0=ALU.mult, op1=ALU.add).then_inc(S.shared_added, 1)
                dve.wait_ge(S.shared_added, PAIRS * 2 * l + 2 * PAIRS)

            def xg_copy(l, i, k):
                i, k = i + k // (2 * CHUNKS), k % (2 * CHUNKS)
                n = l * E * CHUNKS + 2 * CHUNKS * i + k
                dve.wait_ge(S.xg_tr, n + 1)
                need(dve, S.h_done, n - 1)
                dve.tensor_copy(xgT[:, k % 2, :], bank[4 + k % 2][:, 0:CH * P]).then_inc(S.xgT_ready, 1)

            def y_copy(l, i, k):
                if k < 0:
                    i, k = i - 1, k + 2 * CHUNKS
                n = l * E * CHUNKS + 2 * CHUNKS * i + k
                r, ex = k % RING, 2 * i + k // CHUNKS
                dve.wait_ge(S.yo_done, n + 1)
                need(dve, sca[r], 32 * (l * E * CHUNKS // RING + 2 * i + k // RING))
                dve.tensor_tensor(yo[:, r, :, :], bank[6 + k % 2][:, 0:CH * P].rearrange("p (a d) -> p a d", a=CH),
                                  b2_b[:, bass.ds(ex, 1), :].broadcast_to([P, CH, D]), ALU.add).then_inc(S.yo_ready, 1)

            def expert_pair(l, i, first, last):
                for k in range(2 * CHUNKS):
                    if not (last and k == 2 * CHUNKS - 1):
                        xg_copy(l, i, k + 1)
                    if not (first and k == 0):
                        y_copy(l, i, k - 1)

            def combine(l, pair, c):
                if c == 0:
                    dve.wait_ge(S.y_in, 32 * (l * PAIRS + pair + 1))
                else:
                    dve.wait_ge(S.comb, l * PAIRS + pair + 1)
                for j in range(4):
                    t = 4 * pair + j
                    xs = x[:, bass.ds(t, 1), :].rearrange("p a d -> p (a d)")
                    a = dve.scalar_tensor_tensor(out=xs, in0=yab[:, c, j, :], scalar=gate[:, c, bass.ds(t, 1)],
                                                 in1=xs, op0=ALU.mult, op1=ALU.add)
                a.then_inc((S.comb, S.y_used)[c], 1)

            AB, CB, OB, MB, XB, ZB = bank[0:2], bank[2:4], bank[4], bank[5], bank[6], bank[7]

            def maxes_b(t, par, g):
                U = 2 * GRP * t + GRP * par + g
                need(dve, S.negT_done, U - 1)
                for k in range(3):
                    dve.wait_ge(S.a_done, 3 * U + k + 1)
                    heads, first = (4, 0) if k == 0 else (2, 2 * k - 2)
                    dst = negp[:, g % 2, min(k, 1), 96:P].rearrange("p (j r) -> p j r", r=8)[:, first:first + heads, 0]
                    dve.tensor_reduce(dst, AB[(g + k) % 2][:, :].rearrange("p (j k) -> p j k", j=heads), AX.X, ALU.max,
                                      negate=True).then_inc(S.amax_done, 1)

            def split(t, par):
                n = 2 * t + par
                dve.wait_ge(S.qk32_ready, n + 1)
                need(dve, (S.qks_stored0, S.qks_stored1)[par], 16 * t)
                dve.tensor_copy(qks[:, par, 0, :, :], qk32[:, :, :]).then_inc(S.hilo_hi, 1)
                dve.wait_ge(S.hilo_hi, n + 1)
                dve.tensor_tensor(qks[:, par, 1, :, :], qk32[:, :, :], qks[:, par, 0, :, :].bitcast(F32),
                                  ALU.subtract).then_inc(S.hilo_done, 1)

            def v_bias(t, par):
                n = 2 * t + par
                dve.wait_ge(S.vb_done, n + 1)
                need(dve, S.v_set, n - 1)
                dve.tensor_tensor(v_s[:, par, :, :], ZB[:, 0:SEQ].rearrange("p (k d) -> p k d", k=2),
                                  bv_b[:, :, :].rearrange("p h d -> p (h d)").unsqueeze(1).broadcast_to([P, 2, D]),
                                  ALU.add).then_inc(S.vb_ready, 1)

            def divide(t, par):
                n = 2 * t + par
                dve.wait_ge(S.otr_done, n + 1)
                need(dve, S.onT_done, n)
                o = [bk[:, :].rearrange("p (h r) -> p h r", r=32) for bk in (XB, ZB)]
                for qt in range(2):
                    a = dve.reciprocal(osum[:, qt, :], o[qt][:, :, HD])
                a.then_inc(S.osum_ready, 1)
                dve.wait_ge(S.osum_ready, n + 1)
                for qt in range(2):
                    a = dve.tensor_tensor(on[:, qt, :, :], o[qt][:, :, 0:HD],
                                          osum[:, qt, :].unsqueeze(2).broadcast_to([P, HEADS, HD]), ALU.mult)
                a.then_inc(S.on_ready, 1)

            def add_out(t, par):
                n = 2 * t + par
                dve.wait_ge(S.pr_done, n + 1)
                dve.wait_ge(S.ob_added, t + 1)
                xs = x[:, bass.ds(4 * t + 2 * par, 2), :]
                dve.tensor_tensor(xs, xs, XB[:, 0:SEQ].rearrange("p (k d) -> p k d", k=2), ALU.add).then_inc(S.xb_added, 1)

            def stats_b(i):
                alone(dve, S.y_used, i + 1, S.const_dve)
                stats(i, PAIRS + i + 1, st, mv, S.ln_stats, S.ln_mv)

            def norm_b(i):
                need(dve, S.tb_done, 2 * i)
                norm(i, PAIRS + i + 1, xn, mv, rstd, S.ln_rstd, S.xn_ready)

            def attn_b_pair(i):
                for h in range(2):
                    for g in range(GRP):
                        if valid(i):
                            maxes_b(i, h, g)
                        if g == 0 and h == 0 and valid(i - 2):
                            norm_r(PAIRS + i - 2, i - 2)
                        if g == 0 and h == 1 and valid(i + 2):
                            combine(0, i + 2, 1)
                        if g == 1 and valid(i + 1):
                            split(i + 1, h)
                            v_bias(i + 1, h)
                        if g == 2 and valid(i - 1):
                            add_out(i - 1, h)
                        if g == 2 and valid(i + 2):
                            if h == 0:
                                combine(0, i + 2, 0)
                            else:
                                stats_b(i + 2)
                        t, par, gg = shifted_group(i, h, g, -GRP)
                        if g == 3 and valid(t):
                            divide(t, par)
                        if g == 3 and h == 1:
                            if valid(i + 2):
                                norm_b(i + 2)
                            if valid(i - 1):
                                alone(dve, S.xb_added, 2 * i, S.const_dve)
                                stats(i - 1, PAIRS + i, st2, mv2, S.ln2_stats, S.ln2_mv)

            for l in range(LAYERS):
                routing(l)
                add_shared(l)
                xg_copy(l, 0, 0)
                expert_pair(l, 0, True, False)
                with dve.Fori(1, E // 2 - 1) as i:
                    expert_pair(l, i, False, False)
                expert_pair(l, E // 2 - 1, False, True)
                y_copy(l, E // 2 - 1, 2 * CHUNKS - 1)
                if l == 0:
                    dve.wait_ge(S.wb_in, 16 * 4)
                    dve.wait_ge(S.init_b, 7)
                    combine(0, 0, 0)
                    combine(0, 0, 1)
                    stats_b(0)
                    norm_b(0)
                    for i in range(-1, 2):
                        attn_b_pair(i)
                    with dve.Fori(2, PAIRS - 2) as i:
                        attn_b_pair(i)
                    for i in range(PAIRS - 2, PAIRS + 1):
                        attn_b_pair(i)
                    norm_r(2 * PAIRS - 1, PAIRS - 1)
            with dve.Fori(0, PAIRS) as i:
                combine(1, i, 0)
                combine(1, i, 1)



_INS = ['L0_attn_a_x', 'L0_attn_a_head_dim_mask', 'L0_attn_a_w_q', 'L0_attn_a_w_k', 'L0_attn_a_w_v', 'L0_attn_a_w_o',
        'L0_attn_b_attn_W', 'L0_attn_b_attn_b', 'L0_attn_b_out_W', 'L0_attn_b_out_b', 'L0_ffn_router_w', 'L0_ffn_w1',
        'L0_ffn_b1', 'L0_ffn_w2', 'L0_ffn_b2', 'L0_ffn_sw1', 'L0_ffn_sb1', 'L0_ffn_sw2', 'L0_ffn_sb2']


def kernel(**inputs):
    import numpy as np
    import concourse.bacc as bacc
    from concourse.bass_utils import run_bass_kernel_spmd

    nc = bacc.Bacc("TRN2", target_bir_lowering=False, num_devices=1)
    arrays, args = {}, []
    for name in _INS:
        a = np.ascontiguousarray(inputs[name])
        arrays[f"in_{name}"] = a
        args.append(nc.dram_tensor(f"in_{name}", a.shape, mybir.dt.from_np(a.dtype), kind="ExternalInput").ap())
    out = nc.dram_tensor("out_x", (SEQS, SEQ, D), F32, kind="ExternalOutput").ap()
    build(nc, *args, out)
    r = run_bass_kernel_spmd(nc, [arrays], core_ids=[0])
    return r.results[0]["out_x"]
```

```python
import math
from contextlib import ExitStack

import concourse.bass as bass
from concourse import mybir

ALU = mybir.AluOpType
ACT = mybir.ActivationFunctionType
AX = mybir.AxisListType
F32 = mybir.dt.float32
BF16 = mybir.dt.bfloat16
F32R = mybir.dt.float32r
I32 = mybir.dt.int32
U32 = mybir.dt.uint32

P = 128
SEQS, SEQ, D = 16, 256, 128
T = SEQS * SEQ
NT = T // P
PAIRS = SEQS // 2
E, F = 8, 512
FT = F // P
CAP = min(max(4, math.ceil(2 * 1.25 * T / E)), T)
ST = CAP // P
CH = 2
CHUNKS = ST // CH
SLOT_TILES = E * ST
RING = 5
EPS = 1e-5
TINY = 1.1920928955078125e-07
MASKED = -1e30
SHARED_SCALE = 0.1
HEADS, HD = 16, 8
GRP = HEADS // 4
LAYERS = 2


def need(eng, sem, value):
    if not isinstance(value, int) or value > 0:
        eng.wait_ge(sem, value)


def alone(eng, sem, value, set_already):
    if not isinstance(value, int):
        value = eng.to_reg(value)
        eng.wait_ge(set_already, 1)
    need(eng, sem, value)


def valid(pair):
    return not isinstance(pair, int) or 0 <= pair < PAIRS


def shifted_group(i, h, g, by):
    q = GRP * h + g + by
    return i + q // (2 * GRP), q // GRP % 2, q % GRP


def shifted_seq(i, h, by):
    return i + (h + by) // 2, (h + by) % 2


class Signals:
    pass


def build(nc, x_in, hd_mask, w_q, w_k, w_v, w_o, attn_W, attn_b, out_W, out_b, router_w,
          w1, b1, w2, b2, sw1, sb1, sw2, sb2, out):
    with ExitStack() as ctx:
        def sb(name, shape, dt=F32):
            return ctx.enter_context(nc.sbuf_tensor(name, shape, dt))

        def sem(name):
            return ctx.enter_context(nc.semaphore(name))

        xn_rows = nc.dram_tensor("xn_rows", [T, D], F32).ap()
        y_rows = nc.dram_tensor("y_rows", [2 * T, D], F32).ap()
        y_slots = nc.dram_tensor("y_slots", [E * CAP, D], F32).ap()

        qk_rows = nc.dram_tensor("qk_rows", [2, P, 2, 2, SEQ], F32).ap()

        bank = [ctx.enter_context(nc.psum_tensor(f"bank{k}", [P, 512], F32)) for k in range(8)]

        ident = sb("ident", [P, P])
        ident_bf = sb("ident_bf", [P, P], BF16)
        before = sb("before", [P, P], BF16)
        ones_bf = sb("ones_bf", [P, P], BF16)
        iota_lo = sb("iota_lo", [P, P], BF16)
        iota_hi = sb("iota_hi", [P, SLOT_TILES], BF16)
        part1 = sb("part1", [P, 1])
        rev = sb("rev", [P, E])
        slot_base = sb("slot_base", [P, E, NT])
        tile_code = sb("tile_code", [P, 2 * NT], BF16)
        carry = sb("carry", [P, 2 * E * NT])
        neg_half = sb("neg_half", [P, 4])

        wq = sb("wq", [P, D]); wk = sb("wk", [P, D]); wv = sb("wv", [P, D]); wo = sb("wo", [P, D])
        mask_i = sb("mask_i", [P, 1], I32); mask_f = sb("mask_f", [P, 1])
        wT = sb("wT", [P, 3, D])
        wo_m = sb("wo_m", [P, D])
        m_qk = sb("m_qk", [P, D])
        m_vo = sb("m_vo", [P, D])
        router = sb("router", [P, E])
        sw1_s = sb("sw1_s", [P, F]); sw2_s = sb("sw2_s", [P, FT, D])
        bias_rows = sb("bias_rows", [38, P]); bias_T = sb("bias_T", [P, 38])
        b2_b = sb("b2_b", [P, E, D]); sb2_b = sb("sb2_b", [P, D])

        x = sb("x", [P, NT, D])
        xnT_all = sb("xnT_all", [P, T])
        logits = sb("logits", [P, NT, E])
        gate = sb("gate", [P, 2, NT])

        st = sb("st", [P, 4, 6]); mv = sb("mv", [P, 4, 2]); ve = sb("ve", [P, 4]); rstd = sb("rstd", [P, 4])
        st2 = sb("st2", [P, 4, 6]); mv2 = sb("mv2", [P, 4, 2]); ve2 = sb("ve2", [P, 4]); rstd2 = sb("rstd2", [P, 4])
        xn = sb("xn", [P, 4, D])
        xn2 = sb("xn2", [P, 4, D])
        logT = sb("logT", [E, 512])

        xnT = sb("xnT", [P, 2, SEQ]); v_s = sb("v_s", [P, 2, 2, D])
        negmax = sb("negmax", [P, 2, 2]); psums = sb("psums", [P, 2, 2]); rsum = sb("rsum", [P, 2, 2])

        r1 = sb("r1", [P, NT]); r2 = sb("r2", [P, NT])
        G = sb("G", [P, NT, E])
        MK = sb("MK", [P, 2, E, NT], BF16)
        keep1 = sb("keep1", [P, E])
        fill = sb("fill", [P, 2, NT]); slot = sb("slot", [P, 2, NT]); slot_i = sb("slot_i", [P, 2, NT], I32)
        slot_u = sb("slot_u", [P, 2, NT], U32); slot_cur = sb("slot_cur", [P, 2, 4], U32)
        hi_i = sb("hi_i", [P, 2, NT], I32); lo_i = sb("lo_i", [P, 2, NT], I32)
        hi_f = sb("hi_f", [P, 2, NT]); hi_b = sb("hi_b", [P, 2 * NT], BF16); lo_b = sb("lo_b", [P, 2 * NT], BF16)
        den = sb("den", [P, NT])
        with ExitStack() as shared_place:
            y_all = shared_place.enter_context(nc.sbuf_tensor("y_all", [P, 2, NT, D], F32))
        with ExitStack() as shared_place:
            def sb_r(name, shape, dt=F32):
                return shared_place.enter_context(nc.sbuf_tensor(name, shape, dt))

            shared = sb_r("shared", [P, NT, D])
            hsh = sb_r("hsh", [P, 2, FT, 512])
            G1 = sb_r("G1", [P, NT, E]); t1 = sb_r("t1", [P, NT, E]); m1 = sb_r("m1", [P, NT, E])
            INC = sb_r("INC", [P, 2, E, NT]); POS = sb_r("POS", [P, 2, E, NT]); KM = sb_r("KM", [P, 2, E, NT])
            GK = sb_r("GK", [P, 2, E, NT])
            OH = sb_r("OH", [P, 2 * NT, SLOT_TILES], BF16)
            OL = sb_r("OL", [P, 2 * NT, P], BF16)
            RH = sb_r("RH", [P, 2 * NT, 2, SLOT_TILES], BF16)

        zero_rows = shared

        bdk = sb("bdk", [P, 2, GRP, 4, SEQ], F32R)
        pt = sb("pt", [P, 2, 3, 512])
        qc = sb("qc", [P, 2, GRP, SEQ], F32R)
        qk32 = sb("qk32", [P, 2, SEQ])
        qks = sb("qks", [P, 2, 2, 2, SEQ], F32R)
        oT = sb("oT", [P, GRP, SEQ])
        on = sb("on", [P, 2, HEADS, HD]); onT = sb("onT", [P, SEQ]); osum = sb("osum", [P, 2, HEADS])
        probs = sb("probs", [P, 2, 2, SEQ]); pT = sb("pT", [P, 2, SEQ]); gT = sb("gT", [P, SEQ])
        xg = sb("xg", [P, RING, CH, D])
        yo = sb("yo", [P, RING, CH, D])
        hT = sb("hT", [P, 2, FT, CH * P])
        row_f = sb("row_f", [P, SLOT_TILES]); row_e = sb("row_e", [P, SLOT_TILES])
        tok_idx = sb("tok_idx", [P, SLOT_TILES], U32); row_idx = sb("row_idx", [P, SLOT_TILES], U32)

        w1_s = [sb(f"w1_s{k}", [P, F]) for k in range(2)]
        w2_s = [sb(f"w2_s{k}", [P, FT, D]) for k in range(2)]
        tok_cur = sb("tok_cur", [P, 2, ST], U32); row_cur = sb("row_cur", [P, 2, ST], U32)
        b1_cur = sb("b1_cur", [P, 2, FT])
        xgT = sb("xgT", [P, 2, CH * P])
        yab = sb("yab", [P, 2, 4, D])

        kc = sb("kc", [P, 2, GRP, SEQ], F32R)
        v_ext = sb("v_ext", [P, 2, 2, HEADS, 32])
        negp = sb("negp", [P, 2, 2, P])
        cmask = sb("cmask", [P, P], BF16)
        head_p = sb("head_p", [P, 4, 4]); head_m = sb("head_m", [P, 4])
        qkv_w = sb("qkv_w", [P, HEADS, 3, HD]); w3 = sb("w3", [P, 3, HEADS, HD]); ow = sb("ow", [P, D])
        bv_b = sb("bv_b", [P, HEADS, HD]); ob_b = sb("ob_b", [P, D]); bq_s = sb("bq_s", [P, 1])


        S = Signals()
        S.const_pool = sem("const_pool")
        S.const_dve = sem("const_dve")
        S.x_head = sem("x_head")
        S.x_tail = sem("x_tail")
        S.w_in = sem("w_in")
        S.w_moe_in = sem("w_moe_in")
        S.zero_set = sem("zero_set")
        S.y_zeroed = sem("y_zeroed")
        S.const_chain = sem("const_chain")
        S.bias_tr = sem("bias_tr")
        S.bias_set = sem("bias_set")
        S.w_tr = sem("w_tr")
        S.w_trs = sem("w_trs")
        S.wfold_mm = sem("wfold_mm")
        S.wfold = sem("wfold")
        S.ln_stats = sem("ln_stats")
        S.ln_mv = sem("ln_mv")
        S.ln_ve = sem("ln_ve")
        S.ln_rstd = sem("ln_rstd")
        S.xn_ready = sem("xn_ready")
        S.xn_tr = sem("xn_tr")
        S.xnT_ready = sem("xnT_ready")
        S.g_done = sem("g_done")
        S.gT_ready = sem("gT_ready")
        S.v_done = sem("v_done")
        S.v_ready = sem("v_ready")
        S.scores_done = sem("scores_done")
        S.max_ready = sem("max_ready")
        S.probs_ready = sem("probs_ready")
        S.probs_tr = sem("probs_tr")
        S.pT_ready = sem("pT_ready")
        S.y_done = sem("y_done")
        S.rsum_ready = sem("rsum_ready")
        S.attn_added = sem("attn_added")
        S.ln2_stats = sem("ln2_stats")
        S.ln2_mv = sem("ln2_mv")
        S.ln2_ve = sem("ln2_ve")
        S.ln2_rstd = sem("ln2_rstd")
        S.xn2_ready = sem("xn2_ready")
        S.xn2_tr = sem("xn2_tr")
        S.xn2T_ready = sem("xn2T_ready")
        S.xn2_stored = sem("xn2_stored")
        S.logT_done = sem("logT_done")
        S.logT_ready = sem("logT_ready")
        S.log_done = sem("log_done")
        S.log_ready = sem("log_ready")
        S.route = sem("route")
        S.shifted = sem("shifted")
        S.exped = sem("exped")
        S.masks_ready = sem("masks_ready")
        S.count_done = sem("count_done")
        S.onehot_ready = sem("onehot_ready")
        S.index_done = sem("index_done")
        S.index_ready = sem("index_ready")
        S.sh1_done = sem("sh1_done")
        S.sh1_ready = sem("sh1_ready")
        S.sh2_done = sem("sh2_done")
        S.sh2_ready = sem("sh2_ready")
        S.shared_added = sem("shared_added")
        S.xg_tr = sem("xg_tr")
        S.xgT_ready = sem("xgT_ready")
        S.h_done = sem("h_done")
        S.h_ready = sem("h_ready")
        S.yo_done = sem("yo_done")
        S.yo_ready = sem("yo_ready")
        S.w1_in0 = sem("w1_in0")
        S.w1_in1 = sem("w1_in1")
        S.idx_cur = sem("idx_cur")
        S.b1_set = sem("b1_set")
        S.comb = sem("comb")
        S.slot_cur = sem("slot_cur")
        S.bd_act = sem("bd_act")
        S.y_used = sem("y_used")
        S.stored = sem("stored")
        S.final_ready = sem("final_ready")
        S.wb_in = sem("wb_in")
        S.init_b = sem("init_b")
        S.tb_done = sem("tb_done")
        S.tb_ready = sem("tb_ready")
        S.qk_done = sem("qk_done")
        S.qk32_ready = sem("qk32_ready")
        S.vb_done = sem("vb_done")
        S.vb_ready = sem("vb_ready")
        S.hilo_hi = sem("hilo_hi")
        S.hilo_done = sem("hilo_done")
        S.qks_stored0 = sem("qks_stored0")
        S.qks_stored1 = sem("qks_stored1")
        S.kc_in0 = sem("kc_in0")
        S.kc_in1 = sem("kc_in1")
        S.qc_in0 = sem("qc_in0")
        S.qc_in1 = sem("qc_in1")
        S.bd_done = sem("bd_done")
        S.a_done = sem("a_done")
        S.amax_done = sem("amax_done")
        S.negT_done = sem("negT_done")
        S.neg_set = sem("neg_set")
        S.c_done = sem("c_done")
        S.exp_done = sem("exp_done")
        S.aff_done = sem("aff_done")
        S.pv_done = sem("pv_done")
        S.ot_ready = sem("ot_ready")
        S.otr_done = sem("otr_done")
        S.osum_ready = sem("osum_ready")
        S.on_ready = sem("on_ready")
        S.onT_done = sem("onT_done")
        S.onT_ready = sem("onT_ready")
        S.pr_done = sem("pr_done")
        S.xb_added = sem("xb_added")
        S.ob_added = sem("ob_added")
        S.v_set = sem("v_set")
        gat = [sem(f"gathered{k}") for k in range(RING)]
        sca = [sem(f"scattered{k}") for k in range(RING)]
        sto = [sem(f"slots_stored{k}") for k in range(RING)]
        y_back = [sem(f"y_back{k}") for k in range(4)]
        y_in = [sem(f"y_in{c}") for c in range(2)]
        N_CONST_POOL = 17

        x_rows = x_in.rearrange("b (h p) d -> p (b h) d", p=P)
        out_rows = out.rearrange("b (h p) d -> p (b h) d", p=P)

        block = ctx.enter_context(nc.Block())

        @block.sync
        def _(sp):
            sp.dma_start(x[:, 0:4, :], x_rows[:, 0:4, :]).then_inc(S.x_head, 16)
            sp.dma_start(x[:, 4:NT, :], x_rows[:, 4:NT, :]).then_inc(S.x_tail, 16)
            sp.dma_start(sw1_s[:, :], sw1).then_inc(S.w_moe_in, 16)
            sp.dma_start(sw2_s[:, :, :], sw2.rearrange("(f p) d -> p f d", p=P)).then_inc(S.w_moe_in, 16)
            sp.dma_start(b2_b[:, :, :], b2.unsqueeze(0).broadcast_to([P, E, D])).then_inc(S.w_moe_in, 16)
            sp.dma_start(sb2_b[:, :], sb2.unsqueeze(0).broadcast_to([P, D])).then_inc(S.w_moe_in, 16)
            sp.dma_start(qkv_w[:, :, :, :].rearrange("p h c d -> p (h c d)"), attn_W).then_inc(S.wb_in, 16)
            sp.dma_start(ow[:, :], out_W).then_inc(S.wb_in, 16)
            sp.dma_start(ob_b[:, :], out_b.unsqueeze(0).broadcast_to([P, D])).then_inc(S.wb_in, 16)
            sp.dma_start(bv_b[:, :, :], attn_b.rearrange("(h c d) -> c h d", c=3, d=HD)[2:3].broadcast_to([P, HEADS, HD])
                         ).then_inc(S.wb_in, 16)

            def store_xn(l, i):
                alone(sp, S.xn2_ready, PAIRS * l + i + 1, S.x_head)
                sp.dma_start(xn_rows.rearrange("(t p) d -> p t d", p=P)[:, bass.ds(4 * i, 4), :],
                             xn2[:, :, :]).then_inc(S.xn2_stored, 16)

            def weights(l, i, h):
                sm = (S.w1_in0, S.w1_in1)[h]
                alone(sp, S.yo_done, l * E * CHUNKS + (2 * i + h - 1) * CHUNKS, S.x_head)
                sp.dma_start(w1_s[h][:, :], w1[bass.ds(2 * i + h, 1), :, :].rearrange("a p f -> p (a f)")).then_inc(sm, 16)
                sp.dma_start(w2_s[h][:, :, :], w2[bass.ds(2 * i + h, 1), :, :].rearrange("a (f p) d -> p (a f) d", p=P)).then_inc(sm, 16)

            def store_slots(i, k):
                r, c = k % RING, k % CHUNKS
                alone(sp, S.yo_ready, 2 * CHUNKS * i + k + 1, S.x_head)
                rows = y_slots.rearrange("(e s p) d -> p e s d", e=E, p=P)
                for j in range(CH):
                    sp.dma_start(rows[:, bass.ds(2 * i + k // CHUNKS, 1), c * CH + j, :], yo[:, r, j:j + 1, :]).then_inc(sto[r], 16)

            def expert_pair(i, more):
                for k in range(2 * CHUNKS):
                    store_slots(i, k)
                    if more and k % CHUNKS == CHUNKS - 1:
                        weights(0, i + 1, k // CHUNKS)

            def restack(t, par):
                n = 2 * t + par
                rows_stored, k_in, q_in = ((S.qks_stored0, S.kc_in0, S.qc_in0), (S.qks_stored1, S.kc_in1, S.qc_in1))[par]
                alone(sp, S.hilo_done, n + 1, S.x_head)
                need(sp, k_in, 48 * t)
                need(sp, q_in, 48 * t)
                sp.dma_start(qk_rows[par], qks[:, par, :, :, :].bitcast(F32)).then_inc(rows_stored, 16)
                alone(sp, rows_stored, 16 * t + 16, S.x_head)
                need(sp, S.bd_done, GRP * (n - 1))
                need(sp, S.bd_act, GRP * (n - 1))
                rows = qk_rows[par].rearrange("(g r) a b t -> r g a b t", g=GRP)
                for part, half in enumerate((0, 1, 0)):
                    sp.dma_start(kc[32 * part:32 * part + 32, par, :, :].bitcast(F32), rows[:, :, half, 1, :]).then_inc(k_in, 16)
                need(sp, S.c_done, 3 * GRP * (n - 1))
                for part, half in enumerate((0, 0, 1)):
                    sp.dma_start(qc[32 * part:32 * part + 32, par, :, :].bitcast(F32), rows[:, :, half, 0, :]).then_inc(q_in, 16)

            def attn_b_pair(i):
                if valid(i + 1):
                    restack(i + 1, 0)
                if valid(i - 2):
                    store_xn(1, i - 2)
                if valid(i + 1):
                    restack(i + 1, 1)

            with sp.Fori(0, PAIRS) as i:
                store_xn(0, i)
            weights(0, 0, 0)
            weights(0, 0, 1)
            with sp.Fori(0, E // 2 - 1) as i:
                expert_pair(i, True)
            expert_pair(E // 2 - 1, False)
            weights(1, 0, 0)
            weights(1, 0, 1)
            for i in range(-1, 2):
                attn_b_pair(i)
            with sp.Fori(2, PAIRS - 3) as i:
                attn_b_pair(i)
            for i in range(PAIRS - 3, PAIRS + 1):
                attn_b_pair(i)
            store_xn(1, PAIRS - 1)
            with sp.Fori(1, E // 2) as i:
                weights(1, i, 0)
                weights(1, i, 1)
            for k in range(RING):
                sp.wait_ge(sca[k], 32 * E * CHUNKS // RING)
            sp.wait_ge(S.shared_added, 2 * PAIRS * LAYERS)
            part = NT // 4
            for k in range(4):
                for c in range(2):
                    src = y_rows[c * T:(c + 1) * T, :].rearrange("(t p) d -> p t d", p=P)
                    sp.dma_start(y_all[:, c, part * k:part * k + part, :], src[:, part * k:part * k + part, :]).then_inc(y_back[k], 16)
            with sp.Fori(0, PAIRS) as i:
                alone(sp, S.y_used, PAIRS + i + 1, S.x_head)
                sp.dma_start(out_rows[:, bass.ds(4 * i, 4), :], x[:, bass.ds(4 * i, 4), :]).then_inc(S.stored, 16)
            sp.wait_ge(S.stored, 16 * PAIRS)

        @block.gpsimd
        def _(pool):
            n_const = 0

            def const(ins):
                nonlocal n_const
                n_const += 1
                return ins.then_inc(S.const_pool, 1)

            const(pool.memset(zero_rows[:, :, :], 0.0))
            const(pool.memset(ident[:, :], 0.0))
            const(pool.memset(before[:, :], 1.0))
            pool.wait_ge(S.const_pool, 3)
            for half in range(2):
                pool.dma_start(y_rows[half * T:(half + 1) * T, :].rearrange("(t p) d -> p t d", p=P),
                               zero_rows[:, :, :]).then_inc(S.y_zeroed, 16)
            const(pool.affine_select(out=ident[:, :], in_=ident[:, :], compare_op=ALU.not_equal, fill=1.0,
                                     base=0, pattern=[[-1, P]], channel_multiplier=1))
            const(pool.affine_select(out=before[:, :], in_=before[:, :], compare_op=ALU.is_gt, fill=0.0,
                                     base=0, pattern=[[1, P]], channel_multiplier=-1))
            const(pool.memset(neg_half[:, :], -0.5))
            const(pool.memset(ones_bf[:, :], 1.0))
            const(pool.iota(iota_lo[:, :], [[1, P]], base=0, channel_multiplier=0, allow_small_or_imprecise_dtypes=True))
            const(pool.iota(iota_hi[:, :], [[1, SLOT_TILES]], base=0, channel_multiplier=0, allow_small_or_imprecise_dtypes=True))
            const(pool.iota(part1[:, :], [[1, 1]], base=1, channel_multiplier=1, allow_small_or_imprecise_dtypes=True))
            const(pool.iota(rev[:, :], [[-1, E]], base=E, channel_multiplier=0, allow_small_or_imprecise_dtypes=True))
            const(pool.iota(slot_base[:, :, :], [[CAP, E], [0, NT]], base=0, channel_multiplier=0, allow_small_or_imprecise_dtypes=True))
            const(pool.iota(tile_code[:, :], [[1, 2 * NT]], base=0, channel_multiplier=0, allow_small_or_imprecise_dtypes=True))
            const(pool.memset(carry[:, :], 1.0))
            const(pool.memset(cmask[:, :], 0.0))
            pool.wait_ge(S.const_pool, n_const)
            const(pool.memset(carry[:, :].rearrange("p (r t) -> p r t", t=NT)[:, :, 0:1], 0.0))
            const(pool.affine_select(out=cmask[:, :], in_=cmask[:, :], compare_op=ALU.is_ge, fill=MASKED,
                                     base=0, pattern=[[-1, P]], channel_multiplier=1))
            assert n_const == N_CONST_POOL, n_const

            def rstd_of(mv_, ve_, out_, s_in, s_mid, s_out, n):
                alone(pool, s_in, n, S.const_pool)
                pool.tensor_scalar(ve_[:, :], mv_[:, :, 1], EPS, 1.0, ALU.add, ALU.mult).then_inc(s_mid, 1)
                alone(pool, s_mid, n, S.const_pool)
                pool.tensor_tensor(out_[:, :], ve_[:, :], neg_half[:, :], ALU.pow).then_inc(s_out, 1)

            rstd_of(mv, ve, rstd, S.ln_mv, S.ln_ve, S.ln_rstd, 1)
            rstd_of(mv, ve, rstd, S.ln_mv, S.ln_ve, S.ln_rstd, 2)
            with pool.Fori(0, PAIRS - 2) as i:
                rstd_of(mv, ve, rstd, S.ln_mv, S.ln_ve, S.ln_rstd, i + 3)
                rstd_of(mv2, ve2, rstd2, S.ln2_mv, S.ln2_ve, S.ln2_rstd, i + 1)
            for i in range(PAIRS - 2, PAIRS):
                rstd_of(mv2, ve2, rstd2, S.ln2_mv, S.ln2_ve, S.ln2_rstd, i + 1)

            alone(pool, S.wb_in, 16 * 4, S.const_pool)
            for c in range(3):
                pool.tensor_copy(w3[:, c, :, :], qkv_w[:, :, c, :])
            pool.tensor_copy(ident_bf[:, :], ident[:, :]).then_inc(S.init_b, 1)
            pool.wait_ge(S.init_b, 1)
            pool.memset(kc[96:P, :, :, :].bitcast(F32), 1.0).then_inc(S.init_b, 1)
            pool.wait_ge(S.init_b, 2)
            pool.memset(negp[:, :, :, :], 0.0)
            pool.memset(v_ext[:, :, :, :, 0:HD], 0.0)
            pool.memset(v_ext[:, :, :, :, HD + 1:32], 0.0)
            pool.memset(v_ext[:, :, :, :, HD:HD + 1], 1.0)
            pool.memset(head_p[:, :, :], 1.0).then_inc(S.init_b, 1)
            pool.wait_ge(S.init_b, 3)
            pool.affine_select(out=head_p[:, :, :], in_=head_p[:, :, :], compare_op=ALU.is_ge, fill=0.0,
                               base=0, pattern=[[-32, 4], [-8, 4]], channel_multiplier=1).then_inc(S.init_b, 1)
            pool.wait_ge(S.init_b, 4)
            pool.affine_select(out=head_p[:, :, :], in_=head_p[:, :, :], compare_op=ALU.is_ge, fill=0.0,
                               base=HD - 1, pattern=[[32, 4], [8, 4]], channel_multiplier=-1).then_inc(S.init_b, 1)
            pool.wait_ge(S.init_b, 5)
            pool.tensor_tensor(head_p[:, 0:2, :], head_p[:, 0:2, :], head_p[:, 2:4, :], ALU.add).then_inc(S.init_b, 1)
            pool.wait_ge(S.init_b, 6)
            pool.tensor_tensor(head_m[:, :], head_p[:, 0, :], head_p[:, 1, :], ALU.add).then_inc(S.init_b, 1)

            def take_idx(n, h, ex):
                pool.tensor_copy(tok_cur[:, h, :], tok_idx[:, bass.ds(ST * ex, ST)]).then_inc(S.idx_cur, 1)
                pool.tensor_copy(row_cur[:, h, :], row_idx[:, bass.ds(ST * ex, ST)]).then_inc(S.idx_cur, 1)
                alone(pool, S.idx_cur, n, S.const_pool)

            def gather(l, i, k):
                i, k = i + k // (2 * CHUNKS), k % (2 * CHUNKS)
                h, c, r = k // CHUNKS, k % CHUNKS, k % RING
                alone(pool, S.xg_tr, l * E * CHUNKS + 2 * CHUNKS * i + k - RING + 1, S.const_pool)
                for j in range(CH):
                    pool.indirect_dma_start(xg[:, r, j, :], None, xn_rows,
                                            bass.IndirectOffsetOnAxis(ap=tok_cur[:, h, c * CH + j:c * CH + j + 1], axis=0)
                                            ).then_inc(gat[r], 16)

            def scatter(l, i, k):
                h, c, r = k // CHUNKS, k % CHUNKS, k % RING
                alone(pool, S.yo_ready, l * E * CHUNKS + 2 * CHUNKS * i + k + 1, S.const_pool)
                for j in range(CH):
                    pool.indirect_dma_start(y_rows, bass.IndirectOffsetOnAxis(ap=row_cur[:, h, c * CH + j:c * CH + j + 1], axis=0),
                                            yo[:, r, j, :], None, bounds_check=2 * T - 1, oob_is_err=False
                                            ).then_inc(sca[r], 16)

            AHEAD = 3

            def expert_pair(l, i, last):
                for k in range(2 * CHUNKS):
                    if not last or k + AHEAD < 2 * CHUNKS:
                        gather(l, i, k + AHEAD)
                    if l == 1:
                        scatter(l, i, k)
                    if not last and k == CHUNKS:
                        for r in range(RING):
                            alone(pool, (gat, sca)[l][r], 32 * (2 * i + 1), S.const_pool)
                        take_idx(2 * E * l + 4 * i + 6, 0, 2 * i + 2)
                if not last:
                    for r in range(RING):
                        alone(pool, (gat, sca)[l][r], 32 * (2 * i + 2), S.const_pool)
                    take_idx(2 * E * l + 4 * i + 8, 1, 2 * i + 3)

            def block_diag(t, par, g):
                U = 2 * GRP * t + GRP * par + g
                if g == 0:
                    alone(pool, (S.kc_in0, S.kc_in1)[par], 48 * t + 48, S.const_pool)
                alone(pool, S.c_done, 3 * (U - 2 * GRP) + 3, S.const_pool)
                for j in range(2):
                    a = pool.tensor_scalar(bdk[:, par, g, j, :], kc[:, par, g, :].bitcast(F32), head_m[:, j:j + 1], 1.0,
                                           ALU.mult, ALU.mult)
                a.then_inc(S.bd_done, 1)

            def causal(t, par, g):
                U = 2 * GRP * t + GRP * par + g
                alone(pool, S.exp_done, 3 * U + 3, S.const_pool)
                first = pt[:, g % 2, 0:2, :].rearrange("p u (j q) -> p (u j) q", j=2)[:, :, 0:P]
                second = pt[:, g % 2, 2, :].rearrange("p (j q) -> p j q", j=4)
                for blk in (first, second):
                    a = pool.affine_select(out=blk, in_=blk, compare_op=ALU.is_ge, fill=0.0, base=0,
                                           pattern=[[0, 4], [1, P]], channel_multiplier=-1)
                a.then_inc(S.aff_done, 1)

            def place_v(t, par):
                n = 2 * t + par
                alone(pool, S.vb_ready, n + 1, S.const_pool)
                alone(pool, S.pv_done, GRP * (n - 1), S.const_pool)
                pool.tensor_copy(v_ext[:, par, :, :, 0:HD], v_s[:, par, :, :].rearrange("p k (h d) -> p k h d", d=HD)
                                 ).then_inc(S.v_set, 1)

            def y_gather(p, c, j):
                if j == 0:
                    alone(pool, y_in[c], 64 * p, S.const_pool)
                    n = 2 * p + c + 1
                    pool.tensor_copy(slot_cur[:, c, :], slot_u[:, c, bass.ds(4 * p, 4)]).then_inc(S.slot_cur, 1)
                    alone(pool, S.slot_cur, n, S.const_pool)
                    alone(pool, (S.comb, S.y_used)[c], p, S.const_pool)
                pool.indirect_dma_start(yab[:, c, j, :], None, y_slots,
                                        bass.IndirectOffsetOnAxis(ap=slot_cur[:, c, j:j + 1], axis=0)).then_inc(y_in[c], 16)

            def add_ob(i):
                alone(pool, S.xn_ready, PAIRS + i + 1, S.const_pool)
                xs = x[:, bass.ds(4 * i, 4), :]
                pool.tensor_tensor(xs, xs, ob_b[:, :].unsqueeze(1).broadcast_to([P, 4, D]), ALU.add).then_inc(S.ob_added, 1)

            def attn_b_pair(i):
                for h in range(2):
                    for g in range(GRP):
                        if h == 1 and g == 2 and valid(i + 2):
                            rstd_of(mv, ve, rstd, S.ln_mv, S.ln_ve, S.ln_rstd, PAIRS + i + 3)
                        t, par, gg = shifted_group(i, h, g, 2)
                        if valid(t):
                            block_diag(t, par, gg)
                        if h == 0 and g == 0 and valid(i - 2):
                            rstd_of(mv2, ve2, rstd2, S.ln2_mv, S.ln2_ve, S.ln2_rstd, PAIRS + i - 1)
                        t, par, gg = shifted_group(i, h, g, -2)
                        if valid(t):
                            causal(t, par, gg)
                        if h == 0 and g == 1 and valid(i + 1):
                            add_ob(i + 1)
                        t, par, gg = shifted_group(i, h, g, GRP)
                        if g == 3 and valid(t):
                            place_v(t, par)
                        q = GRP * h + g - 2
                        if valid(i + 3 + q // (2 * GRP)) and not (isinstance(i, int) and i + 3 + q // (2 * GRP) < 1):
                            y_gather(i + 3 + q // (2 * GRP), q % (2 * GRP) // 4, q % 4)

            for l in range(LAYERS):
                alone(pool, S.index_ready, l + 1, S.const_pool)
                if l == 0:
                    alone(pool, S.y_zeroed, 32, S.const_pool)
                alone(pool, S.xn2_stored, 16 * PAIRS * (l + 1), S.const_pool)
                take_idx(2 * E * l + 2, 0, 0)
                take_idx(2 * E * l + 4, 1, 1)
                for k in range(AHEAD):
                    gather(l, 0, k)
                expert_pair(l, 0, False)
                with pool.Fori(1, E // 2 - 1) as i:
                    expert_pair(l, i, False)
                expert_pair(l, E // 2 - 1, True)
                if l == 0:
                    for r in range(RING):
                        alone(pool, sto[r], 32 * E * CHUNKS // RING, S.const_pool)
                    for c in range(2):
                        for k in range(4):
                            y_gather(0, c, k)
                    for k in range(4):
                        y_gather(1, 0, k)
                    rstd_of(mv, ve, rstd, S.ln_mv, S.ln_ve, S.ln_rstd, PAIRS + 1)
                    for k in range(2):
                        y_gather(1, 1, k)
                    pool.wait_ge(S.init_b, 7)
                    for i in range(-1, 2):
                        attn_b_pair(i)
                    with pool.Fori(2, PAIRS - 3) as i:
                        attn_b_pair(i)
                    for i in range(PAIRS - 3, PAIRS + 1):
                        attn_b_pair(i)
                    rstd_of(mv2, ve2, rstd2, S.ln2_mv, S.ln2_ve, S.ln2_rstd, 2 * PAIRS)

        @block.tensor
        def _(pe):
            pe.wait_ge(S.const_pool, N_CONST_POOL)
            pe.wait_ge(S.w_in, 16 * 10)
            pe.transpose(bank[0][:, 0:38], bias_rows[:, :], ident[0:38, 0:38]).then_inc(S.bias_tr, 1)
            for k, w in enumerate((wq, wk, wv)):
                m = pe.transpose(bank[1][:, k * P:(k + 1) * P], w[:, :], ident[:, :])
            m.then_inc(S.w_tr, 1)
            pe.wait_ge(S.w_trs, 2)
            pe.matmul(bank[2][:, 0:P], wT[:, 0, :], wT[:, 1, :], start=True, stop=True)
            pe.matmul(bank[2][:, P:2 * P], wT[:, 2, :], wo_m[:, :], start=True, stop=True).then_inc(S.wfold_mm, 1)
            pe.wait_ge(S.wfold, 1)
            pe.wait_ge(S.bias_set, 1)

            RT_, GT_, V_, S_, PT_, Y_, L_ = bank[0], bank[1], bank[2], bank[3:5], bank[5], bank[6], bank[7]
            R_ = L_

            def a_transpose(t, par):
                n = 2 * t + par
                if par == 0:
                    pe.wait_ge(S.xn_ready, t + 1)
                need(pe, S.xnT_ready, n)
                for j in range(2):
                    m = pe.transpose(RT_[:, j * P:(j + 1) * P], xn[:, 2 * par + j, :], ident[:, :])
                m.then_inc(S.xn_tr, 1)

            def a_project(t, par):
                n = 2 * t + par
                pe.wait_ge(S.xnT_ready, n + 1)
                need(pe, S.gT_ready, n)
                pe.matmul(GT_[:, 0:SEQ], m_qk[:, :], xnT[:, par, :], start=True, stop=True).then_inc(S.g_done, 1)
                need(pe, S.v_ready, n)
                for j in range(2):
                    m = pe.matmul(V_[:, j * P:(j + 1) * P], xnT[:, par, j * P:(j + 1) * P], m_vo[:, :], start=True, stop=True)
                m.then_inc(S.v_done, 1)

            def a_scores(t, par):
                n = 2 * t + par
                pe.wait_ge(S.gT_ready, n + 1)
                need(pe, S.probs_ready, n - 1)
                for q in range(2):
                    m = pe.matmul(S_[par][:, q * SEQ:(q + 1) * SEQ], gT[:, q * P:(q + 1) * P], xnT[:, par, :], start=True, stop=True)
                m.then_inc(S.scores_done, 1)

            def a_probs_transpose(t, par):
                n = 2 * t + par
                pe.wait_ge(S.probs_ready, n + 1)
                need(pe, S.pT_ready, n)
                for kt in range(2):
                    for q in range(2):
                        m = pe.transpose(PT_[:, kt * SEQ + q * P:kt * SEQ + (q + 1) * P], probs[:, par, q, kt * P:(kt + 1) * P], ident[:, :])
                m.then_inc(S.probs_tr, 1)

            def a_values(t, par):
                n = 2 * t + par
                pe.wait_ge(S.pT_ready, n + 1)
                pe.wait_ge(S.v_ready, n + 1)
                need(pe, S.attn_added, n)
                for q in range(2):
                    for kt in range(2):
                        m = pe.matmul(Y_[:, q * P:(q + 1) * P], pT[:, kt, q * P:(q + 1) * P], v_s[:, par, kt, :],
                                      start=(kt == 0), stop=(kt == 1))
                m.then_inc(S.y_done, 1)

            def r_transpose(n, bk=R_):
                pe.wait_ge(S.xn2_ready, n + 1)
                need(pe, S.log_ready, n)
                for j in range(4):
                    m = pe.transpose(bk[:, j * P:(j + 1) * P], xn2[:, j, :], ident[:, :])
                m.then_inc(S.xn2_tr, 1)

            def r_logits(n, i, bk=L_):
                pe.wait_ge(S.xn2T_ready, n + 1)
                pe.matmul(bk[0:E, 0:512], router[:, :], xnT_all[:, bass.ds(512 * i, 512)], start=True, stop=True).then_inc(S.logT_done, 1)

            def r_back(n, bk=R_):
                alone(pe, S.logT_ready, n + 1, S.const_pool)
                for j in range(4):
                    m = pe.transpose(bk[:, j * E:(j + 1) * E], logT[:, j * P:(j + 1) * P], ident[0:E, 0:E])
                m.then_inc(S.log_done, 1)

            def attn_a_pair(i):
                for h in range(2):
                    if valid(i):
                        a_probs_transpose(i, h)
                    if valid(shifted_seq(i, h, 1)[0]):
                        a_scores(*shifted_seq(i, h, 1))
                    if valid(i - 1) and h == 1:
                        r_logits(i - 1, i - 1)
                    if valid(shifted_seq(i, h, 2)[0]):
                        a_project(*shifted_seq(i, h, 2))
                    if valid(i):
                        a_values(i, h)
                    if valid(shifted_seq(i, h, 3)[0]):
                        a_transpose(*shifted_seq(i, h, 3))
                    if valid(i - 1):
                        if h == 0:
                            r_transpose(i - 1)
                        else:
                            r_back(i - 1)

            for i in range(-2, 1):
                attn_a_pair(i)
            with pe.Fori(1, PAIRS - 2) as i:
                attn_a_pair(i)
            for i in range(PAIRS - 2, PAIRS + 1):
                attn_a_pair(i)

            HB = bank[0:4]
            XT = bank[4:6]
            YB = bank[6:8]

            def sh_first(l, c, cb):
                for f in range(FT):
                    need(pe, S.sh1_ready, l * PAIRS * FT + 4 * c - FT + f + 1)
                    pe.matmul(HB[f][:, :], sw1_s[:, f * P:(f + 1) * P], xnT_all[:, bass.ds(512 * c, 512)],
                              start=True, stop=True).then_inc(S.sh1_done, 1)

            def sh_second(l, c, cb):
                pe.wait_ge(S.sh1_ready, l * PAIRS * FT + FT * c + FT)
                need(pe, S.sh2_ready, l * PAIRS + c - 1)
                for t in range(4):
                    for f in range(FT):
                        m = pe.matmul(YB[cb][:, t * P:(t + 1) * P], hsh[:, cb, f, t * P:(t + 1) * P], sw2_s[:, f, :],
                                      start=(f == 0), stop=(f == FT - 1))
                m.then_inc(S.sh2_done, 1)

            def shared_pair(l, i, first):
                for h in range(2):
                    c = 2 * i + h
                    sh_first(l, c, h)
                    if not (first and h == 0):
                        sh_second(l, c - 1, 1 - h)

            def counts(l):
                pe.wait_ge(S.masks_ready, l + 1)
                flat = MK[:, :, :, :].rearrange("p c e t -> p (c e t)")
                pe.matmul(XT[0][:, :], before[:, :], flat, start=True, stop=True)
                pe.matmul(XT[1][:, :], ones_bf[:, :], flat, start=True, stop=True).then_inc(S.count_done, 1)

            def index(l):
                pe.wait_ge(S.onehot_ready, l + 1)
                for n in range(2 * NT):
                    m = pe.matmul(XT[0][:, 0:2 * SLOT_TILES], OL[:, n, :], RH[:, n, :, :].rearrange("p a s -> p (a s)"),
                                  start=(n == 0), stop=(n == 2 * NT - 1))
                m.then_inc(S.index_done, 1)

            def x_tr(l, i, k):
                i, k = i + k // (2 * CHUNKS), k % (2 * CHUNKS)
                r = k % RING
                pe.wait_ge(gat[r], 32 * (l * E * CHUNKS // RING + 2 * i + k // RING + 1))
                n = l * E * CHUNKS + 2 * CHUNKS * i + k
                need(pe, S.xgT_ready, n - 1)
                for j in range(CH):
                    m = pe.transpose(XT[k % 2][:, j * P:(j + 1) * P], xg[:, r, j, :], ident[:, :])
                m.then_inc(S.xg_tr, 1)

            def first_mm(l, i, k):
                n = l * E * CHUNKS + 2 * CHUNKS * i + k
                h = k // CHUNKS
                if k % CHUNKS == 0:
                    pe.wait_ge((S.w1_in0, S.w1_in1)[h], 32 * (l * E // 2 + i + 1))
                pe.wait_ge(S.xgT_ready, n + 1)
                need(pe, S.h_ready, n - 1)
                for f in range(FT):
                    bk = HB[2 * (k % 2) + f // 2]
                    m = pe.matmul(bk[:, (f % 2) * 256:(f % 2) * 256 + 256], w1_s[h][:, f * P:(f + 1) * P], xgT[:, k % 2, :],
                                  start=True, stop=True)
                m.then_inc(S.h_done, 1)

            def second_mm(l, i, k):
                if k < 0:
                    i, k = i - 1, k + 2 * CHUNKS
                n = l * E * CHUNKS + 2 * CHUNKS * i + k
                h = k // CHUNKS
                pe.wait_ge(S.h_ready, n + 1)
                need(pe, S.yo_ready, n - 1)
                for j in range(CH):
                    for f in range(FT):
                        m = pe.matmul(YB[k % 2][:, j * P:(j + 1) * P], hT[:, k % 2, f, j * P:(j + 1) * P], w2_s[h][:, f, :],
                                      start=(f == 0), stop=(f == FT - 1))
                m.then_inc(S.yo_done, 1)

            def expert_pair(l, i, first, last):
                for k in range(2 * CHUNKS):
                    first_mm(l, i, k)
                    if not (last and k == 2 * CHUNKS - 1):
                        x_tr(l, i, k + 1)
                    if not (first and k == 0):
                        second_mm(l, i, k - 1)

            AB, CB, OB, MB, XB, ZB = bank[0:2], bank[2:4], bank[4], bank[5], bank[6], bank[7]

            def pass1(t, par, g, k):
                U = 2 * GRP * t + GRP * par + g
                if k == 0:
                    if g == 0:
                        pe.wait_ge((S.qc_in0, S.qc_in1)[par], 48 * t + 48)
                    pe.wait_ge(S.bd_done, U + 1)
                    pe.wait_ge(S.bd_act, U + 1)
                bk, qt = AB[(g + k) % 2], min(k, 1)
                need(pe, S.amax_done, 3 * U + k - 1)
                q = qc[0:96, par, g, qt * P:qt * P + P]
                if k == 0:
                    pe.matmul(bk[:, :], q, bdk[0:96, par, g, :, 0:P], start=True, stop=False)
                    m = pe.matmul(bk[:, :], ident_bf[:, :], cmask[:, :].unsqueeze(1).broadcast_to([P, 4, P]),
                                  start=False, stop=True)
                else:
                    pe.matmul(bk[:, :], q, bdk[0:96, par, g, 2 * k - 2:2 * k, :], start=True, stop=False)
                    m = pe.matmul(bk[:, :].rearrange("p (j k) -> p j k", j=2)[:, :, P:SEQ], ident_bf[:, :],
                                  cmask[:, :].unsqueeze(1).broadcast_to([P, 2, P]), start=False, stop=True)
                m.then_inc(S.a_done, 1)

            def neg_transpose(t, par, g):
                U = 2 * GRP * t + GRP * par + g
                pe.wait_ge(S.amax_done, 3 * U + 3)
                need(pe, S.neg_set, U)
                for qt in range(2):
                    m = pe.transpose(MB[:, qt * P:qt * P + P], negp[:, g % 2, qt, :], ident[:, :])
                m.then_inc(S.negT_done, 1)

            def pass2(t, par, g, k):
                U = 2 * GRP * t + GRP * par + g
                if k == 0:
                    pe.wait_ge(S.neg_set, U + 1)
                bk = CB[(g + k) % 2]
                need(pe, S.exp_done, 3 * U + k - 1)
                if k < 2:
                    for j in range(2):
                        m = pe.matmul(bk[:, j * SEQ:j * SEQ + SEQ], bdk[:, par, g, 2 * k + j, 0:P], qc[:, par, g, :],
                                      start=True, stop=True)
                else:
                    for j in range(4):
                        m = pe.matmul(bk[:, j * P:j * P + P], bdk[:, par, g, j, P:SEQ], qc[:, par, g, P:SEQ],
                                      start=True, stop=True)
                m.then_inc(S.c_done, 1)

            def values(t, par, g):
                n = 2 * t + par
                U = GRP * n + g
                pe.wait_ge(S.aff_done, U + 1)
                if g == 0:
                    pe.wait_ge(S.v_set, n + 1)
                if g % 2 == 0:
                    need(pe, S.ot_ready, 2 * n + g // 2)
                c0 = (g % 2) * SEQ
                for kt in range(2):
                    for j in range(4):
                        if kt == 0:
                            rhs = pt[:, g % 2, j // 2, (j % 2) * SEQ:(j % 2) * SEQ + SEQ]
                        else:
                            rhs = pt[:, g % 2, 2, j * P:j * P + P]
                        m = pe.matmul(OB[32 * j:32 * j + 32, c0 + kt * P:c0 + SEQ], v_ext[:, par, kt, 4 * g + j, :], rhs,
                                      start=(kt == 0), stop=(kt == 1))
                m.then_inc(S.pv_done, 1)

            def b_transpose(t, par):
                n = 2 * t + par
                pe.wait_ge(S.xn_ready, PAIRS + t + 1)
                need(pe, S.vb_ready, n)
                need(pe, S.on_ready, n - 3)
                for j in range(2):
                    m = pe.transpose(ZB[:, j * P:(j + 1) * P], xn[:, 2 * par + j, :], ident[:, :])
                m.then_inc(S.tb_done, 1)

            def b_project(t, par):
                n = 2 * t + par
                pe.wait_ge(S.tb_ready, n + 1)
                need(pe, S.onT_ready, n - 3)
                need(pe, S.qk32_ready, n)
                for c in range(2):
                    m = pe.matmul(XB[:, c * SEQ:(c + 1) * SEQ], w3[:, c, :, :].rearrange("p h d -> p (h d)"), xnT[:, par, :],
                                  start=True, stop=True)
                m.then_inc(S.qk_done, 1)
                for j in range(2):
                    m = pe.matmul(ZB[:, j * P:(j + 1) * P], xnT[:, par, j * P:(j + 1) * P],
                                  w3[:, 2, :, :].rearrange("p h d -> p (h d)"), start=True, stop=True)
                m.then_inc(S.vb_done, 1)

            def o_back(t, par):
                n = 2 * t + par
                pe.wait_ge(S.ot_ready, 2 * n + 2)
                need(pe, S.xb_added, n)
                for qt in range(2):
                    for g in range(GRP):
                        m = pe.transpose((XB, ZB)[qt][:, g * P:(g + 1) * P], oT[:, g, qt * P:(qt + 1) * P], ident[:, :])
                m.then_inc(S.otr_done, 1)

            def on_transpose(t, par):
                n = 2 * t + par
                pe.wait_ge(S.on_ready, n + 1)
                for qt in range(2):
                    m = pe.transpose(XB[:, qt * P:(qt + 1) * P], on[:, qt, :, :].rearrange("p h d -> p (h d)"), ident[:, :])
                m.then_inc(S.onT_done, 1)

            def out_project(t, par):
                n = 2 * t + par
                pe.wait_ge(S.onT_ready, n + 1)
                need(pe, S.qk32_ready, min(n + 5, SEQS) if isinstance(n, int) else n + 5)
                for qt in range(2):
                    m = pe.matmul(XB[:, qt * P:(qt + 1) * P], onT[:, qt * P:(qt + 1) * P], ow[:, :], start=True, stop=True)
                m.then_inc(S.pr_done, 1)

            def attn_b_pair(i):
                for h in range(2):
                    for g in range(GRP):
                        g1, g2, g3 = (shifted_group(i, h, g, -k) for k in (1, 2, 3))
                        if valid(i):
                            pass1(i, h, g, 0)
                        if valid(g1[0]):
                            neg_transpose(*g1)
                        if g == 3 and h == 1 and valid(i - 2):
                            r_back(PAIRS + i - 2, ZB)
                        if valid(i):
                            pass1(i, h, g, 1)
                        if valid(g2[0]):
                            pass2(*g2, 0)
                            pass2(*g2, 1)
                        if valid(i):
                            pass1(i, h, g, 2)
                        if valid(g3[0]):
                            values(*g3)
                        if valid(g2[0]):
                            pass2(*g2, 2)
                        if g == 0:
                            if valid(i - 1):
                                on_transpose(i - 1, h)
                            if valid(i + 1):
                                b_transpose(i + 1, h)
                        if g == 1 and valid(i + 1):
                            b_project(i + 1, h)
                        if g == 2:
                            if valid(i - 1):
                                out_project(i - 1, h)
                            if valid(i + 1):
                                pe.wait_ge(S.vb_ready, 2 * i + h + 3)
                            if valid(i - 2) and h == 0:
                                r_transpose(PAIRS + i - 2, ZB)
                            if valid(i - 2) and h == 1:
                                r_logits(PAIRS + i - 2, i - 2, ZB)
                        t, par, gg = shifted_group(i, h, g, -GRP)
                        if g == 3 and valid(t):
                            if valid(i - 2):
                                if h == 0:
                                    pe.wait_ge(S.xn2T_ready, PAIRS + i - 1)
                                else:
                                    pe.wait_ge(S.log_ready, PAIRS + i - 1)
                            o_back(t, par)

            for l in range(LAYERS):
                if l == 0:
                    pe.wait_ge(S.w_moe_in, 16 * 4)
                pe.wait_ge(S.log_ready, PAIRS * (l + 1))
                shared_pair(l, 0, True)
                counts(l)
                with pe.Fori(1, PAIRS // 2 - 1) as i:
                    shared_pair(l, i, False)
                index(l)
                shared_pair(l, PAIRS // 2 - 1, False)
                sh_second(l, PAIRS - 1, 1)
                pe.wait_ge(S.index_ready, l + 1)
                pe.wait_ge(S.sh2_ready, PAIRS * (l + 1))
                x_tr(l, 0, 0)
                expert_pair(l, 0, True, False)
                with pe.Fori(1, E // 2 - 1) as i:
                    expert_pair(l, i, False, False)
                expert_pair(l, E // 2 - 1, False, True)
                second_mm(l, E // 2 - 1, 2 * CHUNKS - 1)
                if l == 0:
                    pe.wait_ge(S.init_b, 7)
                    for i in range(-1, 2):
                        attn_b_pair(i)
                    with pe.Fori(2, PAIRS - 2) as i:
                        attn_b_pair(i)
                    for i in range(PAIRS - 2, PAIRS + 1):
                        attn_b_pair(i)
                    r_transpose(2 * PAIRS - 1, ZB)
                    r_logits(2 * PAIRS - 1, PAIRS - 1, ZB)
                    r_back(2 * PAIRS - 1, ZB)
        @block.scalar
        def _(act):
            for dst, src in ((wq, w_q), (wk, w_k), (wv, w_v), (wo, w_o), (router, router_w)):
                act.dma_start(dst[:, :], src).then_inc(S.w_in, 16)
            act.dma_start(mask_i[:, :], hd_mask.rearrange("(p a) -> p a", a=1)).then_inc(S.w_in, 16)
            act.dma_start(bias_rows[0:E * FT, :], b1.rearrange("e (f p) -> (e f) p", p=P)).then_inc(S.w_in, 16)
            act.dma_start(bias_rows[E * FT:E * FT + FT, :], sb1.rearrange("(f p) -> f p", p=P)).then_inc(S.w_in, 16)
            qkv_b = attn_b.rearrange("(h c d) -> c h d", c=3, d=8)
            act.dma_start(bias_rows[36:37, :], qkv_b[0:1].rearrange("c h d -> c h d")).then_inc(S.w_in, 16)
            act.dma_start(bias_rows[37:38, :], qkv_b[1:2].rearrange("c h d -> c h d")).then_inc(S.w_in, 16)
            act.wait_ge(S.w_tr, 1)
            act.activation(wT[:, :, :].rearrange("p a d -> p (a d)"), bank[1][:, 0:3 * P], ACT.Copy).then_inc(S.w_trs, 1)
            act.wait_ge(S.bias_tr, 1)
            act.activation(bias_T[:, :], bank[0][:, 0:38], ACT.Copy).then_inc(S.bias_set, 1)

            RT_, GT_, V_, S_, PT_, Y_, L_ = bank[0], bank[1], bank[2], bank[3:5], bank[5], bank[6], bank[7]
            R_ = L_

            def xnT_copy(t, par):
                n = 2 * t + par
                act.wait_ge(S.xn_tr, n + 1)
                need(act, S.scores_done, n - 1)
                act.activation(xnT[:, par, :], RT_[:, 0:SEQ], ACT.Copy).then_inc(S.xnT_ready, 1)

            def v_copy(t, par):
                n = 2 * t + par
                act.wait_ge(S.v_done, n + 1)
                need(act, S.y_done, n - 1)
                act.activation(v_s[:, par, :, :].rearrange("p a d -> p (a d)"), V_[:, 0:SEQ], ACT.Copy).then_inc(S.v_ready, 1)

            def exps(t, par):
                n = 2 * t + par
                act.wait_ge(S.max_ready, n + 1)
                need(act, S.probs_tr, n - 1)
                for q in range(2):
                    a = act.activation(probs[:, par, q, :], S_[par][:, q * SEQ:(q + 1) * SEQ], ACT.Exp,
                                       bias=negmax[:, par, q:q + 1], accum_out=psums[:, par, q:q + 1])
                a.then_inc(S.probs_ready, 1)

            def r_copy(n, i, bk=R_):
                act.wait_ge(S.xn2_tr, n + 1)
                act.activation(xnT_all[:, bass.ds(512 * i, 512)], bk[:, :], ACT.Copy).then_inc(S.xn2T_ready, 1)

            def logT_copy(n, bk=L_):
                act.wait_ge(S.logT_done, n + 1)
                need(act, S.log_done, n)
                act.activation(logT[:, :], bk[0:E, 0:512], ACT.Copy).then_inc(S.logT_ready, 1)

            def log_copy(n, i, bk=R_):
                act.wait_ge(S.log_done, n + 1)
                act.activation(logits[:, bass.ds(4 * i, 4), :].rearrange("p t e -> p (t e)"), bk[:, 0:4 * E], ACT.Copy).then_inc(S.log_ready, 1)

            def g_copy(t, par):
                n = 2 * t + par
                act.wait_ge(S.g_done, n + 1)
                need(act, S.scores_done, n)
                act.activation(gT[:, :], GT_[:, 0:SEQ], ACT.Copy).then_inc(S.gT_ready, 1)

            def p_copy(t, par):
                n = 2 * t + par
                act.wait_ge(S.probs_tr, n + 1)
                need(act, S.y_done, n)
                act.activation(pT[:, :, :].rearrange("p a k -> p (a k)"), PT_[:, :], ACT.Copy).then_inc(S.pT_ready, 1)

            def attn_a_pair(i):
                for h in range(2):
                    if valid(i):
                        p_copy(i, h)
                    if valid(shifted_seq(i, h, 2)[0]):
                        g_copy(*shifted_seq(i, h, 2))
                    if valid(i - 1) and h == 1:
                        logT_copy(i - 1)
                    if valid(shifted_seq(i, h, 1)[0]):
                        exps(*shifted_seq(i, h, 1))
                    if valid(shifted_seq(i, h, 2)[0]):
                        v_copy(*shifted_seq(i, h, 2))
                    if valid(shifted_seq(i, h, 3)[0]):
                        xnT_copy(*shifted_seq(i, h, 3))
                    if valid(i - 1):
                        if h == 0:
                            r_copy(i - 1, i - 1)
                        else:
                            log_copy(i - 1, i - 1)

            for i in range(-2, 1):
                attn_a_pair(i)
            with act.Fori(1, PAIRS - 2) as i:
                attn_a_pair(i)
            for i in range(PAIRS - 2, PAIRS + 1):
                attn_a_pair(i)

            HB, YB = bank[0:4], bank[6:8]

            def sh_silu(l, c, cb):
                need(act, S.sh2_done, l * PAIRS + c - 1)
                for f in range(FT):
                    act.wait_ge(S.sh1_done, l * PAIRS * FT + FT * c + f + 1)
                    act.activation(hsh[:, cb, f, :], HB[f][:, :], ACT.Silu,
                                   bias=bias_T[:, E * FT + f:E * FT + f + 1]).then_inc(S.sh1_ready, 1)

            def sh_out(l, c, cb):
                act.wait_ge(S.sh2_done, l * PAIRS + c + 1)
                act.activation(shared[:, bass.ds(4 * c, 4), :].rearrange("p t d -> p (t d)"), YB[cb][:, :], ACT.Copy,
                               scale=SHARED_SCALE).then_inc(S.sh2_ready, 1)

            def shared_pair(l, i, first):
                for h in range(2):
                    c = 2 * i + h
                    sh_silu(l, c, h)
                    if not (first and h == 0):
                        sh_out(l, c - 1, 1 - h)

            def silus(l, i, k):
                n = l * E * CHUNKS + 2 * CHUNKS * i + k
                h = k // CHUNKS
                if k % CHUNKS == 0:
                    e = 2 * i + h
                    act.activation(b1_cur[:, h, :], bias_T[:, bass.ds(FT * e, FT)], ACT.Copy).then_inc(S.b1_set, 1)
                    act.wait_ge(S.b1_set, l * E + e + 1)
                act.wait_ge(S.h_done, n + 1)
                need(act, S.yo_done, n - 1)
                for f in range(FT):
                    a = act.activation(hT[:, k % 2, f, :], HB[2 * (k % 2) + f // 2][:, (f % 2) * 256:(f % 2) * 256 + 256],
                                       ACT.Silu, bias=b1_cur[:, h, f:f + 1])
                a.then_inc(S.h_ready, 1)

            act.activation(bq_s[:, :], bias_T[:, 36:37], ACT.Copy, scale=HD ** -0.5)

            AB, CB, OB, MB, XB, ZB = bank[0:2], bank[2:4], bank[4], bank[5], bank[6], bank[7]

            def o_copy(t, par, half):
                n = 2 * t + par
                act.wait_ge(S.pv_done, GRP * n + 2 * half + 2)
                need(act, S.otr_done, n)
                act.activation(oT[:, 2 * half:2 * half + 2, :].rearrange("p g t -> p (g t)"), OB[:, :], ACT.Copy).then_inc(S.ot_ready, 1)

            def on_copy(t, par):
                n = 2 * t + par
                act.wait_ge(S.onT_done, n + 1)
                need(act, S.pr_done, n)
                act.activation(onT[:, :], XB[:, 0:SEQ], ACT.Copy).then_inc(S.onT_ready, 1)

            def bt_copy(t, par):
                n = 2 * t + par
                act.wait_ge(S.tb_done, n + 1)
                need(act, S.vb_done, n - 1)
                act.activation(xnT[:, par, :], ZB[:, 0:SEQ], ACT.Copy).then_inc(S.tb_ready, 1)

            def qk_bias(t, par):
                n = 2 * t + par
                act.wait_ge(S.qk_done, n + 1)
                need(act, S.hilo_done, n)
                act.activation(qk32[:, 0, :], XB[:, 0:SEQ], ACT.Identity, bias=bq_s[:, 0:1], scale=HD ** -0.5)
                act.activation(qk32[:, 1, :], XB[:, SEQ:2 * SEQ], ACT.Identity, bias=bias_T[:, 37:38]).then_inc(S.qk32_ready, 1)

            def block_diag(t, par, g):
                U = 2 * GRP * t + GRP * par + g
                if g == 0:
                    act.wait_ge((S.kc_in0, S.kc_in1)[par], 48 * t + 48)
                need(act, S.c_done, 3 * (U - 2 * GRP) + 3)
                for j in range(2, 4):
                    a = act.activation(bdk[:, par, g, j, :], kc[:, par, g, :].bitcast(F32), ACT.Copy, scale=head_m[:, j:j + 1])
                a.then_inc(S.bd_act, 1)

            def neg_copy(t, par, g):
                U = 2 * GRP * t + GRP * par + g
                act.wait_ge(S.negT_done, U + 1)
                act.activation(qc[96:P, par, g, :], MB[96:P, 0:SEQ], ACT.Copy).then_inc(S.neg_set, 1)

            def exps_b(t, par, g):
                U = 2 * GRP * t + GRP * par + g
                need(act, S.pv_done, U - 1)
                for k in range(3):
                    act.wait_ge(S.c_done, 3 * U + k + 1)
                    act.activation(pt[:, g % 2, k, :], CB[(g + k) % 2][:, :], ACT.Exp).then_inc(S.exp_done, 1)

            def attn_b_pair(i):
                for h in range(2):
                    for g in range(GRP):
                        t, par, gg = shifted_group(i, h, g, -GRP)
                        if g % 2 == 1 and valid(t):
                            o_copy(t, par, g // 2)
                        if g == 1:
                            if valid(i - 1):
                                on_copy(i - 1, h)
                            if valid(i + 1):
                                bt_copy(i + 1, h)
                        if g == 2 and valid(i + 1):
                            qk_bias(i + 1, h)
                        if g == 3 and valid(i - 2):
                            if h == 0:
                                r_copy(PAIRS + i - 2, i - 2, ZB)
                            else:
                                logT_copy(PAIRS + i - 2, ZB)
                        t, par, gg = shifted_group(i, h, g, -1)
                        if valid(t):
                            neg_copy(t, par, gg)
                        if g == 3 and h == 1 and valid(i - 2):
                            log_copy(PAIRS + i - 2, i - 2, ZB)
                        t, par, gg = shifted_group(i, h, g, 2)
                        if valid(t):
                            block_diag(t, par, gg)
                        t, par, gg = shifted_group(i, h, g, -2)
                        if valid(t):
                            exps_b(t, par, gg)

            for l in range(LAYERS):
                act.wait_ge(S.y_zeroed, 32)
                act.wait_ge(S.shifted, l + 1)
                act.activation(G[:, :, :], G[:, :, :], ACT.Exp).then_inc(S.exped, 1)
                shared_pair(l, 0, True)
                with act.Fori(1, PAIRS // 2) as i:
                    shared_pair(l, i, False)
                sh_out(l, PAIRS - 1, 1)
                for k in range(2 * CHUNKS):
                    silus(l, 0, k)
                with act.Fori(1, E // 2) as i:
                    for k in range(2 * CHUNKS):
                        silus(l, i, k)
                if l == 0:
                    act.wait_ge(S.init_b, 7)
                    for i in range(-1, 2):
                        attn_b_pair(i)
                    with act.Fori(2, PAIRS - 2) as i:
                        attn_b_pair(i)
                    for i in range(PAIRS - 2, PAIRS + 1):
                        attn_b_pair(i)
                    r_copy(2 * PAIRS - 1, PAIRS - 1, ZB)
                    logT_copy(2 * PAIRS - 1, ZB)
                    log_copy(2 * PAIRS - 1, PAIRS - 1, ZB)

        @block.vector
        def _(dve):
            dve.wait_ge(S.w_in, 16 * 10)
            dve.tensor_copy(mask_f[:, :], mask_i[:, :]).then_inc(S.const_dve, 1)
            dve.wait_ge(S.const_dve, 1)
            dve.tensor_scalar(wo_m[:, :], wo[:, :], mask_f[:, 0:1], None, ALU.mult).then_inc(S.w_trs, 1)
            dve.wait_ge(S.wfold_mm, 1)
            dve.tensor_scalar(m_qk[:, :], bank[2][:, 0:P], float(D) ** -0.5, None, ALU.mult)
            dve.tensor_copy(m_vo[:, :], bank[2][:, P:2 * P]).then_inc(S.wfold, 1)

            GT_, S_, PT_, Y_ = bank[1], bank[3:5], bank[5], bank[6]

            def stats(i, n, st_, mv_, s_st, s_mv):
                for j in range(4):
                    a = dve.bn_stats(st_[:, j, :], x[:, bass.ds(4 * i + j, 1), :].rearrange("p a d -> p (a d)"))
                a.then_inc(s_st, 1)
                alone(dve, s_st, n, S.const_dve)
                for j in range(4):
                    a = dve.bn_aggr(mv_[:, j, :], st_[:, j, :])
                a.then_inc(s_mv, 1)

            def norm(i, n, dst, mv_, rstd_, s_rstd, s_out):
                dve.wait_ge(s_rstd, n)
                for j in range(4):
                    a = dve.tensor_scalar(dst[:, j, :], x[:, bass.ds(4 * i + j, 1), :].rearrange("p a d -> p (a d)"),
                                          mv_[:, j, 0:1], rstd_[:, j:j + 1], ALU.subtract, ALU.mult)
                a.then_inc(s_out, 1)

            def norm_a(i):
                need(dve, S.xn_tr, 2 * i)
                norm(i, i + 1, xn, mv, rstd, S.ln_rstd, S.xn_ready)

            def norm_r(n, i):
                need(dve, S.xn2_tr, n)
                need(dve, S.xn2_stored, 16 * n)
                norm(i, n + 1, xn2, mv2, rstd2, S.ln2_rstd, S.xn2_ready)

            def maxes(t, par):
                n = 2 * t + par
                dve.wait_ge(S.scores_done, n + 1)
                dve.tensor_reduce(negmax[:, par, :], S_[par][:, :].rearrange("p (q k) -> p q k", q=2), AX.X, ALU.max,
                                  negate=True).then_inc(S.max_ready, 1)

            def inverse_sums(t, par):
                n = 2 * t + par
                dve.wait_ge(S.probs_ready, n + 1)
                dve.reciprocal(rsum[:, par, :], psums[:, par, :]).then_inc(S.rsum_ready, 1)

            def add_attn(t, par):
                n = 2 * t + par
                dve.wait_ge(S.y_done, n + 1)
                dve.wait_ge(S.rsum_ready, n + 1)
                for q in range(2):
                    xs = x[:, bass.ds(4 * t + 2 * par + q, 1), :].rearrange("p a d -> p (a d)")
                    a = dve.scalar_tensor_tensor(out=xs, in0=Y_[:, q * P:(q + 1) * P], scalar=rsum[:, par, q:q + 1], in1=xs,
                                                 op0=ALU.mult, op1=ALU.add)
                a.then_inc(S.attn_added, 1)

            def attn_a_pair(i):
                for h in range(2):
                    if valid(i):
                        inverse_sums(i, h)
                    if valid(shifted_seq(i, h, 1)[0]):
                        maxes(*shifted_seq(i, h, 1))
                    if valid(i - 1) and h == 0:
                        norm_r(i - 1, i - 1)
                    if valid(i + 2) and h == 1:
                        need(dve, S.xn_tr, 2 * i + 4)
                        norm(i + 2, i + 3, xn, mv, rstd, S.ln_rstd, S.xn_ready)
                    if valid(i):
                        add_attn(i, h)
                    if valid(i + 2) and h == 0:
                        if isinstance(i, int) and i <= 0:
                            dve.wait_ge(S.x_head if i == -2 else S.x_tail, 16)
                        stats(i + 2, i + 3, st, mv, S.ln_stats, S.ln_mv)
                    if valid(i) and h == 1:
                        alone(dve, S.attn_added, 2 * i + 2, S.const_dve)
                        stats(i, i + 1, st2, mv2, S.ln2_stats, S.ln2_mv)

            for i in range(-2, 1):
                attn_a_pair(i)
            with dve.Fori(1, PAIRS - 2) as i:
                attn_a_pair(i)
            for i in range(PAIRS - 2, PAIRS + 1):
                attn_a_pair(i)

            steps = [0]

            def step(ins, wait=True):
                steps[0] += 1
                ins.then_inc(S.route, 1)
                if wait:
                    dve.wait_ge(S.route, steps[0])

            def over_e(a):
                return a.unsqueeze(2).broadcast_to([P, NT, E])

            def routing(l):
                XT = bank[4:6]
                dve.wait_ge(S.log_ready, PAIRS * (l + 1))
                if l == 0:
                    dve.wait_ge(S.const_pool, N_CONST_POOL)
                    dve.wait_ge(S.w_moe_in, 16 * 4)
                step(dve.tensor_reduce(r1[:, :], logits[:, :, :], AX.X, ALU.max))
                dve.tensor_tensor(G[:, :, :], logits[:, :, :], over_e(r1[:, :]), ALU.subtract).then_inc(S.shifted, 1)
                dve.wait_ge(S.exped, l + 1)
                step(dve.tensor_reduce(r1[:, :], G[:, :, :], AX.X, ALU.add))
                step(dve.reciprocal(r2[:, :], r1[:, :]))
                step(dve.tensor_tensor(G[:, :, :], G[:, :, :], over_e(r2[:, :]), ALU.mult))
                rev_b = rev[:, :].unsqueeze(1).broadcast_to([P, NT, E])
                for c, g in enumerate((G, G1)):
                    step(dve.tensor_reduce(r1[:, :], g[:, :, :], AX.X, ALU.max))
                    step(dve.tensor_tensor(t1[:, :, :], g[:, :, :], over_e(r1[:, :]), ALU.is_equal))
                    step(dve.tensor_tensor(t1[:, :, :], t1[:, :, :], rev_b, ALU.mult))
                    step(dve.tensor_reduce(r2[:, :], t1[:, :, :], AX.X, ALU.max))
                    step(dve.tensor_tensor(m1[:, :, :], t1[:, :, :], over_e(r2[:, :]), ALU.is_equal))
                    a = dve.tensor_copy(MK[:, c, :, :].rearrange("p e t -> p t e"), m1[:, :, :])
                    if c == 0:
                        step(dve.tensor_tensor(t1[:, :, :], G[:, :, :], m1[:, :, :], ALU.mult))
                        step(dve.tensor_tensor(G1[:, :, :], G[:, :, :], t1[:, :, :], ALU.subtract))
                a.then_inc(S.masks_ready, 1)
                dve.wait_ge(S.masks_ready, l + 1)
                flat = lambda a: a[:, :, :, :].rearrange("p c e t -> p (c e t)")
                dve.wait_ge(S.count_done, l + 1)
                step(dve.tensor_tensor_scan(flat(INC), carry[:, :], XT[1][:, :], 0.0, ALU.mult, ALU.add))
                step(dve.tensor_tensor(flat(POS), flat(INC), XT[0][:, :], ALU.add), False)
                step(dve.tensor_scalar(keep1[:, :], INC[:, 0, :, NT - 1], float(CAP), None, ALU.min))
                step(dve.tensor_tensor(flat(POS), flat(POS), XT[1][:, :], ALU.subtract))
                step(dve.tensor_tensor(POS[:, 1, :, :], POS[:, 1, :, :], keep1[:, :].unsqueeze(2).broadcast_to([P, E, NT]), ALU.add))
                step(dve.scalar_tensor_tensor(out=flat(KM), in0=flat(POS), scalar=float(CAP), in1=flat(MK), op0=ALU.is_lt, op1=ALU.mult))
                for c in range(2):
                    step(dve.tensor_tensor(POS[:, c, :, :], POS[:, c, :, :], slot_base[:, :, :], ALU.add), c == 1)
                step(dve.tensor_tensor(flat(POS), flat(POS), flat(KM), ALU.mult), False)
                for c in range(2):
                    step(dve.tensor_tensor(GK[:, c, :, :], KM[:, c, :, :], G[:, :, :].rearrange("p t e -> p e t"), ALU.mult), c == 1)
                for c in range(2):
                    step(dve.tensor_reduce(slot[:, c, :], POS[:, c, :, :].rearrange("p e t -> p t e"), AX.X, ALU.add), False)
                    step(dve.tensor_reduce(fill[:, c, :], KM[:, c, :, :].rearrange("p e t -> p t e"), AX.X, ALU.add), c == 1)
                step(dve.tensor_copy(slot_i[:, :, :], slot[:, :, :]))
                if l == 0:
                    dve.tensor_copy(slot_u[:, :, :], slot[:, :, :])
                step(dve.tensor_scalar(hi_i[:, :, :], slot_i[:, :, :], 7, None, ALU.logical_shift_right), False)
                step(dve.tensor_scalar(lo_i[:, :, :], slot_i[:, :, :], 127, None, ALU.bitwise_and), False)
                step(dve.tensor_scalar(fill[:, :, :], fill[:, :, :], -float(P), float(P), ALU.mult, ALU.add))
                step(dve.tensor_copy(hi_f[:, :, :], hi_i[:, :, :]), False)
                step(dve.tensor_copy(lo_b[:, :], lo_i[:, :, :].rearrange("p c t -> p (c t)")))
                step(dve.tensor_tensor(hi_b[:, :], hi_f[:, :, :].rearrange("p c t -> p (c t)"),
                                       fill[:, :, :].rearrange("p c t -> p (c t)"), ALU.add))
                n2 = 2 * NT
                step(dve.tensor_tensor(OL[:, :, :], iota_lo[:, :].unsqueeze(1).broadcast_to([P, n2, P]),
                                       lo_b[:, :].unsqueeze(2).broadcast_to([P, n2, P]), ALU.is_equal), False)
                step(dve.tensor_tensor(OH[:, :, :], iota_hi[:, :].unsqueeze(1).broadcast_to([P, n2, SLOT_TILES]),
                                       hi_b[:, :].unsqueeze(2).broadcast_to([P, n2, SLOT_TILES]), ALU.is_equal))
                dve.tensor_scalar(RH[:, :, 0, :], OH[:, :, :], part1[:, 0:1], None, ALU.mult)
                dve.tensor_tensor(RH[:, :, 1, :], OH[:, :, :], tile_code[:, :].unsqueeze(2).broadcast_to([P, n2, SLOT_TILES]),
                                  ALU.mult).then_inc(S.onehot_ready, 1)
                for c in range(2):
                    step(dve.tensor_reduce(gate[:, c, :], GK[:, c, :, :].rearrange("p e t -> p t e"), AX.X, ALU.add), c == 1)
                step(dve.tensor_tensor(den[:, :], gate[:, 0, :], gate[:, 1, :], ALU.add))
                step(dve.tensor_scalar(den[:, :], den[:, :], TINY, None, ALU.max))
                step(dve.reciprocal(r1[:, :], den[:, :]))
                step(dve.tensor_tensor(gate[:, :, :], gate[:, :, :], r1[:, :].unsqueeze(1).broadcast_to([P, 2, NT]), ALU.mult))
                dve.wait_ge(S.index_done, l + 1)
                a_, b_ = XT[0][:, 0:SLOT_TILES], XT[0][:, SLOT_TILES:2 * SLOT_TILES]
                step(dve.tensor_scalar(row_f[:, :], b_, float(P), -1.0, ALU.mult, ALU.add))
                step(dve.tensor_tensor(row_f[:, :], a_, row_f[:, :], ALU.add))
                step(dve.tensor_scalar(row_e[:, :], b_, float(NT), -float(T), ALU.is_ge, ALU.mult))
                step(dve.tensor_tensor(row_e[:, :], row_e[:, :], row_f[:, :], ALU.add))
                step(dve.tensor_scalar(tok_idx[:, :], row_e[:, :], 0.0, None, ALU.max))
                step(dve.tensor_scalar(row_e[:, :], a_, 0.0, 4.0 * T, ALU.is_equal, ALU.mult))
                dve.tensor_tensor(row_idx[:, :], row_e[:, :], row_f[:, :], ALU.add).then_inc(S.index_ready, 1)

            def add_shared(l, i, k):
                if k % 2 == 0 or k > 7:
                    return
                h, n = k // 4, 2 * PAIRS * l + 4 * i + k // 2
                xs = x[:, bass.ds(8 * i + 4 * h, 4), :]
                if k % 4 == 1:
                    dve.wait_ge(S.sh2_ready, PAIRS * l + 2 * i + h + 1)
                    dve.tensor_tensor(xs, xs, shared[:, bass.ds(8 * i + 4 * h, 4), :], ALU.add).then_inc(S.shared_added, 1)
                else:
                    dve.wait_ge(S.shared_added, n)
                    dve.scalar_tensor_tensor(out=xs, in0=sb2_b[:, :].unsqueeze(1).broadcast_to([P, 4, D]),
                                             scalar=SHARED_SCALE, in1=xs, op0=ALU.mult, op1=ALU.add).then_inc(S.shared_added, 1)

            def xg_copy(l, i, k):
                i, k = i + k // (2 * CHUNKS), k % (2 * CHUNKS)
                n = l * E * CHUNKS + 2 * CHUNKS * i + k
                dve.wait_ge(S.xg_tr, n + 1)
                need(dve, S.h_done, n - 1)
                dve.tensor_copy(xgT[:, k % 2, :], bank[4 + k % 2][:, 0:CH * P]).then_inc(S.xgT_ready, 1)

            def y_copy(l, i, k):
                if k < 0:
                    i, k = i - 1, k + 2 * CHUNKS
                n = l * E * CHUNKS + 2 * CHUNKS * i + k
                r, ex = k % RING, 2 * i + k // CHUNKS
                dve.wait_ge(S.yo_done, n + 1)
                need(dve, (sto, sca)[l][r], 32 * (2 * i + k // RING))
                dve.tensor_tensor(yo[:, r, :, :], bank[6 + k % 2][:, 0:CH * P].rearrange("p (a d) -> p a d", a=CH),
                                  b2_b[:, bass.ds(ex, 1), :].broadcast_to([P, CH, D]), ALU.add).then_inc(S.yo_ready, 1)

            def expert_pair(l, i, first, last):
                for k in range(2 * CHUNKS):
                    if not (last and k == 2 * CHUNKS - 1):
                        xg_copy(l, i, k + 1)
                    if not (first and k == 0):
                        y_copy(l, i, k - 1)
                    add_shared(l, i, k)

            def combine(l, pair, c):
                if l == 0:
                    dve.wait_ge(y_in[c], 64 * (pair + 1))
                if c == 1:
                    dve.wait_ge(S.comb, l * PAIRS + pair + 1)
                for j in range(4):
                    t = 4 * pair + j
                    xs = x[:, bass.ds(t, 1), :].rearrange("p a d -> p (a d)")
                    row = yab[:, c, j, :] if l == 0 else y_all[:, c, t, :]
                    a = dve.scalar_tensor_tensor(out=xs, in0=row, scalar=gate[:, c, bass.ds(t, 1)],
                                                 in1=xs, op0=ALU.mult, op1=ALU.add)
                a.then_inc((S.comb, S.y_used)[c], 1)

            AB, CB, OB, MB, XB, ZB = bank[0:2], bank[2:4], bank[4], bank[5], bank[6], bank[7]

            def max_b(t, par, g, k):
                U = 2 * GRP * t + GRP * par + g
                if k == 0:
                    need(dve, S.negT_done, U - 1)
                dve.wait_ge(S.a_done, 3 * U + k + 1)
                heads, first = (4, 0) if k == 0 else (2, 2 * k - 2)
                dst = negp[:, g % 2, min(k, 1), 96:P].rearrange("p (j r) -> p j r", r=8)[:, first:first + heads, 0]
                dve.tensor_reduce(dst, AB[(g + k) % 2][:, :].rearrange("p (j k) -> p j k", j=heads), AX.X, ALU.max,
                                  negate=True).then_inc(S.amax_done, 1)

            def split(t, par):
                n = 2 * t + par
                dve.wait_ge(S.qk32_ready, n + 1)
                need(dve, (S.qks_stored0, S.qks_stored1)[par], 16 * t)
                dve.tensor_copy(qks[:, par, 0, :, :], qk32[:, :, :]).then_inc(S.hilo_hi, 1)
                dve.wait_ge(S.hilo_hi, n + 1)
                dve.tensor_tensor(qks[:, par, 1, :, :], qk32[:, :, :], qks[:, par, 0, :, :].bitcast(F32),
                                  ALU.subtract).then_inc(S.hilo_done, 1)

            def v_bias(t, par):
                n = 2 * t + par
                dve.wait_ge(S.vb_done, n + 1)
                need(dve, S.v_set, n - 1)
                dve.tensor_tensor(v_s[:, par, :, :], ZB[:, 0:SEQ].rearrange("p (k d) -> p k d", k=2),
                                  bv_b[:, :, :].rearrange("p h d -> p (h d)").unsqueeze(1).broadcast_to([P, 2, D]),
                                  ALU.add).then_inc(S.vb_ready, 1)

            def divide(t, par):
                n = 2 * t + par
                dve.wait_ge(S.otr_done, n + 1)
                need(dve, S.onT_done, n)
                o = [bk[:, :].rearrange("p (h r) -> p h r", r=32) for bk in (XB, ZB)]
                for qt in range(2):
                    a = dve.reciprocal(osum[:, qt, :], o[qt][:, :, HD])
                a.then_inc(S.osum_ready, 1)
                dve.wait_ge(S.osum_ready, n + 1)
                for qt in range(2):
                    a = dve.tensor_tensor(on[:, qt, :, :], o[qt][:, :, 0:HD],
                                          osum[:, qt, :].unsqueeze(2).broadcast_to([P, HEADS, HD]), ALU.mult)
                a.then_inc(S.on_ready, 1)

            def add_out(t, par):
                n = 2 * t + par
                dve.wait_ge(S.pr_done, n + 1)
                dve.wait_ge(S.ob_added, t + 1)
                xs = x[:, bass.ds(4 * t + 2 * par, 2), :]
                dve.tensor_tensor(xs, xs, XB[:, 0:SEQ].rearrange("p (k d) -> p k d", k=2), ALU.add).then_inc(S.xb_added, 1)

            def stats_b(i):
                alone(dve, S.y_used, i + 1, S.const_dve)
                stats(i, PAIRS + i + 1, st, mv, S.ln_stats, S.ln_mv)

            def norm_b(i):
                need(dve, S.tb_done, 2 * i)
                norm(i, PAIRS + i + 1, xn, mv, rstd, S.ln_rstd, S.xn_ready)

            def attn_b_pair(i):
                for h in range(2):
                    for g in range(GRP):
                        if valid(i):
                            max_b(i, h, g, 0)
                        if g == 0 and valid(i - 1):
                            divide(i - 1, h)
                        if g == 3 and valid(i - 1):
                            add_out(i - 1, h)
                        if valid(i):
                            max_b(i, h, g, 1)
                            max_b(i, h, g, 2)
                        if g == 1:
                            if h == 0 and valid(i - 2):
                                norm_r(PAIRS + i - 2, i - 2)
                            if valid(i + 2):
                                combine(0, i + 2, h)
                                if h == 1:
                                    stats_b(i + 2)
                        if g == 2 and valid(i + 1):
                            split(i + 1, h)
                            v_bias(i + 1, h)
                        if g == 2 and h == 1 and valid(i + 2):
                            norm_b(i + 2)
                        if g == 3 and h == 1 and valid(i - 1):
                            alone(dve, S.xb_added, 2 * i, S.const_dve)
                            stats(i - 1, PAIRS + i, st2, mv2, S.ln2_stats, S.ln2_mv)

            for l in range(LAYERS):
                routing(l)
                xg_copy(l, 0, 0)
                expert_pair(l, 0, True, False)
                with dve.Fori(1, E // 2 - 1) as i:
                    expert_pair(l, i, False, False)
                expert_pair(l, E // 2 - 1, False, True)
                y_copy(l, E // 2 - 1, 2 * CHUNKS - 1)
                if l == 0:
                    dve.wait_ge(S.wb_in, 16 * 4)
                    dve.wait_ge(S.init_b, 7)
                    dve.wait_ge(S.shared_added, 2 * PAIRS)
                    combine(0, 0, 0)
                    combine(0, 0, 1)
                    stats_b(0)
                    norm_b(0)
                    for i in range(-1, 2):
                        attn_b_pair(i)
                    with dve.Fori(2, PAIRS - 2) as i:
                        attn_b_pair(i)
                    for i in range(PAIRS - 2, PAIRS + 1):
                        attn_b_pair(i)
                    norm_r(2 * PAIRS - 1, PAIRS - 1)
            for i in range(PAIRS):
                if i % 2 == 0:
                    dve.wait_ge(y_back[i // 2], 32)
                combine(1, i, 0)
                combine(1, i, 1)



_INS = ['L0_attn_a_x', 'L0_attn_a_head_dim_mask', 'L0_attn_a_w_q', 'L0_attn_a_w_k', 'L0_attn_a_w_v', 'L0_attn_a_w_o',
        'L0_attn_b_attn_W', 'L0_attn_b_attn_b', 'L0_attn_b_out_W', 'L0_attn_b_out_b', 'L0_ffn_router_w', 'L0_ffn_w1',
        'L0_ffn_b1', 'L0_ffn_w2', 'L0_ffn_b2', 'L0_ffn_sw1', 'L0_ffn_sb1', 'L0_ffn_sw2', 'L0_ffn_sb2']


def kernel(**inputs):
    import numpy as np
    import concourse.bacc as bacc
    from concourse.bass_utils import run_bass_kernel_spmd

    nc = bacc.Bacc("TRN2", target_bir_lowering=False, num_devices=1)
    arrays, args = {}, []
    for name in _INS:
        a = np.ascontiguousarray(inputs[name])
        arrays[f"in_{name}"] = a
        args.append(nc.dram_tensor(f"in_{name}", a.shape, mybir.dt.from_np(a.dtype), kind="ExternalInput").ap())
    out = nc.dram_tensor("out_x", (SEQS, SEQ, D), F32, kind="ExternalOutput").ap()
    build(nc, *args, out)
    r = run_bass_kernel_spmd(nc, [arrays], core_ids=[0])
    return r.results[0]["out_x"]
```

```python
import math
from contextlib import ExitStack

import concourse.bass as bass
from concourse import mybir

ALU = mybir.AluOpType
ACT = mybir.ActivationFunctionType
AX = mybir.AxisListType
F32 = mybir.dt.float32
BF16 = mybir.dt.bfloat16
F32R = mybir.dt.float32r
I32 = mybir.dt.int32
U32 = mybir.dt.uint32

P = 128
SEQS, SEQ, D = 16, 256, 128
T = SEQS * SEQ
NT = T // P
PAIRS = SEQS // 2
E, F = 8, 512
FT = F // P
CAP = min(max(4, math.ceil(2 * 1.25 * T / E)), T)
ST = CAP // P
CH = 2
CHUNKS = ST // CH
SHC = 4
SHW = (T - SHC * 512) // 256
WORK = [[0, 1, 2, 3, 4, 5, 6, 7, 8, 9], [None, 0, 1, 2, 3, 4, None, 5, 6, 7, 8, 9]]
FIRST = [None, None, 0, 1, 2, 3, 4, 5, 6, 7, 8, 9]
AFTER = SHW - 2
PIECES = E // 2
LAYER_WORK = E * CHUNKS + SHW
SLOT_TILES = E * ST
RING = 5
EPS = 1e-5
TINY = 1.1920928955078125e-07
MASKED = -1e30
SHARED_SCALE = 0.1
HEADS, HD = 16, 8
GRP = HEADS // 4
LAYERS = 2


def need(eng, sem, value):
    if not isinstance(value, int) or value > 0:
        eng.wait_ge(sem, value)


def alone(eng, sem, value, set_already):
    if not isinstance(value, int):
        value = eng.to_reg(value)
        eng.wait_ge(set_already, 1)
    need(eng, sem, value)


def order(l, i):
    return FIRST if isinstance(i, int) and i == 0 else WORK[l]


def work(l, i, v):
    after = isinstance(i, int) and i == PIECES
    before = 0 if isinstance(i, int) and i == 0 else len(FIRST) - len(WORK[l])
    return LAYER_WORK * l + len(WORK[l]) * i + before + v, None if after else order(l, i)[v]


def work_of(l, i, k):
    return work(l, i, order(l, i).index(k))[0]


def before_reuse(l, i, h):
    if isinstance(i, int) and i == 0:
        l, i = l - 1, E // 2
        if l < 0:
            return 0
    return work_of(l, i - 1, h * CHUNKS + CHUNKS - 1) + (2 if l == 1 and h == 0 else 1)


def piece_start(l, i, v):
    if isinstance(i, int) and i == PIECES:
        return SHC * 512 + 256 * (SHW - AFTER + v)
    return SHC * 512 + 512 * i + 256 * order(l, i)[:v].count(None)


def valid(pair):
    return not isinstance(pair, int) or 0 <= pair < PAIRS


def shifted_group(i, h, g, by):
    q = GRP * h + g + by
    return i + q // (2 * GRP), q // GRP % 2, q % GRP


def shifted_seq(i, h, by):
    return i + (h + by) // 2, (h + by) % 2


class Signals:
    pass


def build(nc, x_in, hd_mask, w_q, w_k, w_v, w_o, attn_W, attn_b, out_W, out_b, router_w,
          w1, b1, w2, b2, sw1, sb1, sw2, sb2, out):
    with ExitStack() as ctx:
        def sb(name, shape, dt=F32):
            return ctx.enter_context(nc.sbuf_tensor(name, shape, dt))

        def sem(name):
            return ctx.enter_context(nc.semaphore(name))

        xn_rows = nc.dram_tensor("xn_rows", [T, D], F32).ap()
        y_rows = nc.dram_tensor("y_rows", [2 * T, D], F32).ap()
        y_slots = nc.dram_tensor("y_slots", [E * CAP, D], F32).ap()

        qk_rows = nc.dram_tensor("qk_rows", [2, P, 2, 2, SEQ], F32).ap()

        bank = [ctx.enter_context(nc.psum_tensor(f"bank{k}", [P, 512], F32)) for k in range(8)]

        ident = sb("ident", [P, P])
        ident_bf = sb("ident_bf", [P, P], BF16)
        before = sb("before", [P, P], BF16)
        ones_bf = sb("ones_bf", [P, P], BF16)
        iota_lo = sb("iota_lo", [P, P], BF16)
        iota_hi = sb("iota_hi", [P, SLOT_TILES], BF16)
        part1 = sb("part1", [P, 1])
        rev = sb("rev", [P, E])
        slot_base = sb("slot_base", [P, E, NT])
        tile_code = sb("tile_code", [P, 2 * NT], BF16)
        carry = sb("carry", [P, 2 * E * NT])
        neg_half = sb("neg_half", [P, 4])

        wq = sb("wq", [P, D]); wk = sb("wk", [P, D]); wv = sb("wv", [P, D]); wo = sb("wo", [P, D])
        mask_i = sb("mask_i", [P, 1], I32); mask_f = sb("mask_f", [P, 1])
        wT = sb("wT", [P, 3, D])
        wo_m = sb("wo_m", [P, D])
        m_qk = sb("m_qk", [P, D])
        m_vo = sb("m_vo", [P, D])
        router = sb("router", [P, E])
        sw1_s = sb("sw1_s", [P, F]); sw2_s = sb("sw2_s", [P, FT, D])
        bias_rows = sb("bias_rows", [38, P]); bias_T = sb("bias_T", [P, 38])
        b2_b = sb("b2_b", [P, E, D]); sb2_b = sb("sb2_b", [P, D])

        x = sb("x", [P, NT, D])
        xnT_all = sb("xnT_all", [P, T])
        logits = sb("logits", [P, NT, E])
        gate = sb("gate", [P, 2, NT])

        st = sb("st", [P, 4, 6]); mv = sb("mv", [P, 4, 2]); ve = sb("ve", [P, 4]); rstd = sb("rstd", [P, 4])
        st2 = sb("st2", [P, 4, 6]); mv2 = sb("mv2", [P, 4, 2]); ve2 = sb("ve2", [P, 4]); rstd2 = sb("rstd2", [P, 4])
        xn = sb("xn", [P, 4, D])
        xn2 = sb("xn2", [P, 4, D])
        logT = sb("logT", [E, 512])

        xnT = sb("xnT", [P, 2, SEQ]); v_s = sb("v_s", [P, 2, 2, D])
        negmax = sb("negmax", [P, 2, 2]); psums = sb("psums", [P, 2, 2]); rsum = sb("rsum", [P, 2, 2])

        r1 = sb("r1", [P, NT]); r2 = sb("r2", [P, NT])
        G = sb("G", [P, NT, E])
        MK = sb("MK", [P, 2, E, NT], BF16)
        keep1 = sb("keep1", [P, E])
        slot = sb("slot", [P, 2, NT]); slot_i = sb("slot_i", [P, 2, NT], I32)
        slot_u = sb("slot_u", [P, 2, NT], U32); slot_cur = sb("slot_cur", [P, 2, 4], U32)
        hi_i = sb("hi_i", [P, 2, NT], I32); lo_i = sb("lo_i", [P, 2, NT], I32)
        hi_b = sb("hi_b", [P, 2 * NT], BF16); lo_b = sb("lo_b", [P, 2 * NT], BF16)
        den = sb("den", [P, NT])
        with ExitStack() as shared_place:
            y_all = shared_place.enter_context(nc.sbuf_tensor("y_all", [P, 2, NT, D], F32))
            xT_hl = shared_place.enter_context(nc.sbuf_tensor("xT_hl", [P, 2, 2, CH * P], F32R))
            sw1_hl = shared_place.enter_context(nc.sbuf_tensor("sw1_hl", [P, 2, F], F32R))
            w1_hl = [shared_place.enter_context(nc.sbuf_tensor(f"w1_hl{k}", [P, 2, F], F32R)) for k in range(2)]
        with ExitStack() as shared_place:
            def sb_r(name, shape, dt=F32):
                return shared_place.enter_context(nc.sbuf_tensor(name, shape, dt))

            shared = sb_r("shared", [P, NT, D])
            hsh = sb_r("hsh", [P, 2, FT, 512])
            G1 = sb_r("G1", [P, NT, E]); t1 = sb_r("t1", [P, NT, E]); m1 = sb_r("m1", [P, NT, E])
            INC = sb_r("INC", [P, 2, E, NT]); POS = sb_r("POS", [P, 2, E, NT]); KM = sb_r("KM", [P, 2, E, NT])
            GK = sb_r("GK", [P, 2, E, NT])
            OH = sb_r("OH", [P, 2 * NT, SLOT_TILES], BF16)
            OL = sb_r("OL", [P, 2 * NT, P], BF16)
            RH = sb_r("RH", [P, 2 * NT, 2, SLOT_TILES], BF16)

        zero_rows = shared

        bdk = sb("bdk", [P, 2, GRP, 4, SEQ], F32R)
        pt = sb("pt", [P, 2, 3, 512])
        qc = sb("qc", [P, 2, GRP, SEQ], F32R)
        qk32 = sb("qk32", [P, 2, SEQ])
        qks = sb("qks", [P, 2, 2, 2, SEQ], F32R)
        oT = sb("oT", [P, GRP, SEQ])
        on = sb("on", [P, 2, HEADS, HD]); onT = sb("onT", [P, SEQ]); osum = sb("osum", [P, 2, HEADS])
        probs = sb("probs", [P, 2, 2, SEQ]); pT = sb("pT", [P, 2, SEQ]); gT = sb("gT", [P, SEQ])
        xg = sb("xg", [P, RING, CH, D])
        yo = sb("yo", [P, RING, CH, D])
        hT = sb("hT", [P, 2, FT, CH * P])
        row_f = sb("row_f", [P, SLOT_TILES]); row_e = sb("row_e", [P, SLOT_TILES])
        tok_idx = sb("tok_idx", [P, SLOT_TILES], U32); row_idx = sb("row_idx", [P, SLOT_TILES], U32)

        w1_s = [sb(f"w1_s{k}", [P, F]) for k in range(2)]
        w2_s = [sb(f"w2_s{k}", [P, FT, D]) for k in range(2)]
        tok_cur = sb("tok_cur", [P, 2, ST], U32); row_cur = sb("row_cur", [P, 2, ST], U32)
        b1_cur = sb("b1_cur", [P, 2, FT])
        
        yab = sb("yab", [P, 2, 4, D])

        kc = sb("kc", [P, 2, GRP, SEQ], F32R)
        v_ext = sb("v_ext", [P, 2, 2, HEADS, 32])
        negp = sb("negp", [P, 2, 2, P])
        cmask = sb("cmask", [P, P], BF16)
        head_p = sb("head_p", [P, 4, 4]); head_m = sb("head_m", [P, 4])
        qkv_w = sb("qkv_w", [P, HEADS, 3, HD]); w3 = sb("w3", [P, 3, HEADS, HD]); ow = sb("ow", [P, D])
        bv_b = sb("bv_b", [P, HEADS, HD]); ob_b = sb("ob_b", [P, D]); bq_s = sb("bq_s", [P, 1])


        S = Signals()
        S.const_pool = sem("const_pool")
        S.const_dve = sem("const_dve")
        S.x_head = sem("x_head")
        S.x_second = sem("x_second")
        S.x_tail = sem("x_tail")
        S.w_in = sem("w_in")
        S.w_moe_in = sem("w_moe_in")
        S.zero_set = sem("zero_set")
        S.y_zeroed = sem("y_zeroed")
        S.bias_in = sem("bias_in")
        S.bias_tr = sem("bias_tr")
        S.bias_set = sem("bias_set")
        S.w_tr = sem("w_tr")
        S.w_trs = sem("w_trs")
        S.wfold_mm = sem("wfold_mm")
        S.wfold = sem("wfold")
        S.ln_stats = sem("ln_stats")
        S.ln_mv = sem("ln_mv")
        S.ln_ve = sem("ln_ve")
        S.ln_rstd = sem("ln_rstd")
        S.xn_ready = sem("xn_ready")
        S.xn_tr = sem("xn_tr")
        S.xnT_ready = sem("xnT_ready")
        S.g_done = sem("g_done")
        S.gT_ready = sem("gT_ready")
        S.v_done = sem("v_done")
        S.v_ready = sem("v_ready")
        S.scores_done = sem("scores_done")
        S.max_ready = sem("max_ready")
        S.probs_ready = sem("probs_ready")
        S.probs_tr = sem("probs_tr")
        S.pT_ready = sem("pT_ready")
        S.y_done = sem("y_done")
        S.rsum_ready = sem("rsum_ready")
        S.attn_added = sem("attn_added")
        S.ln2_stats = sem("ln2_stats")
        S.ln2_mv = sem("ln2_mv")
        S.ln2_ve = sem("ln2_ve")
        S.ln2_rstd = sem("ln2_rstd")
        S.xn2_ready = sem("xn2_ready")
        S.xn2_tr = sem("xn2_tr")
        S.xn2T_ready = sem("xn2T_ready")
        S.xn2_stored = sem("xn2_stored")
        S.logT_done = sem("logT_done")
        S.logT_ready = sem("logT_ready")
        S.log_done = sem("log_done")
        S.log_ready = sem("log_ready")
        S.route = sem("route")
        S.shifted = sem("shifted")
        S.exped = sem("exped")
        S.masks_ready = sem("masks_ready")
        S.count_done = sem("count_done")
        S.onehot_ready = sem("onehot_ready")
        S.oh_ready = sem("oh_ready")
        S.rh_ready = sem("rh_ready")
        S.index_done = sem("index_done")
        S.index_ready = sem("index_ready")
        S.sh1_done = sem("sh1_done")
        S.sh1_ready = sem("sh1_ready")
        S.sh2_done = sem("sh2_done")
        S.sh2_ready = sem("sh2_ready")
        S.shared_added = sem("shared_added")
        S.xg_tr = sem("xg_tr")
        S.xT_hi = sem("xT_hi")
        S.xT_ready = sem("xT_ready")
        S.w1_hi = sem("w1_hi")
        S.sw1_split = sem("sw1_split")
        S.w1_split = sem("w1_split")
        S.h_done = sem("h_done")
        S.h_ready = sem("h_ready")
        S.yo_done = sem("yo_done")
        S.yo_ready = sem("yo_ready")
        S.w1_in0 = sem("w1_in0")
        S.w1_in1 = sem("w1_in1")
        S.tok_set = sem("tok_set")
        S.row_set = sem("row_set")
        S.b1_set = sem("b1_set")
        S.comb = sem("comb")
        S.slot_cur = sem("slot_cur")
        S.bd_act = sem("bd_act")
        S.y_used = sem("y_used")
        S.stored = sem("stored")
        S.tail_scaled = sem("tail_scaled")
        S.wb_in = sem("wb_in")
        S.init_b = sem("init_b")
        S.tb_done = sem("tb_done")
        S.tb_ready = sem("tb_ready")
        S.qk_done = sem("qk_done")
        S.qk32_ready = sem("qk32_ready")
        S.vb_done = sem("vb_done")
        S.vb_ready = sem("vb_ready")
        S.hilo_hi = sem("hilo_hi")
        S.hilo_done = sem("hilo_done")
        S.qks_stored0 = sem("qks_stored0")
        S.qks_stored1 = sem("qks_stored1")
        S.kc_in0 = sem("kc_in0")
        S.kc_in1 = sem("kc_in1")
        S.qc_in0 = sem("qc_in0")
        S.qc_in1 = sem("qc_in1")
        S.bd_done = sem("bd_done")
        S.a_done = sem("a_done")
        S.amax_done = sem("amax_done")
        S.negT_done = sem("negT_done")
        S.neg_set = sem("neg_set")
        S.c_done = sem("c_done")
        S.exp_done = sem("exp_done")
        S.aff_done = sem("aff_done")
        S.pv_done = sem("pv_done")
        S.ot_ready = sem("ot_ready")
        S.otr_done = sem("otr_done")
        S.osum_ready = sem("osum_ready")
        S.on_ready = sem("on_ready")
        S.onT_done = sem("onT_done")
        S.onT_ready = sem("onT_ready")
        S.pr_done = sem("pr_done")
        S.xb_added = sem("xb_added")
        S.ob_added = sem("ob_added")
        S.v_set = sem("v_set")
        gat = [sem(f"gathered{k}") for k in range(RING)]
        sca = [sem(f"scattered{k}") for k in range(RING)]
        sto = [sem(f"slots_stored{k}") for k in range(RING)]
        y_back = [sem(f"y_back{k}") for k in range(4)]
        tail_first = [sem(f"tail_first{k}") for k in range(2)]
        tail_done = [sem(f"tail_done{k}") for k in range(2)]
        y_in = [sem(f"y_in{c}") for c in range(2)]
        N_CONST_POOL = 16

        x_rows = x_in.rearrange("b (h p) d -> p (b h) d", p=P)
        out_rows = out.rearrange("b (h p) d -> p (b h) d", p=P)

        block = ctx.enter_context(nc.Block())

        TAIL_POOL, TAIL_DVE = (1, 4), (0, 2, 3, 5, 6, 7)
        TAIL_SCALED = ((0, 1), (1, 0), (1, 1), (2, 1), (3, 1), (4, 0), (4, 1), (5, 1), (6, 1))

        def scale_tail(act):
            act.wait_ge(S.yo_ready, LAYERS * LAYER_WORK)
            for pair, c in TAIL_SCALED:
                act.wait_ge(y_back[pair // 2], 32)
                for t in range(4 * pair, 4 * pair + 4):
                    a = act.activation(y_all[:, c, t, :], y_all[:, c, t, :], ACT.Copy, scale=gate[:, c, t:t + 1])
                a.then_inc(S.tail_scaled, 1)

        def combine_tail(eng, pairs, who):
            eng.wait_ge(S.yo_ready, LAYERS * LAYER_WORK)
            for n, pair in enumerate(pairs):
                eng.wait_ge(y_back[pair // 2], 32)
                for c in range(2):
                    if (pair, c) in TAIL_SCALED:
                        eng.wait_ge(S.tail_scaled, TAIL_SCALED.index((pair, c)) + 1)
                        xs = x[:, 4 * pair:4 * pair + 4, :]
                        a = eng.tensor_tensor(xs, xs, y_all[:, c, 4 * pair:4 * pair + 4, :], ALU.add)
                    else:
                        for t in range(4 * pair, 4 * pair + 4):
                            a = eng.scalar_tensor_tensor(out=x[:, t, :], in0=y_all[:, c, t, :], scalar=gate[:, c, t:t + 1],
                                                         in1=x[:, t, :], op0=ALU.mult, op1=ALU.add)
                    a.then_inc((tail_first, tail_done)[c][who], 1)
                    if c == 0:
                        eng.wait_ge(tail_first[who], n + 1)

        @block.sync
        def _(sp):
            sp.dma_start(x[:, 0:4, :], x_rows[:, 0:4, :]).then_inc(S.x_head, 16)
            sp.dma_start(x[:, 4:8, :], x_rows[:, 4:8, :]).then_inc(S.x_second, 16)
            sp.wait_ge(S.w_in, 16 * 5)
            sp.dma_start(x[:, 8:NT, :], x_rows[:, 8:NT, :]).then_inc(S.x_tail, 16)
            sp.dma_start(sw1_s[:, :], sw1).then_inc(S.w_moe_in, 16)
            sp.dma_start(sw2_s[:, :, :], sw2.rearrange("(f p) d -> p f d", p=P)).then_inc(S.w_moe_in, 16)
            sp.dma_start(b2_b[:, :, :], b2.unsqueeze(0).broadcast_to([P, E, D])).then_inc(S.w_moe_in, 16)
            sp.dma_start(sb2_b[:, :], sb2.unsqueeze(0).broadcast_to([P, D])).then_inc(S.w_moe_in, 16)
            sp.dma_start(qkv_w[:, :, :, :].rearrange("p h c d -> p (h c d)"), attn_W).then_inc(S.wb_in, 16)
            sp.dma_start(ow[:, :], out_W).then_inc(S.wb_in, 16)
            sp.dma_start(ob_b[:, :], out_b.unsqueeze(0).broadcast_to([P, D])).then_inc(S.wb_in, 16)
            sp.dma_start(bv_b[:, :, :], attn_b.rearrange("(h c d) -> c h d", c=3, d=HD)[2:3].broadcast_to([P, HEADS, HD])
                         ).then_inc(S.wb_in, 16)

            def store_xn(l, i):
                alone(sp, S.xn2_ready, PAIRS * l + i + 1, S.x_head)
                sp.dma_start(xn_rows.rearrange("(t p) d -> p t d", p=P)[:, bass.ds(4 * i, 4), :],
                             xn2[:, :, :]).then_inc(S.xn2_stored, 16)

            def weights(l, i, h):
                sm = (S.w1_in0, S.w1_in1)[h]
                alone(sp, S.yo_done, before_reuse(l, i, h), S.x_head)
                alone(sp, S.w1_split, (l * E // 2 + i - 1) * 2 + h + 1, S.x_head)
                sp.dma_start(w1_s[h][:, :], w1[bass.ds(2 * i + h, 1), :, :].rearrange("a p f -> p (a f)")).then_inc(sm, 16)
                sp.dma_start(w2_s[h][:, :, :], w2[bass.ds(2 * i + h, 1), :, :].rearrange("a (f p) d -> p (a f) d", p=P)).then_inc(sm, 16)

            def store_slots(i, k):
                r, c = k % RING, k % CHUNKS
                alone(sp, S.yo_ready, work_of(0, i, k) + 1, S.x_head)
                rows = y_slots.rearrange("(e s p) d -> p e s d", e=E, p=P)
                for j in range(CH):
                    sp.dma_start(rows[:, bass.ds(2 * i + k // CHUNKS, 1), c * CH + j, :], yo[:, r, j:j + 1, :]).then_inc(sto[r], 16)

            def expert_pair(i, more):
                for k in range(2 * CHUNKS):
                    store_slots(i, k)
                    if more and k % CHUNKS == CHUNKS - 1:
                        weights(0, i + 1, k // CHUNKS)

            def restack(t, par):
                n = 2 * t + par
                rows_stored, k_in, q_in = ((S.qks_stored0, S.kc_in0, S.qc_in0), (S.qks_stored1, S.kc_in1, S.qc_in1))[par]
                alone(sp, S.hilo_done, n + 1, S.x_head)
                need(sp, k_in, 48 * t)
                need(sp, q_in, 48 * t)
                sp.dma_start(qk_rows[par], qks[:, par, :, :, :].bitcast(F32)).then_inc(rows_stored, 16)
                alone(sp, rows_stored, 16 * t + 16, S.x_head)
                need(sp, S.bd_done, GRP * (n - 1))
                need(sp, S.bd_act, GRP * (n - 1))
                rows = qk_rows[par].rearrange("(g r) a b t -> r g a b t", g=GRP)
                for part, half in enumerate((0, 1, 0)):
                    sp.dma_start(kc[32 * part:32 * part + 32, par, :, :].bitcast(F32), rows[:, :, half, 1, :]).then_inc(k_in, 16)
                need(sp, S.c_done, 3 * GRP * (n - 1))
                for part, half in enumerate((0, 0, 1)):
                    sp.dma_start(qc[32 * part:32 * part + 32, par, :, :].bitcast(F32), rows[:, :, half, 0, :]).then_inc(q_in, 16)

            def attn_b_pair(i):
                if valid(i + 1):
                    restack(i + 1, 0)
                if valid(i - 2):
                    store_xn(1, i - 2)
                if valid(i + 1):
                    restack(i + 1, 1)

            with sp.Fori(0, PAIRS) as i:
                store_xn(0, i)
            weights(0, 0, 0)
            weights(0, 0, 1)
            with sp.Fori(0, E // 2 - 1) as i:
                expert_pair(i, True)
            expert_pair(E // 2 - 1, False)
            weights(1, 0, 0)
            weights(1, 0, 1)
            for i in range(-1, 2):
                attn_b_pair(i)
            with sp.Fori(2, PAIRS - 3) as i:
                attn_b_pair(i)
            for i in range(PAIRS - 3, PAIRS + 1):
                attn_b_pair(i)
            store_xn(1, PAIRS - 1)
            with sp.Fori(1, E // 2) as i:
                weights(1, i, 0)
                weights(1, i, 1)
            for k in range(RING):
                sp.wait_ge(sca[k], 32 * E * CHUNKS // RING)
            sp.wait_ge(S.shared_added, 3 * E // 2 * LAYERS)
            part = NT // 4
            for k in range(4):
                for c in range(2):
                    src = y_rows[c * T:(c + 1) * T, :].rearrange("(t p) d -> p t d", p=P)
                    sp.dma_start(y_all[:, c, part * k:part * k + part, :], src[:, part * k:part * k + part, :]).then_inc(y_back[k], 16)
            for i in range(PAIRS):
                if i in TAIL_DVE:
                    sp.wait_ge(tail_done[0], TAIL_DVE.index(i) + 1)
                else:
                    sp.wait_ge(tail_done[1], TAIL_POOL.index(i) + 1)
                sp.dma_start(out_rows[:, 4 * i:4 * i + 4, :], x[:, 4 * i:4 * i + 4, :]).then_inc(S.stored, 16)
            sp.wait_ge(S.stored, 16 * PAIRS)

        @block.gpsimd
        def _(pool):
            n_const = 0

            def const(ins):
                nonlocal n_const
                n_const += 1
                return ins.then_inc(S.const_pool, 1)

            const(pool.memset(ident[:, :], 0.0))
            const(pool.memset(before[:, :], 0.0))
            pool.wait_ge(S.const_pool, 2)
            const(pool.affine_select(out=ident[:, :], in_=ident[:, :], compare_op=ALU.not_equal, fill=1.0,
                                     base=0, pattern=[[-1, P]], channel_multiplier=1))
            const(pool.affine_select(out=before[:, :], in_=before[:, :], compare_op=ALU.is_gt, fill=-1.0,
                                     base=0, pattern=[[1, P]], channel_multiplier=-1))
            const(pool.memset(neg_half[:, :], -0.5))
            const(pool.memset(ones_bf[:, :], 1.0))
            const(pool.iota(iota_lo[:, :], [[1, P]], base=0, channel_multiplier=0, allow_small_or_imprecise_dtypes=True))
            const(pool.iota(iota_hi[:, :], [[1, SLOT_TILES]], base=0, channel_multiplier=0, allow_small_or_imprecise_dtypes=True))
            const(pool.iota(part1[:, :], [[1, 1]], base=1, channel_multiplier=1, allow_small_or_imprecise_dtypes=True))
            const(pool.iota(rev[:, :], [[-1, E]], base=E, channel_multiplier=0, allow_small_or_imprecise_dtypes=True))
            const(pool.iota(slot_base[:, :, :], [[CAP, E], [0, NT]], base=1, channel_multiplier=0, allow_small_or_imprecise_dtypes=True))
            const(pool.iota(tile_code[:, :], [[1, 2 * NT]], base=0, channel_multiplier=0, allow_small_or_imprecise_dtypes=True))
            const(pool.memset(carry[:, :], 1.0))
            const(pool.memset(cmask[:, :], 0.0))
            pool.wait_ge(S.const_pool, n_const)
            const(pool.memset(carry[:, :].rearrange("p (r t) -> p r t", t=NT)[:, :, 0:1], 0.0))
            const(pool.affine_select(out=cmask[:, :], in_=cmask[:, :], compare_op=ALU.is_ge, fill=MASKED,
                                     base=0, pattern=[[-1, P]], channel_multiplier=1))
            assert n_const == N_CONST_POOL, n_const

            def rstd_of(mv_, ve_, out_, s_in, s_mid, s_out, n):
                alone(pool, s_in, n, S.const_pool)
                pool.tensor_scalar(ve_[:, :], mv_[:, :, 1], EPS, 1.0, ALU.add, ALU.mult).then_inc(s_mid, 1)
                alone(pool, s_mid, n, S.const_pool)
                pool.tensor_tensor(out_[:, :], ve_[:, :], neg_half[:, :], ALU.pow).then_inc(s_out, 1)

            rstd_of(mv, ve, rstd, S.ln_mv, S.ln_ve, S.ln_rstd, 1)
            pool.memset(zero_rows[:, :, :], 0.0).then_inc(S.zero_set, 1)
            rstd_of(mv, ve, rstd, S.ln_mv, S.ln_ve, S.ln_rstd, 2)
            pool.wait_ge(S.zero_set, 1)
            for half in range(2):
                pool.dma_start(y_rows[half * T:(half + 1) * T, :].rearrange("(t p) d -> p t d", p=P),
                               zero_rows[:, :, :]).then_inc(S.y_zeroed, 16)
            with pool.Fori(0, PAIRS - 2) as i:
                rstd_of(mv, ve, rstd, S.ln_mv, S.ln_ve, S.ln_rstd, i + 3)
                rstd_of(mv2, ve2, rstd2, S.ln2_mv, S.ln2_ve, S.ln2_rstd, i + 1)
            for i in range(PAIRS - 2, PAIRS):
                rstd_of(mv2, ve2, rstd2, S.ln2_mv, S.ln2_ve, S.ln2_rstd, i + 1)

            alone(pool, S.wb_in, 16 * 4, S.const_pool)
            for c in range(3):
                pool.tensor_copy(w3[:, c, :, :], qkv_w[:, :, c, :])
            pool.tensor_copy(ident_bf[:, :], ident[:, :]).then_inc(S.init_b, 1)
            pool.wait_ge(S.init_b, 1)
            pool.memset(kc[96:P, :, :, :].bitcast(F32), 1.0).then_inc(S.init_b, 1)
            pool.wait_ge(S.init_b, 2)
            pool.memset(negp[:, :, :, :], 0.0)
            pool.memset(v_ext[:, :, :, :, 0:HD], 0.0)
            pool.memset(v_ext[:, :, :, :, HD + 1:32], 0.0)
            pool.memset(v_ext[:, :, :, :, HD:HD + 1], 1.0)
            pool.memset(head_p[:, :, :], 1.0).then_inc(S.init_b, 1)
            pool.wait_ge(S.init_b, 3)
            pool.affine_select(out=head_p[:, :, :], in_=head_p[:, :, :], compare_op=ALU.is_ge, fill=0.0,
                               base=0, pattern=[[-32, 4], [-8, 4]], channel_multiplier=1).then_inc(S.init_b, 1)
            pool.wait_ge(S.init_b, 4)
            pool.affine_select(out=head_p[:, :, :], in_=head_p[:, :, :], compare_op=ALU.is_ge, fill=0.0,
                               base=HD - 1, pattern=[[32, 4], [8, 4]], channel_multiplier=-1).then_inc(S.init_b, 1)
            pool.wait_ge(S.init_b, 5)
            pool.tensor_tensor(head_p[:, 0:2, :], head_p[:, 0:2, :], head_p[:, 2:4, :], ALU.add).then_inc(S.init_b, 1)
            pool.wait_ge(S.init_b, 6)
            pool.tensor_tensor(head_m[:, :], head_p[:, 0, :], head_p[:, 1, :], ALU.add).then_inc(S.init_b, 1)

            def take_tokens(n, h, ex):
                pool.tensor_copy(tok_cur[:, h, :], tok_idx[:, bass.ds(ST * ex, ST)]).then_inc(S.tok_set, 1)
                alone(pool, S.tok_set, n, S.const_pool)

            def take_rows(n, h, ex):
                pool.tensor_copy(row_cur[:, h, :], row_idx[:, bass.ds(ST * ex, ST)]).then_inc(S.row_set, 1)
                alone(pool, S.row_set, n, S.const_pool)

            def gather(l, i, k):
                i, k = i + k // (2 * CHUNKS), k % (2 * CHUNKS)
                h, c, r = k // CHUNKS, k % CHUNKS, k % RING
                alone(pool, S.xg_tr, l * E * CHUNKS + 2 * CHUNKS * i + k - RING + 1, S.const_pool)
                for j in range(CH):
                    pool.indirect_dma_start(xg[:, r, j, :], None, xn_rows,
                                            bass.IndirectOffsetOnAxis(ap=tok_cur[:, h, c * CH + j:c * CH + j + 1], axis=0)
                                            ).then_inc(gat[r], 16)

            def scatter(l, i, k):
                h, c, r = k // CHUNKS, k % CHUNKS, k % RING
                alone(pool, S.yo_ready, work_of(l, i, k) + 1, S.const_pool)
                for j in range(CH):
                    pool.indirect_dma_start(y_rows, bass.IndirectOffsetOnAxis(ap=row_cur[:, h, c * CH + j:c * CH + j + 1], axis=0),
                                            yo[:, r, j, :], None, bounds_check=2 * T - 1, oob_is_err=False
                                            ).then_inc(sca[r], 16)

            AHEAD = 4

            def expert_pair(l, i, last):
                for k in range(2 * CHUNKS):
                    if not last or k + AHEAD < 2 * CHUNKS:
                        gather(l, i, k + AHEAD)
                    if l == 1:
                        scatter(l, i, k)
                    if not last and k == CHUNKS:
                        for r in range(RING):
                            alone(pool, gat[r], 32 * (l * E * CHUNKS // RING + 2 * i + 1), S.const_pool)
                        take_tokens(E * l + 2 * i + 3, 0, 2 * i + 2)
                    if l == 1 and k == 3 and not (isinstance(i, int) and i == 0):
                        for r in range(RING):
                            alone(pool, sca[r], 32 * (2 * i), S.const_pool)
                        take_rows(2 * i + 2, 1, 2 * i + 1)
                if not last:
                    for r in range(RING):
                        alone(pool, gat[r], 32 * (l * E * CHUNKS // RING + 2 * i + 2), S.const_pool)
                    take_tokens(E * l + 2 * i + 4, 1, 2 * i + 3)
                    if l == 1:
                        for r in range(RING):
                            alone(pool, sca[r], 32 * (2 * i + 1), S.const_pool)
                        take_rows(2 * i + 3, 0, 2 * i + 2)

            def block_diag(t, par, g):
                U = 2 * GRP * t + GRP * par + g
                if g == 0:
                    alone(pool, (S.kc_in0, S.kc_in1)[par], 48 * t + 48, S.const_pool)
                alone(pool, S.c_done, 3 * (U - 2 * GRP) + 3, S.const_pool)
                for j in range(2):
                    a = pool.tensor_scalar(bdk[:, par, g, j, :], kc[:, par, g, :].bitcast(F32), head_m[:, j:j + 1], 1.0,
                                           ALU.mult, ALU.mult)
                a.then_inc(S.bd_done, 1)

            def causal(t, par, g):
                U = 2 * GRP * t + GRP * par + g
                alone(pool, S.exp_done, 3 * U + 3, S.const_pool)
                first = pt[:, g % 2, 0:2, :].rearrange("p u (j q) -> p (u j) q", j=2)[:, :, 0:P]
                second = pt[:, g % 2, 2, :].rearrange("p (j q) -> p j q", j=4)
                for blk in (first, second):
                    a = pool.affine_select(out=blk, in_=blk, compare_op=ALU.is_ge, fill=0.0, base=0,
                                           pattern=[[0, 4], [1, P]], channel_multiplier=-1)
                a.then_inc(S.aff_done, 1)

            def y_gather(p, c, j):
                if j == 0:
                    alone(pool, y_in[c], 64 * p, S.const_pool)
                    n = 2 * p + c + 1
                    pool.tensor_copy(slot_cur[:, c, :], slot_u[:, c, bass.ds(4 * p, 4)]).then_inc(S.slot_cur, 1)
                    alone(pool, S.slot_cur, n, S.const_pool)
                    alone(pool, (S.comb, S.y_used)[c], p, S.const_pool)
                pool.indirect_dma_start(yab[:, c, j, :], None, y_slots,
                                        bass.IndirectOffsetOnAxis(ap=slot_cur[:, c, j:j + 1], axis=0)).then_inc(y_in[c], 16)

            def add_ob(i):
                alone(pool, S.xn_ready, PAIRS + i + 1, S.const_pool)
                xs = x[:, bass.ds(4 * i, 4), :]
                pool.tensor_tensor(xs, xs, ob_b[:, :].unsqueeze(1).broadcast_to([P, 4, D]), ALU.add).then_inc(S.ob_added, 1)

            def attn_b_pair(i):
                for h in range(2):
                    for g in range(GRP):
                        t, par, gg = shifted_group(i, h, g, 2)
                        if valid(t):
                            block_diag(t, par, gg)
                        if h == 1 and g == 2 and valid(i + 2):
                            rstd_of(mv, ve, rstd, S.ln_mv, S.ln_ve, S.ln_rstd, PAIRS + i + 3)
                        t, par, gg = shifted_group(i, h, g, -2)
                        if valid(t):
                            causal(t, par, gg)
                        if h == 0 and g == 0 and valid(i - 2):
                            rstd_of(mv2, ve2, rstd2, S.ln2_mv, S.ln2_ve, S.ln2_rstd, PAIRS + i - 1)
                        if h == 1 and g == 0 and valid(i + 1):
                            add_ob(i + 1)
                        q = GRP * h + g - 2
                        if valid(i + 3 + q // (2 * GRP)) and not (isinstance(i, int) and i + 3 + q // (2 * GRP) < 1):
                            y_gather(i + 3 + q // (2 * GRP), q % (2 * GRP) // 4, q % 4)

            for l in range(LAYERS):
                alone(pool, S.oh_ready, l + 1, S.const_pool)
                for c in range(2):
                    ns = slice(c * NT, c * NT + NT)
                    pool.tensor_tensor(RH[:, ns, 1, :], OH[:, ns, :], tile_code[:, ns].unsqueeze(2).broadcast_to([P, NT, SLOT_TILES]),
                                       ALU.mult).then_inc(S.rh_ready, 1)
                alone(pool, S.index_ready, l + 1, S.const_pool)
                if l == 0:
                    alone(pool, S.y_zeroed, 32, S.const_pool)
                alone(pool, S.xn2_stored, 16 * PAIRS * (l + 1), S.const_pool)
                take_tokens(E * l + 1, 0, 0)
                for k in range(AHEAD):
                    gather(l, 0, k)
                take_tokens(E * l + 2, 1, 1)
                if l == 1:
                    take_rows(1, 0, 0)
                    take_rows(2, 1, 1)
                expert_pair(l, 0, False)
                with pool.Fori(1, E // 2 - 1) as i:
                    expert_pair(l, i, False)
                expert_pair(l, E // 2 - 1, True)
                if l == 0:
                    for r in range(RING):
                        alone(pool, sto[r], 32 * E * CHUNKS // RING, S.const_pool)
                    for c in range(2):
                        for k in range(4):
                            y_gather(0, c, k)
                    for k in range(4):
                        y_gather(1, 0, k)
                    rstd_of(mv, ve, rstd, S.ln_mv, S.ln_ve, S.ln_rstd, PAIRS + 1)
                    for k in range(2):
                        y_gather(1, 1, k)
                    pool.wait_ge(S.init_b, 7)
                    for i in range(-1, 2):
                        attn_b_pair(i)
                    with pool.Fori(2, PAIRS - 3) as i:
                        attn_b_pair(i)
                    for i in range(PAIRS - 3, PAIRS + 1):
                        attn_b_pair(i)
                    rstd_of(mv2, ve2, rstd2, S.ln2_mv, S.ln2_ve, S.ln2_rstd, 2 * PAIRS)
            combine_tail(pool, TAIL_POOL, 1)

        @block.tensor
        def _(pe):
            def keep_busy(times):
                for _ in range(times):
                    pe.matmul(bank[4][:, 0:P], ident[:, :], ident[:, :], start=True, stop=True)

            pe.wait_ge(S.const_pool, N_CONST_POOL)
            keep_busy(8)
            pe.wait_ge(S.w_in, 16 * 5)
            for k, w in enumerate((wq, wk, wv)):
                m = pe.transpose(bank[1][:, k * P:(k + 1) * P], w[:, :], ident[:, :])
            m.then_inc(S.w_tr, 1)
            pe.wait_ge(S.w_trs, 2)
            pe.matmul(bank[2][:, 0:P], wT[:, 0, :], wT[:, 1, :], start=True, stop=True)
            pe.matmul(bank[2][:, P:2 * P], wT[:, 2, :], wo_m[:, :], start=True, stop=True).then_inc(S.wfold_mm, 1)
            pe.wait_ge(S.wfold, 1)

            RT_, GT_, V_, S_, PT_, Y_, L_ = bank[0], bank[1], bank[2], bank[3:5], bank[5], bank[6], bank[7]
            R_ = L_

            def a_transpose(t, par):
                n = 2 * t + par
                if par == 0:
                    pe.wait_ge(S.xn_ready, t + 1)
                need(pe, S.xnT_ready, n)
                for j in range(2):
                    m = pe.transpose(RT_[:, j * P:(j + 1) * P], xn[:, 2 * par + j, :], ident[:, :])
                m.then_inc(S.xn_tr, 1)

            def a_project(t, par):
                n = 2 * t + par
                pe.wait_ge(S.xnT_ready, n + 1)
                need(pe, S.gT_ready, n)
                pe.matmul(GT_[:, 0:SEQ], m_qk[:, :], xnT[:, par, :], start=True, stop=True).then_inc(S.g_done, 1)
                need(pe, S.v_ready, n)
                for j in range(2):
                    m = pe.matmul(V_[:, j * P:(j + 1) * P], xnT[:, par, j * P:(j + 1) * P], m_vo[:, :], start=True, stop=True)
                m.then_inc(S.v_done, 1)

            def a_scores(t, par):
                n = 2 * t + par
                pe.wait_ge(S.gT_ready, n + 1)
                need(pe, S.probs_ready, n - 1)
                for q in range(2):
                    m = pe.matmul(S_[par][:, q * SEQ:(q + 1) * SEQ], gT[:, q * P:(q + 1) * P], xnT[:, par, :], start=True, stop=True)
                m.then_inc(S.scores_done, 1)

            def a_probs_transpose(t, par):
                n = 2 * t + par
                pe.wait_ge(S.probs_ready, n + 1)
                need(pe, S.pT_ready, n)
                for kt in range(2):
                    for q in range(2):
                        m = pe.transpose(PT_[:, kt * SEQ + q * P:kt * SEQ + (q + 1) * P], probs[:, par, q, kt * P:(kt + 1) * P], ident[:, :])
                m.then_inc(S.probs_tr, 1)

            def a_values(t, par):
                n = 2 * t + par
                pe.wait_ge(S.pT_ready, n + 1)
                pe.wait_ge(S.v_ready, n + 1)
                need(pe, S.attn_added, n)
                for q in range(2):
                    for kt in range(2):
                        m = pe.matmul(Y_[:, q * P:(q + 1) * P], pT[:, kt, q * P:(q + 1) * P], v_s[:, par, kt, :],
                                      start=(kt == 0), stop=(kt == 1))
                m.then_inc(S.y_done, 1)

            def r_transpose(n, bk=R_):
                pe.wait_ge(S.xn2_ready, n + 1)
                need(pe, S.log_ready, n)
                for j in range(4):
                    m = pe.transpose(bk[:, j * P:(j + 1) * P], xn2[:, j, :], ident[:, :])
                m.then_inc(S.xn2_tr, 1)

            def r_logits(n, i, bk=L_):
                pe.wait_ge(S.xn2T_ready, n + 1)
                pe.matmul(bk[0:E, 0:512], router[:, :], xnT_all[:, bass.ds(512 * i, 512)], start=True, stop=True).then_inc(S.logT_done, 1)

            def r_back(n, bk=R_):
                alone(pe, S.logT_ready, n + 1, S.const_pool)
                for j in range(4):
                    m = pe.transpose(bk[:, j * E:(j + 1) * E], logT[:, j * P:(j + 1) * P], ident[0:E, 0:E])
                m.then_inc(S.log_done, 1)

            def attn_a_pair(i):
                for h in range(2):
                    if valid(i):
                        a_probs_transpose(i, h)
                    if valid(shifted_seq(i, h, 1)[0]):
                        a_scores(*shifted_seq(i, h, 1))
                    if valid(i - 1) and h == 1:
                        r_transpose(i - 1)
                    if valid(shifted_seq(i, h, 2)[0]):
                        a_project(*shifted_seq(i, h, 2))
                    if valid(i - 2) and h == 0:
                        r_back(i - 2)
                    if valid(i):
                        a_values(i, h)
                    if valid(shifted_seq(i, h, 3)[0]):
                        a_transpose(*shifted_seq(i, h, 3))
                    if valid(i - 1) and h == 1:
                        r_logits(i - 1, i - 1)

            def sh_first(l, c, cb, fs=range(FT)):
                for f in fs:
                    need(pe, S.sh1_ready, l * SHC * FT + FT * (c - 1) + f + 1)
                    pe.matmul(bank[f][:, :], sw1_s[:, f * P:(f + 1) * P], xnT_all[:, bass.ds(512 * c, 512)],
                              start=True, stop=True).then_inc(S.sh1_done, 1)

            def last_pair_logits(l, bk):
                n = PAIRS * (l + 1) - 1
                sh_first(l, 0, 0, range(0, 3))
                r_transpose(n, bk)
                r_logits(n, PAIRS - 1, bk)
                r_back(n, bk)
                sh_first(l, 0, 0, range(3, FT))

            for i in range(-2, 1):
                attn_a_pair(i)
                if i == -1:
                    pe.wait_ge(S.bias_in, 16 * 5)
                    pe.transpose(L_[:, 0:38], bias_rows[:, :], ident[0:38, 0:38]).then_inc(S.bias_tr, 1)
            pe.wait_ge(S.bias_set, 1)
            for i in range(1, 3):
                attn_a_pair(i)
            with pe.Fori(3, PAIRS - 2) as i:
                attn_a_pair(i)
            for i in range(PAIRS - 2, PAIRS):
                attn_a_pair(i)
            r_back(PAIRS - 2)
            pe.wait_ge(S.w_moe_in, 16 * 4)
            last_pair_logits(0, L_)

            HB = bank[0:4]
            XT = bank[4:6]
            YB = bank[6:8]

            def sh_second(l, c, cb, tiles=range(4)):
                pe.wait_ge(S.sh1_ready, l * SHC * FT + FT * c + FT)
                need(pe, S.sh2_ready, l * SHC + c - 1)
                for t in tiles:
                    for f in range(FT):
                        m = pe.matmul(YB[cb][:, t * P:(t + 1) * P], hsh[:, cb, f, t * P:(t + 1) * P], sw2_s[:, f, :],
                                      start=(f == 0), stop=(f == FT - 1))
                if tiles[-1] == 3:
                    m.then_inc(S.sh2_done, 1)

            def counts(l):
                pe.wait_ge(S.masks_ready, l + 1)
                flat = MK[:, :, :, :].rearrange("p c e t -> p (c e t)")
                pe.matmul(XT[0][:, :], before[:, :], flat, start=True, stop=True)
                pe.matmul(XT[1][:, :], ones_bf[:, :], flat, start=True, stop=True).then_inc(S.count_done, 1)

            def index(l, c):
                pe.wait_ge(S.onehot_ready, 2 * l + c + 1)
                pe.wait_ge(S.rh_ready, 2 * l + c + 1)
                for n in range(c * NT, c * NT + NT):
                    m = pe.matmul(XT[0][:, 0:2 * SLOT_TILES], OL[:, n, :], RH[:, n, :, :].rearrange("p a s -> p (a s)"),
                                  start=(n == 0), stop=(n == 2 * NT - 1))
                m.then_inc(S.index_done, 1)

            def x_tr(l, i, k):
                i, k = i + k // (2 * CHUNKS), k % (2 * CHUNKS)
                r = k % RING
                pe.wait_ge(gat[r], 32 * (l * E * CHUNKS // RING + 2 * i + k // RING + 1))
                n = l * E * CHUNKS + 2 * CHUNKS * i + k
                if not (isinstance(i, int) and i == 0 and k < 2):
                    need(pe, S.xT_ready, work_of(l, i + (k - 2) // (2 * CHUNKS), (k - 2) % (2 * CHUNKS)) + 1)
                for j in range(CH):
                    m = pe.transpose(XT[k % 2][:, j * P:(j + 1) * P], xg[:, r, j, :], ident[:, :])
                m.then_inc(S.xg_tr, 1)

            def first_mm(l, i, v):
                n, k = work(l, i, v)
                if k is None:
                    w = sw1_hl
                    pe.wait_ge(S.sw1_split, 2 * l + 2)
                else:
                    w = w1_hl[k // CHUNKS]
                    if k % CHUNKS == 0:
                        pe.wait_ge(S.w1_split, l * E + 2 * i + k // CHUNKS + 1)
                        pe.wait_ge((S.w1_in0, S.w1_in1)[k // CHUNKS], 32 * (l * E // 2 + i + 1))
                pe.wait_ge(S.xT_ready, n + 1)
                need(pe, S.h_ready, n - 1)
                for f in range(FT):
                    bk = HB[2 * (v % 2) + f // 2]
                    for p, (wp, xp) in enumerate(((1, 0), (0, 1), (0, 0))):
                        m = pe.matmul(bk[:, (f % 2) * 256:(f % 2) * 256 + 256], w[:, wp, f * P:(f + 1) * P],
                                      xT_hl[:, v % 2, xp, :], start=(p == 0), stop=(p == 2))
                m.then_inc(S.h_done, 1)

            def second_mm(l, i, v):
                if v < 0:
                    i, v = i - 1, v + len(order(l, i - 1))
                n, k = work(l, i, v)
                w = sw2_s if k is None else w2_s[k // CHUNKS]
                pe.wait_ge(S.h_ready, n + 1)
                need(pe, S.yo_ready, n - 1)
                for j in range(CH):
                    for f in range(FT):
                        m = pe.matmul(YB[v % 2][:, j * P:(j + 1) * P], hT[:, v % 2, f, j * P:(j + 1) * P], w[:, f, :],
                                      start=(f == 0), stop=(f == FT - 1))
                m.then_inc(S.yo_done, 1)

            def expert_pair(l, i, first, last):
                for v, k in enumerate(order(l, i)):
                    wraps = v + 1 == len(order(l, i))
                    following = order(l, i + 1)[0] if wraps else order(l, i)[v + 1]
                    transposes = following is not None and not (last and wraps)
                    if k is None:
                        first_mm(l, i, v)
                    if transposes and not (first and k is None):
                        x_tr(l, i, following + (2 * CHUNKS if wraps else 0))
                    if k is not None:
                        first_mm(l, i, v)
                    if not (first and v == 0):
                        second_mm(l, i, v - 1)
                    if transposes and first and k is None:
                        pe.wait_ge(S.index_ready, l + 1)
                        x_tr(l, i, following)

            AB, CB, OB, MB, XB, ZB = bank[0:2], bank[2:4], bank[4], bank[5], bank[6], bank[7]

            def pass1(t, par, g, k):
                U = 2 * GRP * t + GRP * par + g
                if k == 0:
                    if g == 0:
                        pe.wait_ge((S.qc_in0, S.qc_in1)[par], 48 * t + 48)
                    pe.wait_ge(S.bd_done, U + 1)
                    pe.wait_ge(S.bd_act, U + 1)
                bk, qt = AB[(g + k) % 2], min(k, 1)
                need(pe, S.amax_done, 3 * U + k - 1)
                q = qc[0:96, par, g, qt * P:qt * P + P]
                if k == 0:
                    pe.matmul(bk[:, :], q, bdk[0:96, par, g, :, 0:P], start=True, stop=False)
                    m = pe.matmul(bk[:, :], ident_bf[:, :], cmask[:, :].unsqueeze(1).broadcast_to([P, 4, P]),
                                  start=False, stop=True)
                else:
                    pe.matmul(bk[:, :], q, bdk[0:96, par, g, 2 * k - 2:2 * k, :], start=True, stop=False)
                    m = pe.matmul(bk[:, :].rearrange("p (j k) -> p j k", j=2)[:, :, P:SEQ], ident_bf[:, :],
                                  cmask[:, :].unsqueeze(1).broadcast_to([P, 2, P]), start=False, stop=True)
                m.then_inc(S.a_done, 1)

            def neg_transpose(t, par, g):
                U = 2 * GRP * t + GRP * par + g
                pe.wait_ge(S.amax_done, 3 * U + 3)
                need(pe, S.neg_set, U)
                for qt in range(2):
                    m = pe.transpose(MB[:, qt * P:qt * P + P], negp[:, g % 2, qt, :], ident[:, :])
                m.then_inc(S.negT_done, 1)

            def pass2(t, par, g, k):
                U = 2 * GRP * t + GRP * par + g
                if k == 0:
                    pe.wait_ge(S.neg_set, U + 1)
                bk = CB[(g + k) % 2]
                need(pe, S.exp_done, 3 * U + k - 1)
                if k < 2:
                    for j in range(2):
                        m = pe.matmul(bk[:, j * SEQ:j * SEQ + SEQ], bdk[:, par, g, 2 * k + j, 0:P], qc[:, par, g, :],
                                      start=True, stop=True)
                else:
                    for j in range(4):
                        m = pe.matmul(bk[:, j * P:j * P + P], bdk[:, par, g, j, P:SEQ], qc[:, par, g, P:SEQ],
                                      start=True, stop=True)
                m.then_inc(S.c_done, 1)

            def values(t, par, g):
                n = 2 * t + par
                U = GRP * n + g
                pe.wait_ge(S.aff_done, U + 1)
                if g == 0:
                    pe.wait_ge(S.v_set, n + 1)
                if g % 2 == 0:
                    need(pe, S.ot_ready, 2 * n + g // 2)
                c0 = (g % 2) * SEQ
                for kt in range(2):
                    for j in range(4):
                        if kt == 0:
                            rhs = pt[:, g % 2, j // 2, (j % 2) * SEQ:(j % 2) * SEQ + SEQ]
                        else:
                            rhs = pt[:, g % 2, 2, j * P:j * P + P]
                        m = pe.matmul(OB[32 * j:32 * j + 32, c0 + kt * P:c0 + SEQ], v_ext[:, par, kt, 4 * g + j, :], rhs,
                                      start=(kt == 0), stop=(kt == 1))
                m.then_inc(S.pv_done, 1)

            def b_transpose(t, par):
                n = 2 * t + par
                pe.wait_ge(S.xn_ready, PAIRS + t + 1)
                need(pe, S.vb_ready, n)
                need(pe, S.on_ready, n - 3)
                for j in range(2):
                    m = pe.transpose(ZB[:, j * P:(j + 1) * P], xn[:, 2 * par + j, :], ident[:, :])
                m.then_inc(S.tb_done, 1)

            def b_project(t, par):
                n = 2 * t + par
                pe.wait_ge(S.tb_ready, n + 1)
                need(pe, S.onT_ready, n - 3)
                need(pe, S.qk32_ready, n)
                for c in range(2):
                    m = pe.matmul(XB[:, c * SEQ:(c + 1) * SEQ], w3[:, c, :, :].rearrange("p h d -> p (h d)"), xnT[:, par, :],
                                  start=True, stop=True)
                m.then_inc(S.qk_done, 1)
                for j in range(2):
                    m = pe.matmul(ZB[:, j * P:(j + 1) * P], xnT[:, par, j * P:(j + 1) * P],
                                  w3[:, 2, :, :].rearrange("p h d -> p (h d)"), start=True, stop=True)
                m.then_inc(S.vb_done, 1)

            def o_back(t, par):
                n = 2 * t + par
                pe.wait_ge(S.ot_ready, 2 * n + 2)
                need(pe, S.xb_added, n)
                for qt in range(2):
                    for g in range(GRP):
                        m = pe.transpose((XB, ZB)[qt][:, g * P:(g + 1) * P], oT[:, g, qt * P:(qt + 1) * P], ident[:, :])
                m.then_inc(S.otr_done, 1)

            def on_transpose(t, par):
                n = 2 * t + par
                pe.wait_ge(S.on_ready, n + 1)
                for qt in range(2):
                    m = pe.transpose(XB[:, qt * P:(qt + 1) * P], on[:, qt, :, :].rearrange("p h d -> p (h d)"), ident[:, :])
                m.then_inc(S.onT_done, 1)

            def out_project(t, par):
                n = 2 * t + par
                pe.wait_ge(S.onT_ready, n + 1)
                need(pe, S.qk32_ready, min(n + 5, SEQS) if isinstance(n, int) else n + 5)
                for qt in range(2):
                    m = pe.matmul(XB[:, qt * P:(qt + 1) * P], onT[:, qt * P:(qt + 1) * P], ow[:, :], start=True, stop=True)
                m.then_inc(S.pr_done, 1)

            def attn_b_pair(i):
                for h in range(2):
                    for g in range(GRP):
                        g1, g2, g3 = (shifted_group(i, h, g, -k) for k in (1, 2, 3))
                        if valid(i):
                            pass1(i, h, g, 0)
                        if valid(g1[0]):
                            neg_transpose(*g1)
                        if g == 3 and h == 1 and valid(i - 2):
                            r_back(PAIRS + i - 2, ZB)
                        if valid(i):
                            pass1(i, h, g, 1)
                        if valid(g2[0]):
                            pass2(*g2, 0)
                            pass2(*g2, 1)
                        if valid(i):
                            pass1(i, h, g, 2)
                        if valid(g3[0]):
                            values(*g3)
                        if valid(g2[0]):
                            pass2(*g2, 2)
                        if g == 0:
                            if valid(i - 1):
                                on_transpose(i - 1, h)
                            if valid(i + 1):
                                b_transpose(i + 1, h)
                        if g == 1 and valid(i + 1):
                            b_project(i + 1, h)
                        if g == 2:
                            if valid(i - 1):
                                out_project(i - 1, h)
                            if valid(i + 1):
                                pe.wait_ge(S.vb_ready, 2 * i + h + 3)
                            if valid(i - 2) and h == 0:
                                r_transpose(PAIRS + i - 2, ZB)
                            if valid(i - 2) and h == 1:
                                r_logits(PAIRS + i - 2, i - 2, ZB)
                        if isinstance(i, int) and i == -1 and h == 0 and g == 2:
                            first_mm(0, PIECES, AFTER - 1)
                            pe.wait_ge(S.qk32_ready, 1)
                            second_mm(0, PIECES, AFTER - 2)
                            pe.wait_ge(S.vb_ready, 1)
                            second_mm(0, PIECES, AFTER - 1)
                            pe.wait_ge(S.yo_ready, E * CHUNKS + SHW)
                        t, par, gg = shifted_group(i, h, g, -GRP)
                        if g == 3 and valid(t):
                            if valid(i - 2):
                                if h == 0:
                                    pe.wait_ge(S.xn2T_ready, PAIRS + i - 1)
                                else:
                                    pe.wait_ge(S.log_ready, PAIRS + i - 1)
                            o_back(t, par)

            for l in range(LAYERS):
                sh_first(l, 1, 1)
                pe.wait_ge(S.log_ready, PAIRS * (l + 1))
                counts(l)
                sh_second(l, 0, 0)
                for c in range(2, SHC):
                    sh_first(l, c, c % 2)
                    sh_second(l, c - 1, 1 - c % 2)
                index(l, 0)
                sh_second(l, SHC - 1, 1, range(0, 2))
                index(l, 1)
                sh_second(l, SHC - 1, 1, range(2, 4))
                pe.wait_ge(S.sh2_ready, SHC * (l + 1))
                expert_pair(l, 0, True, False)
                with pe.Fori(1, E // 2 - 1) as i:
                    expert_pair(l, i, False, False)
                expert_pair(l, E // 2 - 1, False, True)
                if l == 1:
                    second_mm(l, E // 2 - 1, len(WORK[l]) - 1)
                if l == 0:
                    for v in range(AFTER - 1):
                        first_mm(0, PIECES, v)
                        second_mm(0, PIECES, v - 1)
                    keep_busy(16)
                    pe.wait_ge(S.yo_ready, E * CHUNKS + SHW - 2)
                    pe.wait_ge(S.init_b, 7)
                    for i in range(-1, 2):
                        attn_b_pair(i)
                    with pe.Fori(2, PAIRS - 2) as i:
                        attn_b_pair(i)
                    for i in range(PAIRS - 2, PAIRS + 1):
                        attn_b_pair(i)
                    last_pair_logits(1, ZB)
        @block.scalar
        def _(act):
            for dst, src in ((wq, w_q), (wk, w_k), (wv, w_v), (wo, w_o)):
                act.dma_start(dst[:, :], src).then_inc(S.w_in, 16)
            act.dma_start(mask_i[:, :], hd_mask.rearrange("(p a) -> p a", a=1)).then_inc(S.w_in, 16)
            act.dma_start(router[:, :], router_w).then_inc(S.bias_in, 16)
            act.dma_start(bias_rows[0:E * FT, :], b1.rearrange("e (f p) -> (e f) p", p=P)).then_inc(S.bias_in, 16)
            act.dma_start(bias_rows[E * FT:E * FT + FT, :], sb1.rearrange("(f p) -> f p", p=P)).then_inc(S.bias_in, 16)
            qkv_b = attn_b.rearrange("(h c d) -> c h d", c=3, d=8)
            act.dma_start(bias_rows[36:37, :], qkv_b[0:1].rearrange("c h d -> c h d")).then_inc(S.bias_in, 16)
            act.dma_start(bias_rows[37:38, :], qkv_b[1:2].rearrange("c h d -> c h d")).then_inc(S.bias_in, 16)
            act.wait_ge(S.w_tr, 1)
            act.activation(wT[:, :, :].rearrange("p a d -> p (a d)"), bank[1][:, 0:3 * P], ACT.Copy).then_inc(S.w_trs, 1)

            RT_, GT_, V_, S_, PT_, Y_, L_ = bank[0], bank[1], bank[2], bank[3:5], bank[5], bank[6], bank[7]
            R_ = L_

            def xnT_copy(t, par):
                n = 2 * t + par
                act.wait_ge(S.xn_tr, n + 1)
                need(act, S.scores_done, n - 1)
                act.activation(xnT[:, par, :], RT_[:, 0:SEQ], ACT.Copy).then_inc(S.xnT_ready, 1)

            def v_copy(t, par):
                n = 2 * t + par
                act.wait_ge(S.v_done, n + 1)
                need(act, S.y_done, n - 1)
                act.activation(v_s[:, par, :, :].rearrange("p a d -> p (a d)"), V_[:, 0:SEQ], ACT.Copy).then_inc(S.v_ready, 1)

            def exps(t, par):
                n = 2 * t + par
                act.wait_ge(S.max_ready, n + 1)
                need(act, S.probs_tr, n - 1)
                for q in range(2):
                    a = act.activation(probs[:, par, q, :], S_[par][:, q * SEQ:(q + 1) * SEQ], ACT.Exp,
                                       bias=negmax[:, par, q:q + 1], accum_out=psums[:, par, q:q + 1])
                a.then_inc(S.probs_ready, 1)

            def r_copy(n, i, bk=R_):
                act.wait_ge(S.xn2_tr, n + 1)
                act.activation(xnT_all[:, bass.ds(512 * i, 512)], bk[:, :], ACT.Copy).then_inc(S.xn2T_ready, 1)

            def logT_copy(n, bk=L_):
                act.wait_ge(S.logT_done, n + 1)
                need(act, S.log_done, n)
                act.activation(logT[:, :], bk[0:E, 0:512], ACT.Copy).then_inc(S.logT_ready, 1)

            def log_copy(n, i, bk=R_):
                act.wait_ge(S.log_done, n + 1)
                act.activation(logits[:, bass.ds(4 * i, 4), :].rearrange("p t e -> p (t e)"), bk[:, 0:4 * E], ACT.Copy).then_inc(S.log_ready, 1)

            def g_copy(t, par):
                n = 2 * t + par
                act.wait_ge(S.g_done, n + 1)
                need(act, S.scores_done, n)
                act.activation(gT[:, :], GT_[:, 0:SEQ], ACT.Copy).then_inc(S.gT_ready, 1)

            def p_copy(t, par):
                n = 2 * t + par
                act.wait_ge(S.probs_tr, n + 1)
                need(act, S.y_done, n)
                act.activation(pT[:, :, :].rearrange("p a k -> p (a k)"), PT_[:, :], ACT.Copy).then_inc(S.pT_ready, 1)

            def attn_a_pair(i):
                for h in range(2):
                    if valid(i):
                        p_copy(i, h)
                    if valid(i - 2) and h == 0:
                        logT_copy(i - 2)
                    if valid(shifted_seq(i, h, 2)[0]):
                        g_copy(*shifted_seq(i, h, 2))
                    if valid(shifted_seq(i, h, 1)[0]):
                        exps(*shifted_seq(i, h, 1))
                    if valid(shifted_seq(i, h, 2)[0]):
                        v_copy(*shifted_seq(i, h, 2))
                    if valid(i - 1) and h == 1:
                        r_copy(i - 1, i - 1)
                    if valid(shifted_seq(i, h, 3)[0]):
                        xnT_copy(*shifted_seq(i, h, 3))
                    if valid(i - 2) and h == 0:
                        log_copy(i - 2, i - 2)

            for i in range(-2, 1):
                attn_a_pair(i)
                if i == -1:
                    act.wait_ge(S.bias_tr, 1)
                    act.activation(bias_T[:, :], L_[:, 0:38], ACT.Copy).then_inc(S.bias_set, 1)
            for i in range(1, 3):
                attn_a_pair(i)
            with act.Fori(3, PAIRS - 2) as i:
                attn_a_pair(i)
            for i in range(PAIRS - 2, PAIRS + 1):
                attn_a_pair(i)
            logT_copy(PAIRS - 1)
            log_copy(PAIRS - 1, PAIRS - 1)

            HB, YB = bank[0:4], bank[6:8]

            def sh_silu(l, c, cb, fs=range(FT)):
                need(act, S.sh2_done, l * SHC + c - 1)
                for f in fs:
                    act.wait_ge(S.sh1_done, l * SHC * FT + FT * c + f + 1)
                    act.activation(hsh[:, cb, f, :], HB[f][:, :], ACT.Silu,
                                   bias=bias_T[:, E * FT + f:E * FT + f + 1]).then_inc(S.sh1_ready, 1)

            def sh_out(l, c, cb):
                act.wait_ge(S.sh2_done, l * SHC + c + 1)
                act.activation(shared[:, bass.ds(4 * c, 4), :].rearrange("p t d -> p (t d)"), YB[cb][:, :], ACT.Copy,
                               scale=SHARED_SCALE).then_inc(S.sh2_ready, 1)

            def silus(l, i, v):
                n, k = work(l, i, v)
                if k is not None and k % CHUNKS == 0:
                    h = k // CHUNKS
                    e = 2 * i + h
                    act.activation(b1_cur[:, h, :], bias_T[:, bass.ds(FT * e, FT)], ACT.Copy).then_inc(S.b1_set, 1)
                    act.wait_ge(S.b1_set, l * E + e + 1)
                act.wait_ge(S.h_done, n + 1)
                need(act, S.yo_done, n - 1)
                for f in range(FT):
                    b = bias_T[:, E * FT + f:E * FT + f + 1] if k is None else b1_cur[:, k // CHUNKS, f:f + 1]
                    a = act.activation(hT[:, v % 2, f, :], HB[2 * (v % 2) + f // 2][:, (f % 2) * 256:(f % 2) * 256 + 256],
                                       ACT.Silu, bias=b)
                a.then_inc(S.h_ready, 1)

            act.activation(bq_s[:, :], bias_T[:, 36:37], ACT.Copy, scale=HD ** -0.5)

            AB, CB, OB, MB, XB, ZB = bank[0:2], bank[2:4], bank[4], bank[5], bank[6], bank[7]

            def o_copy(t, par, half):
                n = 2 * t + par
                act.wait_ge(S.pv_done, GRP * n + 2 * half + 2)
                need(act, S.otr_done, n)
                act.activation(oT[:, 2 * half:2 * half + 2, :].rearrange("p g t -> p (g t)"), OB[:, :], ACT.Copy).then_inc(S.ot_ready, 1)

            def on_copy(t, par):
                n = 2 * t + par
                act.wait_ge(S.onT_done, n + 1)
                need(act, S.pr_done, n)
                act.activation(onT[:, :], XB[:, 0:SEQ], ACT.Copy).then_inc(S.onT_ready, 1)

            def bt_copy(t, par):
                n = 2 * t + par
                act.wait_ge(S.tb_done, n + 1)
                need(act, S.vb_done, n - 1)
                act.activation(xnT[:, par, :], ZB[:, 0:SEQ], ACT.Copy).then_inc(S.tb_ready, 1)

            def qk_bias(t, par):
                n = 2 * t + par
                act.wait_ge(S.qk_done, n + 1)
                need(act, S.hilo_done, n)
                act.activation(qk32[:, 0, :], XB[:, 0:SEQ], ACT.Identity, bias=bq_s[:, 0:1], scale=HD ** -0.5)
                act.activation(qk32[:, 1, :], XB[:, SEQ:2 * SEQ], ACT.Identity, bias=bias_T[:, 37:38]).then_inc(S.qk32_ready, 1)

            def block_diag(t, par, g):
                U = 2 * GRP * t + GRP * par + g
                if g == 0:
                    act.wait_ge((S.kc_in0, S.kc_in1)[par], 48 * t + 48)
                need(act, S.c_done, 3 * (U - 2 * GRP) + 3)
                for j in range(2, 4):
                    a = act.activation(bdk[:, par, g, j, :], kc[:, par, g, :].bitcast(F32), ACT.Copy, scale=head_m[:, j:j + 1])
                a.then_inc(S.bd_act, 1)

            def neg_copy(t, par, g):
                U = 2 * GRP * t + GRP * par + g
                act.wait_ge(S.negT_done, U + 1)
                act.activation(qc[96:P, par, g, :], MB[96:P, 0:SEQ], ACT.Copy).then_inc(S.neg_set, 1)

            def exps_b(t, par, g):
                U = 2 * GRP * t + GRP * par + g
                need(act, S.pv_done, U - 1)
                for k in range(3):
                    act.wait_ge(S.c_done, 3 * U + k + 1)
                    act.activation(pt[:, g % 2, k, :], CB[(g + k) % 2][:, :], ACT.Exp).then_inc(S.exp_done, 1)

            def place_v(t, par):
                n = 2 * t + par
                need(act, S.vb_ready, n + 1)
                need(act, S.pv_done, GRP * (n - 1))
                act.activation(v_ext[:, par, :, :, 0:HD], v_s[:, par, :, :].rearrange("p k (h d) -> p k h d", d=HD), ACT.Copy
                                 ).then_inc(S.v_set, 1)

            def attn_b_pair(i):
                for h in range(2):
                    for g in range(GRP):
                        t, par, gg = shifted_group(i, h, g, -GRP)
                        if g % 2 == 1 and valid(t):
                            o_copy(t, par, g // 2)
                        if g == 1:
                            if valid(i - 1):
                                on_copy(i - 1, h)
                            if valid(i + 1):
                                bt_copy(i + 1, h)
                        if g == 2 and valid(i + 1):
                            qk_bias(i + 1, h)
                        if isinstance(i, int) and i == -1 and h == 0 and g == 2:
                            silus(0, PIECES, AFTER - 1)
                        if g == 3 and valid(i - 2):
                            if h == 0:
                                r_copy(PAIRS + i - 2, i - 2, ZB)
                            else:
                                logT_copy(PAIRS + i - 2, ZB)
                        t, par, gg = shifted_group(i, h, g, -1)
                        if valid(t):
                            neg_copy(t, par, gg)
                        if g == 3 and h == 1 and valid(i - 2):
                            log_copy(PAIRS + i - 2, i - 2, ZB)
                        t, par, gg = shifted_group(i, h, g, 2)
                        if valid(t):
                            block_diag(t, par, gg)
                        t, par, gg = shifted_group(i, h, g, -2)
                        if valid(t):
                            exps_b(t, par, gg)
                        t, par, gg = shifted_group(i, h, g, GRP)
                        if g == 3 and valid(t):
                            place_v(t, par)

            for l in range(LAYERS):
                act.wait_ge(S.y_zeroed, 32)
                sh_silu(l, 0, 0, range(0, 1))
                act.wait_ge(S.shifted, l + 1)
                act.activation(G[:, :, :], G[:, :, :], ACT.Exp).then_inc(S.exped, 1)
                for c in range(SHC):
                    sh_silu(l, c, c % 2, range(FT) if c > 0 else range(1, FT))
                    if c > 0:
                        sh_out(l, c - 1, 1 - c % 2)
                sh_out(l, SHC - 1, 1)
                for v in range(len(order(l, 0))):
                    silus(l, 0, v)
                with act.Fori(1, E // 2) as i:
                    for v in range(len(WORK[l])):
                        silus(l, i, v)
                if l == 0:
                    for v in range(AFTER - 1):
                        silus(0, PIECES, v)
                    act.wait_ge(S.init_b, 7)
                    for i in range(-1, 2):
                        attn_b_pair(i)
                    with act.Fori(2, PAIRS - 2) as i:
                        attn_b_pair(i)
                    for i in range(PAIRS - 2, PAIRS + 1):
                        attn_b_pair(i)
                    r_copy(2 * PAIRS - 1, PAIRS - 1, ZB)
                    logT_copy(2 * PAIRS - 1, ZB)
                    log_copy(2 * PAIRS - 1, PAIRS - 1, ZB)
            scale_tail(act)

        @block.vector
        def _(dve):
            dve.memset(mask_f[:, :], 0.0).then_inc(S.const_dve, 1)
            GT_, S_, PT_, Y_ = bank[1], bank[3:5], bank[5], bank[6]

            def stats(i, n, st_, mv_, s_st, s_mv):
                for j in range(4):
                    a = dve.bn_stats(st_[:, j, :], x[:, bass.ds(4 * i + j, 1), :].rearrange("p a d -> p (a d)"))
                a.then_inc(s_st, 1)
                alone(dve, s_st, n, S.const_dve)
                for j in range(4):
                    a = dve.bn_aggr(mv_[:, j, :], st_[:, j, :])
                a.then_inc(s_mv, 1)

            def norm(i, n, dst, mv_, rstd_, s_rstd, s_out):
                dve.wait_ge(s_rstd, n)
                for j in range(4):
                    a = dve.tensor_scalar(dst[:, j, :], x[:, bass.ds(4 * i + j, 1), :].rearrange("p a d -> p (a d)"),
                                          mv_[:, j, 0:1], rstd_[:, j:j + 1], ALU.subtract, ALU.mult)
                a.then_inc(s_out, 1)

            def norm_r(n, i):
                need(dve, S.xn2_tr, n)
                need(dve, S.xn2_stored, 16 * n)
                norm(i, n + 1, xn2, mv2, rstd2, S.ln2_rstd, S.xn2_ready)

            def maxes(t, par):
                n = 2 * t + par
                dve.wait_ge(S.scores_done, n + 1)
                dve.tensor_reduce(negmax[:, par, :], S_[par][:, :].rearrange("p (q k) -> p q k", q=2), AX.X, ALU.max,
                                  negate=True).then_inc(S.max_ready, 1)

            def inverse_sums(t, par):
                n = 2 * t + par
                dve.wait_ge(S.probs_ready, n + 1)
                dve.reciprocal(rsum[:, par, :], psums[:, par, :]).then_inc(S.rsum_ready, 1)

            def add_attn(t, par):
                n = 2 * t + par
                dve.wait_ge(S.y_done, n + 1)
                dve.wait_ge(S.rsum_ready, n + 1)
                for q in range(2):
                    xs = x[:, bass.ds(4 * t + 2 * par + q, 1), :].rearrange("p a d -> p (a d)")
                    a = dve.scalar_tensor_tensor(out=xs, in0=Y_[:, q * P:(q + 1) * P], scalar=rsum[:, par, q:q + 1], in1=xs,
                                                 op0=ALU.mult, op1=ALU.add)
                a.then_inc(S.attn_added, 1)

            def attn_a_pair(i):
                for h in range(2):
                    if valid(i):
                        inverse_sums(i, h)
                    if valid(shifted_seq(i, h, 1)[0]):
                        maxes(*shifted_seq(i, h, 1))
                    if valid(i - 1) and h == 0:
                        norm_r(i - 1, i - 1)
                    if valid(i + 2) and h == 1 and not (isinstance(i, int) and i == -2):
                        need(dve, S.xn_tr, 2 * i + 4)
                        norm(i + 2, i + 3, xn, mv, rstd, S.ln_rstd, S.xn_ready)
                    if valid(i):
                        add_attn(i, h)
                    if valid(i + 2) and h == 0:
                        if isinstance(i, int) and i <= 0:
                            dve.wait_ge((S.x_head, S.x_second, S.x_tail)[i + 2], 16)
                        stats(i + 2, i + 3, st, mv, S.ln_stats, S.ln_mv)
                    if valid(i) and h == 1:
                        alone(dve, S.attn_added, 2 * i + 2, S.const_dve)
                        stats(i, i + 1, st2, mv2, S.ln2_stats, S.ln2_mv)

            for i in range(-2, 1):
                if i == -1:
                    dve.wait_ge(S.w_in, 16 * 5)
                    dve.tensor_copy(mask_f[:, :], mask_i[:, :]).then_inc(S.const_dve, 1)
                    dve.wait_ge(S.const_dve, 2)
                    dve.tensor_scalar(wo_m[:, :], wo[:, :], mask_f[:, 0:1], None, ALU.mult).then_inc(S.w_trs, 1)
                    norm(0, 1, xn, mv, rstd, S.ln_rstd, S.xn_ready)
                    dve.wait_ge(S.wfold_mm, 1)
                    dve.tensor_scalar(m_qk[:, :], bank[2][:, 0:P], float(D) ** -0.5, None, ALU.mult)
                    dve.tensor_copy(m_vo[:, :], bank[2][:, P:2 * P]).then_inc(S.wfold, 1)
                attn_a_pair(i)
            for i in range(1, 3):
                attn_a_pair(i)
            with dve.Fori(3, PAIRS - 2) as i:
                attn_a_pair(i)
            for i in range(PAIRS - 2, PAIRS + 1):
                attn_a_pair(i)

            steps = [0]

            def step(ins, wait=True):
                steps[0] += 1
                ins.then_inc(S.route, 1)
                if wait:
                    dve.wait_ge(S.route, steps[0])

            def over_e(a):
                return a.unsqueeze(2).broadcast_to([P, NT, E])

            def routing(l):
                XT = bank[4:6]
                dve.wait_ge(S.log_ready, PAIRS * (l + 1))
                if l == 0:
                    dve.wait_ge(S.const_pool, N_CONST_POOL)
                    dve.wait_ge(S.w_moe_in, 16 * 4)
                step(dve.tensor_reduce(r1[:, :], logits[:, :, :], AX.X, ALU.max))
                dve.tensor_tensor(G[:, :, :], logits[:, :, :], over_e(r1[:, :]), ALU.subtract).then_inc(S.shifted, 1)
                dve.wait_ge(S.exped, l + 1)
                step(dve.tensor_reduce(r1[:, :], G[:, :, :], AX.X, ALU.add))
                step(dve.reciprocal(r2[:, :], r1[:, :]))
                step(dve.tensor_tensor(G[:, :, :], G[:, :, :], over_e(r2[:, :]), ALU.mult))
                rev_b = rev[:, :].unsqueeze(1).broadcast_to([P, NT, E])
                for c, g in enumerate((G, G1)):
                    step(dve.tensor_reduce(r1[:, :], g[:, :, :], AX.X, ALU.max))
                    step(dve.tensor_tensor(t1[:, :, :], g[:, :, :], over_e(r1[:, :]), ALU.is_equal))
                    step(dve.tensor_tensor(t1[:, :, :], t1[:, :, :], rev_b, ALU.mult))
                    step(dve.tensor_reduce(r2[:, :], t1[:, :, :], AX.X, ALU.max))
                    step(dve.tensor_tensor(m1[:, :, :], t1[:, :, :], over_e(r2[:, :]), ALU.is_equal))
                    a = dve.tensor_copy(MK[:, c, :, :].rearrange("p e t -> p t e"), m1[:, :, :])
                    if c == 0:
                        step(dve.tensor_tensor(t1[:, :, :], G[:, :, :], m1[:, :, :], ALU.mult))
                        step(dve.tensor_tensor(G1[:, :, :], G[:, :, :], t1[:, :, :], ALU.subtract))
                a.then_inc(S.masks_ready, 1)
                dve.wait_ge(S.masks_ready, l + 1)
                flat = lambda a: a[:, :, :, :].rearrange("p c e t -> p (c e t)")
                dve.wait_ge(S.count_done, l + 1)
                step(dve.tensor_tensor_scan(flat(INC), carry[:, :], XT[1][:, :], 0.0, ALU.mult, ALU.add))
                step(dve.tensor_tensor(flat(POS), flat(INC), XT[0][:, :], ALU.add), False)
                step(dve.tensor_scalar(keep1[:, :], INC[:, 0, :, NT - 1], float(CAP), None, ALU.min))
                step(dve.tensor_tensor(POS[:, 1, :, :], POS[:, 1, :, :], keep1[:, :].unsqueeze(2).broadcast_to([P, E, NT]), ALU.add))
                step(dve.scalar_tensor_tensor(out=flat(KM), in0=flat(POS), scalar=float(CAP), in1=flat(MK), op0=ALU.is_lt, op1=ALU.mult), False)
                step(dve.tensor_tensor(POS[:, :, :, :], POS[:, :, :, :], slot_base[:, :, :].unsqueeze(1).broadcast_to([P, 2, E, NT]), ALU.add))
                step(dve.tensor_tensor(flat(POS), flat(POS), flat(KM), ALU.mult))
                for c in range(2):
                    step(dve.tensor_reduce(slot[:, c, :], POS[:, c, :, :].rearrange("p e t -> p t e"), AX.X, ALU.add), c == 1)
                step(dve.tensor_scalar(slot_i[:, :, :], slot[:, :, :], -1.0, None, ALU.add))
                step(dve.tensor_scalar(hi_i[:, :, :], slot_i[:, :, :], 7, None, ALU.logical_shift_right), False)
                step(dve.tensor_scalar(lo_i[:, :, :], slot_i[:, :, :], 127, None, ALU.bitwise_and))
                step(dve.tensor_copy(hi_b[:, :], hi_i[:, :, :].rearrange("p c t -> p (c t)")), False)
                step(dve.tensor_copy(lo_b[:, :], lo_i[:, :, :].rearrange("p c t -> p (c t)")))
                n2 = 2 * NT
                dve.tensor_tensor(OH[:, :, :], iota_hi[:, :].unsqueeze(1).broadcast_to([P, n2, SLOT_TILES]),
                                  hi_b[:, :].unsqueeze(2).broadcast_to([P, n2, SLOT_TILES]), ALU.is_equal).then_inc(S.oh_ready, 1)
                dve.wait_ge(S.oh_ready, l + 1)
                dve.tensor_scalar(RH[:, :, 0, :], OH[:, :, :], part1[:, 0:1], None, ALU.mult)
                for c in range(2):
                    ns = slice(c * NT, c * NT + NT)
                    dve.tensor_tensor(OL[:, ns, :], iota_lo[:, :].unsqueeze(1).broadcast_to([P, NT, P]),
                                      lo_b[:, ns].unsqueeze(2).broadcast_to([P, NT, P]), ALU.is_equal).then_inc(S.onehot_ready, 1)
                if l == 0:
                    dve.tensor_scalar(slot_u[:, :, :], slot[:, :, :], -1.0, 0.0, ALU.add, ALU.max)
                for c in range(2):
                    step(dve.tensor_tensor(GK[:, c, :, :], KM[:, c, :, :], G[:, :, :].rearrange("p t e -> p e t"), ALU.mult), c == 1)
                for c in range(2):
                    step(dve.tensor_reduce(gate[:, c, :], GK[:, c, :, :].rearrange("p e t -> p t e"), AX.X, ALU.add), c == 1)
                step(dve.tensor_tensor(den[:, :], gate[:, 0, :], gate[:, 1, :], ALU.add))
                step(dve.tensor_scalar(den[:, :], den[:, :], TINY, None, ALU.max))
                step(dve.reciprocal(r1[:, :], den[:, :]))
                step(dve.tensor_tensor(gate[:, :, :], gate[:, :, :], r1[:, :].unsqueeze(1).broadcast_to([P, 2, NT]), ALU.mult))
                dve.wait_ge(S.index_done, 2 * l + 2)
                a_, b_ = XT[0][:, 0:SLOT_TILES], XT[0][:, SLOT_TILES:2 * SLOT_TILES]
                step(dve.tensor_scalar(row_f[:, :], b_, float(P), -1.0, ALU.mult, ALU.add))
                step(dve.tensor_tensor(row_f[:, :], a_, row_f[:, :], ALU.add))
                step(dve.tensor_scalar(row_e[:, :], b_, float(NT), -float(T), ALU.is_ge, ALU.mult))
                step(dve.tensor_tensor(row_e[:, :], row_e[:, :], row_f[:, :], ALU.add))
                step(dve.tensor_scalar(tok_idx[:, :], row_e[:, :], 0.0, None, ALU.max))
                step(dve.tensor_scalar(row_e[:, :], a_, 0.0, 4.0 * T, ALU.is_equal, ALU.mult))
                dve.tensor_tensor(row_idx[:, :], row_e[:, :], row_f[:, :], ALU.add).then_inc(S.index_ready, 1)
                dve.wait_ge(S.rh_ready, 2 * l + 2)
                x_split(l, 0, 0)
                dve.tensor_copy(sw1_hl[:, 0, :], sw1_s[:, :]).then_inc(S.sw1_split, 1)
                dve.wait_ge(S.sw1_split, 2 * l + 1)
                dve.tensor_tensor(sw1_hl[:, 1, :], sw1_s[:, :], sw1_hl[:, 0, :].bitcast(F32), ALU.subtract
                                  ).then_inc(S.sw1_split, 1)
                w1_split(l, 0, 0)

            def add_shared(l, i, v):
                n = 3 * (l * E // 2 + i)
                c = {0: SHC + i, 2: i, 6: i}.get(v)
                if c is None:
                    return
                xs = x[:, bass.ds(4 * c, 4), :]
                if v == 2:
                    dve.tensor_tensor(xs, xs, shared[:, bass.ds(4 * i, 4), :], ALU.add).then_inc(S.shared_added, 1)
                else:
                    need(dve, S.shared_added, n + (2 if v == 6 else 0))
                    dve.scalar_tensor_tensor(out=xs, in0=sb2_b[:, :].unsqueeze(1).broadcast_to([P, 4, D]),
                                             scalar=SHARED_SCALE, in1=xs, op0=ALU.mult, op1=ALU.add).then_inc(S.shared_added, 1)

            def x_split(l, i, v):
                if not (isinstance(i, int) and i == PIECES):
                    i, v = i + v // len(order(l, i)), v % len(order(l, i))
                n, k = work(l, i, v)
                need(dve, S.h_done, n - 1)
                if k is None:
                    src = xnT_all[:, bass.ds(piece_start(l, i, v), 256)]
                else:
                    dve.wait_ge(S.xg_tr, l * E * CHUNKS + 2 * CHUNKS * i + k + 1)
                    src = bank[4 + k % 2][:, 0:CH * P]
                dve.tensor_copy(xT_hl[:, v % 2, 0, :], src).then_inc(S.xT_hi, 1)
                dve.wait_ge(S.xT_hi, n + 1)
                dve.tensor_tensor(xT_hl[:, v % 2, 1, :], src, xT_hl[:, v % 2, 0, :].bitcast(F32), ALU.subtract
                                  ).then_inc(S.xT_ready, 1)

            def w1_split(l, i, h):
                n = l * E + 2 * i + h
                dve.wait_ge((S.w1_in0, S.w1_in1)[h], 32 * (l * E // 2 + i + 1))
                need(dve, S.h_done, before_reuse(l, i, h))
                dve.tensor_copy(w1_hl[h][:, 0, :], w1_s[h][:, :]).then_inc(S.w1_hi, 1)
                dve.wait_ge(S.w1_hi, n + 1)
                dve.tensor_tensor(w1_hl[h][:, 1, :], w1_s[h][:, :], w1_hl[h][:, 0, :].bitcast(F32), ALU.subtract
                                  ).then_inc(S.w1_split, 1)

            def y_copy(l, i, v):
                if v < 0:
                    i, v = i - 1, v + len(order(l, i - 1))
                n, k = work(l, i, v)
                rows = bank[6 + v % 2][:, 0:CH * P].rearrange("p (a d) -> p a d", a=CH)
                dve.wait_ge(S.yo_done, n + 1)
                if k is None:
                    after = isinstance(i, int) and i == PIECES
                    dve.wait_ge(S.shared_added, 3 * E // 2 if after else 3 * (l * E // 2 + i) + 1)
                    xs = x[:, bass.ds(piece_start(l, i, v) // P, 2), :]
                    dve.scalar_tensor_tensor(out=xs, in0=rows, scalar=SHARED_SCALE, in1=xs, op0=ALU.mult, op1=ALU.add
                                             ).then_inc(S.yo_ready, 1)
                    return
                r, ex = k % RING, 2 * i + k // CHUNKS
                need(dve, (sto, sca)[l][r], 32 * (2 * i + k // RING))
                dve.tensor_tensor(yo[:, r, :, :], rows, b2_b[:, bass.ds(ex, 1), :].broadcast_to([P, CH, D]), ALU.add
                                  ).then_inc(S.yo_ready, 1)

            def expert_pair(l, i, first, last):
                if first:
                    dve.wait_ge(S.sh2_ready, SHC * (l + 1))
                for v, k in enumerate(order(l, i)):
                    if not (last and l == 1 and v == len(WORK[l]) - 1):
                        x_split(l, i, v + 1)
                    if not (first and v == 0):
                        y_copy(l, i, v - 1)
                    add_shared(l, i, v)
                    if v == 1:
                        w1_split(l, i, 1)
                    if v == 8 and not last:
                        w1_split(l, i + 1, 0)

            def combine(pair, c):
                dve.wait_ge(y_in[c], 64 * (pair + 1))
                if c == 1:
                    dve.wait_ge(S.comb, pair + 1)
                for j in range(4):
                    t = 4 * pair + j
                    xs = x[:, bass.ds(t, 1), :].rearrange("p a d -> p (a d)")
                    a = dve.scalar_tensor_tensor(out=xs, in0=yab[:, c, j, :], scalar=gate[:, c, bass.ds(t, 1)],
                                                 in1=xs, op0=ALU.mult, op1=ALU.add)
                a.then_inc((S.comb, S.y_used)[c], 1)

            AB, CB, OB, MB, XB, ZB = bank[0:2], bank[2:4], bank[4], bank[5], bank[6], bank[7]

            def max_b(t, par, g, k):
                U = 2 * GRP * t + GRP * par + g
                if k == 0:
                    need(dve, S.negT_done, U - 1)
                dve.wait_ge(S.a_done, 3 * U + k + 1)
                heads, first = (4, 0) if k == 0 else (2, 2 * k - 2)
                dst = negp[:, g % 2, min(k, 1), 96:P].rearrange("p (j r) -> p j r", r=8)[:, first:first + heads, 0]
                dve.tensor_reduce(dst, AB[(g + k) % 2][:, :].rearrange("p (j k) -> p j k", j=heads), AX.X, ALU.max,
                                  negate=True).then_inc(S.amax_done, 1)

            def split(t, par):
                n = 2 * t + par
                dve.wait_ge(S.qk32_ready, n + 1)
                need(dve, (S.qks_stored0, S.qks_stored1)[par], 16 * t)
                dve.tensor_copy(qks[:, par, 0, :, :], qk32[:, :, :]).then_inc(S.hilo_hi, 1)
                dve.wait_ge(S.hilo_hi, n + 1)
                dve.tensor_tensor(qks[:, par, 1, :, :], qk32[:, :, :], qks[:, par, 0, :, :].bitcast(F32),
                                  ALU.subtract).then_inc(S.hilo_done, 1)

            def v_bias(t, par):
                n = 2 * t + par
                dve.wait_ge(S.vb_done, n + 1)
                need(dve, S.v_set, n - 1)
                dve.tensor_tensor(v_s[:, par, :, :], ZB[:, 0:SEQ].rearrange("p (k d) -> p k d", k=2),
                                  bv_b[:, :, :].rearrange("p h d -> p (h d)").unsqueeze(1).broadcast_to([P, 2, D]),
                                  ALU.add).then_inc(S.vb_ready, 1)

            def divide(t, par):
                n = 2 * t + par
                dve.wait_ge(S.otr_done, n + 1)
                need(dve, S.onT_done, n)
                o = [bk[:, :].rearrange("p (h r) -> p h r", r=32) for bk in (XB, ZB)]
                for qt in range(2):
                    a = dve.reciprocal(osum[:, qt, :], o[qt][:, :, HD])
                a.then_inc(S.osum_ready, 1)
                dve.wait_ge(S.osum_ready, n + 1)
                for qt in range(2):
                    a = dve.tensor_tensor(on[:, qt, :, :], o[qt][:, :, 0:HD],
                                          osum[:, qt, :].unsqueeze(2).broadcast_to([P, HEADS, HD]), ALU.mult)
                a.then_inc(S.on_ready, 1)

            def add_out(t, par):
                n = 2 * t + par
                dve.wait_ge(S.pr_done, n + 1)
                dve.wait_ge(S.ob_added, t + 1)
                xs = x[:, bass.ds(4 * t + 2 * par, 2), :]
                dve.tensor_tensor(xs, xs, XB[:, 0:SEQ].rearrange("p (k d) -> p k d", k=2), ALU.add).then_inc(S.xb_added, 1)

            def stats_b(i):
                alone(dve, S.y_used, i + 1, S.const_dve)
                stats(i, PAIRS + i + 1, st, mv, S.ln_stats, S.ln_mv)

            def norm_b(i):
                need(dve, S.tb_done, 2 * i)
                norm(i, PAIRS + i + 1, xn, mv, rstd, S.ln_rstd, S.xn_ready)

            def attn_b_pair(i):
                for h in range(2):
                    for g in range(GRP):
                        if valid(i):
                            max_b(i, h, g, 0)
                        if g == 2 and valid(i + 1):
                            v_bias(i + 1, h)
                        if g == 0 and valid(i - 1):
                            divide(i - 1, h)
                        if g == 3 and valid(i - 1):
                            add_out(i - 1, h)
                        if valid(i):
                            max_b(i, h, g, 1)
                            max_b(i, h, g, 2)
                        if g == 0 and valid(i + 2):
                            combine(i + 2, h)
                        if g == 1 and h == 0 and valid(i - 2):
                            norm_r(PAIRS + i - 2, i - 2)
                        if g == 1 and h == 1 and valid(i + 2):
                            stats_b(i + 2)
                        if g == 2 and valid(i + 1):
                            split(i + 1, h)
                        if isinstance(i, int) and i == -1 and h == 0 and g == 2:
                            y_copy(0, PIECES, AFTER - 2)
                            y_copy(0, PIECES, AFTER - 1)
                        if g == 2 and h == 1 and valid(i + 2):
                            norm_b(i + 2)
                        if g == 3 and h == 1 and valid(i - 1):
                            alone(dve, S.xb_added, 2 * i, S.const_dve)
                            stats(i - 1, PAIRS + i, st2, mv2, S.ln2_stats, S.ln2_mv)

            for l in range(LAYERS):
                routing(l)
                expert_pair(l, 0, True, False)
                with dve.Fori(1, E // 2 - 1) as i:
                    expert_pair(l, i, False, False)
                expert_pair(l, E // 2 - 1, False, True)
                if l == 1:
                    y_copy(l, E // 2 - 1, len(WORK[l]) - 1)
                if l == 0:
                    for v in range(AFTER - 1):
                        x_split(0, PIECES, v + 1)
                        if v == AFTER - 3:
                            dve.wait_ge(S.shared_added, 3 * E // 2)
                            combine(0, 0)
                            combine(0, 1)
                            stats_b(0)
                        if v == AFTER - 2:
                            norm_b(0)
                        y_copy(0, PIECES, v - 1)
                    dve.wait_ge(S.wb_in, 16 * 4)
                    dve.wait_ge(S.init_b, 7)
                    for i in range(-1, 2):
                        attn_b_pair(i)
                    with dve.Fori(2, PAIRS - 2) as i:
                        attn_b_pair(i)
                    for i in range(PAIRS - 2, PAIRS + 1):
                        attn_b_pair(i)
                    norm_r(2 * PAIRS - 1, PAIRS - 1)
            combine_tail(dve, TAIL_DVE, 0)



_INS = ['L0_attn_a_x', 'L0_attn_a_head_dim_mask', 'L0_attn_a_w_q', 'L0_attn_a_w_k', 'L0_attn_a_w_v', 'L0_attn_a_w_o',
        'L0_attn_b_attn_W', 'L0_attn_b_attn_b', 'L0_attn_b_out_W', 'L0_attn_b_out_b', 'L0_ffn_router_w', 'L0_ffn_w1',
        'L0_ffn_b1', 'L0_ffn_w2', 'L0_ffn_b2', 'L0_ffn_sw1', 'L0_ffn_sb1', 'L0_ffn_sw2', 'L0_ffn_sb2']


def kernel(**inputs):
    import numpy as np
    import concourse.bacc as bacc
    from concourse.bass_utils import run_bass_kernel_spmd

    nc = bacc.Bacc("TRN2", target_bir_lowering=False, num_devices=1)
    arrays, args = {}, []
    for name in _INS:
        a = np.ascontiguousarray(inputs[name])
        arrays[f"in_{name}"] = a
        args.append(nc.dram_tensor(f"in_{name}", a.shape, mybir.dt.from_np(a.dtype), kind="ExternalInput").ap())
    out = nc.dram_tensor("out_x", (SEQS, SEQ, D), F32, kind="ExternalOutput").ap()
    build(nc, *args, out)
    r = run_bass_kernel_spmd(nc, [arrays], core_ids=[0])
    return r.results[0]["out_x"]
```
